# Optimizing a Trainium2 kernel written in Bass

```python
import numpy as np
import jax
import jax.numpy as jnp

def _softmax(x, axis=-1):
    return jax.nn.softmax(x, axis=axis)

def _gelu(x):
    return jax.nn.gelu(x, approximate=True)

def _silu(x):
    return jax.nn.silu(x)

def _sigmoid(x):
    return jax.nn.sigmoid(x)

def _layernorm(x, axis=-1, eps=1e-05):
    m = jnp.mean(x, axis=axis, keepdims=True)
    v = jnp.var(x, axis=axis, keepdims=True)
    return (x - m) / jnp.sqrt(v + eps)

def _scatter_add(tgt, idx, src, axis=0):
    return tgt.at[idx].add(src)

def _segment_sum(src, seg, n):
    return jax.ops.segment_sum(src, seg, n)
kernel_name = 'mk_gnn_resnorm_d4_gnn_r64_1b889c'

def setup_inputs(seed: int=0):
    np.random.seed(seed)
    _w = jnp.asarray

    def _rec_inputs():
        import jax
        import jax.numpy as jnp
        _gk = jax.random.key(seed)
        x = -0.000202 + 1 * jax.random.normal(jax.random.fold_in(_gk, 1), (100000, 64), jnp.float32)
        src = jax.random.randint(jax.random.fold_in(_gk, 2), (50000,), 0, 100000, jnp.int32)
        dst = jnp.minimum((100000 * jax.random.uniform(jax.random.fold_in(_gk, 3), (50000,)) ** 2.0).astype(jnp.int32), 99999)
        _o = jnp.argsort(dst, stable=True)
        src = src[_o]
        dst = dst[_o]
        edge_attr_32 = -5.16925e-05 + 1.00005 * jax.random.normal(jax.random.fold_in(_gk, 13), (50000, 32), jnp.float32)
        edge_weight = jax.random.uniform(jax.random.fold_in(_gk, 15), (50000,), jnp.float32, 0.0, 0.999999)
        return (x, src, dst, edge_attr_32, edge_weight)
    x, src, dst, edge_attr_32, edge_weight = _rec_inputs()

    def _L0_gnn_setup():
        import jax, jax.numpy as jnp
        import numpy as np
        N_NODES = 100000
        N_EDGES = 50000
        EDGE_OUT = 32
        HID = 128
        NODE_OUT = 64
        N_GRAPHS = 16
        key = jax.random.key(seed)
        ks = jax.random.split(key, 9)
        x = jax.random.normal(ks[0], (N_NODES, 64), dtype=jnp.float32)
        edge_index = jax.random.randint(ks[1], (2, N_EDGES), 0, N_NODES, dtype=jnp.int64)
        edge_attr = jax.random.normal(ks[2], (N_EDGES, EDGE_OUT), dtype=jnp.float32)
        u = jax.random.normal(ks[3], (N_GRAPHS, 1), dtype=jnp.float32)
        batch = jnp.sort(jax.random.randint(ks[4], (N_NODES,), 0, N_GRAPHS, dtype=jnp.int64))
        d_in = 3 * EDGE_OUT + 1
        W1 = jax.random.normal(ks[5], (d_in, HID), dtype=jnp.float32) / np.sqrt(d_in)
        b1 = jnp.zeros((HID,), dtype=jnp.float32)
        W2 = jax.random.normal(ks[6], (HID, NODE_OUT), dtype=jnp.float32) / np.sqrt(HID)
        b2 = jnp.zeros((NODE_OUT,), dtype=jnp.float32)
        return {'x': x, 'edge_index': edge_index, 'edge_attr': edge_attr, 'u': u, 'batch': batch, 'W1': W1, 'b1': b1, 'W2': W2, 'b2': b2}
    _L0_gnn_all = _L0_gnn_setup()
    _L0_gnn_in = {k: v for k, v in _L0_gnn_all.items() if k in ('u', 'W1', 'b1', 'W2', 'b2')}
    del _L0_gnn_all

    def _L1_gnn_setup():
        import jax, jax.numpy as jnp
        import numpy as np
        N, E, F_IN, F_OUT, K, T = (100000, 25000, 64, 64, 2, 2)

        def _gcn_norm(row, col, edge_weight, n):
            deg = jax.ops.segment_sum(edge_weight, col, num_segments=n)
            dinv = jnp.where(deg > 0, jax.lax.rsqrt(jnp.maximum(deg, 1e-12)), 0.0)
            return dinv[row] * edge_weight * dinv[col]

        def _propagate(out, row, col, norm, n):
            msgs = out[:, row, :] * norm[None, :, None]
            return jax.vmap(lambda m: jax.ops.segment_sum(m, col, num_segments=n))(msgs)
        key = jax.random.key(seed)
        ks = jax.random.split(key, 7)
        s = 0.1
        return {'x': jax.random.normal(ks[0], (N, F_IN), jnp.float32), 'edge_index': jax.random.randint(ks[1], (2, E), 0, N, dtype=jnp.int32), 'edge_weight': jax.random.uniform(ks[2], (E,), jnp.float32), 'init_weight': jax.random.normal(ks[3], (K, F_IN, F_OUT), jnp.float32) * s, 'weight': jax.random.normal(ks[4], (T - 1, K, F_OUT, F_OUT), jnp.float32) * s, 'root_weight': jax.random.normal(ks[5], (T, K, F_IN, F_OUT), jnp.float32) * s, 'bias': jax.random.normal(ks[6], (T, K, F_OUT), jnp.float32) * s}
    _L1_gnn_all = _L1_gnn_setup()
    _L1_gnn_in = {k: v for k, v in _L1_gnn_all.items() if k in ('init_weight', 'weight', 'root_weight', 'bias')}
    del _L1_gnn_all

    def _L2_gnn_setup():
        import jax, jax.numpy as jnp
        import numpy as np
        N_NODES = 150000
        N_EDGES = 18750
        D_IN = 64
        D_OUT = 64
        key = jax.random.key(seed)
        k1, k2, k3, k4, k5, k6 = jax.random.split(key, 6)
        x = jax.random.normal(k1, (N_NODES, D_IN), dtype=jnp.float32)
        row = jax.random.randint(k2, (N_EDGES,), 0, N_NODES, dtype=jnp.int64)
        col = jax.random.randint(k3, (N_EDGES,), 0, N_NODES, dtype=jnp.int64)
        vals = jax.random.uniform(k4, (N_EDGES,), dtype=jnp.float32)
        W = jax.random.normal(k5, (D_OUT, D_IN), dtype=jnp.float32) / np.sqrt(D_IN)
        b = jax.random.normal(k6, (D_OUT,), dtype=jnp.float32) * 0.01
        return {'x': x, 'row': row, 'col': col, 'vals': vals, 'W': W, 'b': b}
    _L2_gnn_all = _L2_gnn_setup()
    _L2_gnn_in = {k: v for k, v in _L2_gnn_all.items() if k in ('W', 'b')}
    del _L2_gnn_all

    def _L3_gnn_setup():
        import jax, jax.numpy as jnp
        import numpy as np
        from functools import partial
        N_NODES = 50000
        N_EDGES = 12500
        IN_F = 64
        OUT_F = 64
        key = jax.random.key(seed)
        k1, k2, k3, k4, k5 = jax.random.split(key, 5)
        stdv = 1.0 / np.sqrt(OUT_F)
        x = jax.random.normal(k1, (N_NODES, IN_F), dtype=jnp.float32)
        edge_index = jax.random.randint(k2, (2, N_EDGES), 0, N_NODES, dtype=jnp.int64)
        edge_weight = jax.random.uniform(k3, (N_EDGES,), dtype=jnp.float32)
        weight = jax.random.uniform(k4, (IN_F, OUT_F), minval=-stdv, maxval=stdv, dtype=jnp.float32)
        bias = jax.random.uniform(k5, (OUT_F,), minval=-stdv, maxval=stdv, dtype=jnp.float32)
        return {'x': x, 'edge_index': edge_index, 'edge_weight': edge_weight, 'weight': weight, 'bias': bias}
    _L3_gnn_all = _L3_gnn_setup()
    _L3_gnn_in = {k: v for k, v in _L3_gnn_all.items() if k in ('weight', 'bias')}
    del _L3_gnn_all
    return {'x': x, 'src': src, 'dst': dst, 'edge_attr_32': edge_attr_32, 'edge_weight': edge_weight, 'L0_gnn_u': _L0_gnn_in['u'], 'L0_gnn_W1': _L0_gnn_in['W1'], 'L0_gnn_b1': _L0_gnn_in['b1'], 'L0_gnn_W2': _L0_gnn_in['W2'], 'L0_gnn_b2': _L0_gnn_in['b2'], 'L1_gnn_init_weight': _L1_gnn_in['init_weight'], 'L1_gnn_weight': _L1_gnn_in['weight'], 'L1_gnn_root_weight': _L1_gnn_in['root_weight'], 'L1_gnn_bias': _L1_gnn_in['bias'], 'L2_gnn_W': _L2_gnn_in['W'], 'L2_gnn_b': _L2_gnn_in['b'], 'L3_gnn_weight': _L3_gnn_in['weight'], 'L3_gnn_bias': _L3_gnn_in['bias']}

def reference(x, src, dst, edge_attr_32, edge_weight, L0_gnn_u, L0_gnn_W1, L0_gnn_b1, L0_gnn_W2, L0_gnn_b2, L1_gnn_init_weight, L1_gnn_weight, L1_gnn_root_weight, L1_gnn_bias, L2_gnn_W, L2_gnn_b, L3_gnn_weight, L3_gnn_bias):
    import jax
    import jax.numpy as jnp

    def _L0_gnn_ref(x, edge_index, edge_attr, u, batch, W1, b1, W2, b2):
        import jax, jax.numpy as jnp
        import numpy as np
        N_NODES = 100000
        N_EDGES = 50000
        EDGE_OUT = 32
        HID = 128
        NODE_OUT = 64
        N_GRAPHS = 16
        N = x.shape[0]
        row = edge_index[0]
        seg_sum = jax.ops.segment_sum(edge_attr, row, num_segments=N)
        seg_max = jax.ops.segment_max(edge_attr, row, num_segments=N)
        cnt = jax.ops.segment_sum(jnp.ones((edge_attr.shape[0], 1), edge_attr.dtype), row, num_segments=N)
        seg_mean = seg_sum / jnp.maximum(cnt, 1.0)
        seg_max = jnp.where(cnt > 0, seg_max, 0.0)
        h = jnp.concatenate([seg_sum, seg_max, seg_mean, u[batch]], axis=1)
        h = jax.nn.relu(h @ W1 + b1)
        return h @ W2 + b2

    def _L1_gnn_ref(x, edge_index, edge_weight, init_weight, weight, root_weight, bias):
        import jax, jax.numpy as jnp
        import numpy as np
        N, E, F_IN, F_OUT, K, T = (100000, 25000, 64, 64, 2, 2)

        def _gcn_norm(row, col, edge_weight, n):
            deg = jax.ops.segment_sum(edge_weight, col, num_segments=n)
            dinv = jnp.where(deg > 0, jax.lax.rsqrt(jnp.maximum(deg, 1e-12)), 0.0)
            return dinv[row] * edge_weight * dinv[col]

        def _propagate(out, row, col, norm, n):
            msgs = out[:, row, :] * norm[None, :, None]
            return jax.vmap(lambda m: jax.ops.segment_sum(m, col, num_segments=n))(msgs)
        n = x.shape[0]
        row, col = (edge_index[0], edge_index[1])
        norm = _gcn_norm(row, col, edge_weight, n)
        out = x
        for t in range(T):
            if t == 0:
                out = jnp.einsum('nf,kfo->kno', x, init_weight)
            else:
                out = jnp.einsum('kno,kop->knp', out, weight[t - 1])
            out = _propagate(out, row, col, norm, n)
            root = jnp.einsum('nf,kfo->kno', x, root_weight[t])
            out = jax.nn.relu(out + root + bias[t][:, None, :])
        return out.mean(axis=0)

    def _L2_gnn_ref(x, row, col, vals, W, b):
        import jax, jax.numpy as jnp
        import numpy as np
        N_NODES = 150000
        N_EDGES = 18750
        D_IN = 64
        D_OUT = 64
        msgs = vals[:, None] * x[col]
        agg = jax.ops.segment_sum(msgs, row, num_segments=x.shape[0])
        return agg @ W.T + b

    def _L3_gnn_ref(x, edge_index, edge_weight, weight, bias):
        import jax, jax.numpy as jnp
        import numpy as np
        from functools import partial
        N_NODES = 50000
        N_EDGES = 12500
        IN_F = 64
        OUT_F = 64
        num_nodes = x.shape[0]
        support = x @ weight
        row, col = (edge_index[0], edge_index[1])
        deg = jax.ops.segment_sum(jnp.ones_like(row, dtype=jnp.float32), row, num_segments=num_nodes)
        deg_inv_sqrt = jnp.where(deg > 0, jax.lax.rsqrt(jnp.maximum(deg, 1.0)), 0.0)
        norm = deg_inv_sqrt[row] * edge_weight * deg_inv_sqrt[col]
        msgs = norm[:, None] * support[col]
        output = jax.ops.segment_sum(msgs, row, num_segments=num_nodes)
        return output + bias
    edge_index = jnp.stack([src, dst])
    batch0 = jnp.zeros((100000,), jnp.int32)
    x = _layernorm(x + _L0_gnn_ref(x, edge_index, edge_attr_32, L0_gnn_u, batch0, L0_gnn_W1, L0_gnn_b1, L0_gnn_W2, L0_gnn_b2), axis=-1)
    x = _layernorm(x + _L1_gnn_ref(x, edge_index, edge_weight, L1_gnn_init_weight, L1_gnn_weight, L1_gnn_root_weight, L1_gnn_bias), axis=-1)
    x = _layernorm(x + _L2_gnn_ref(x, src, dst, edge_weight, L2_gnn_W, L2_gnn_b), axis=-1)
    x = _layernorm(x + _L3_gnn_ref(x, edge_index, edge_weight, L3_gnn_weight, L3_gnn_bias), axis=-1)
    return x

_drawn_inputs = setup_inputs


def setup_inputs(seed=0):
    import zlib

    import numpy as np

    out = dict(_drawn_inputs(seed))
    spreads = {'L0_gnn_b1': (0.0, 0.1), 'L0_gnn_b2': (0.0, 0.1)}
    factors = {'L2_gnn_b': 5.353}
    for name, (base, spread) in spreads.items():
        noise = np.random.default_rng([zlib.crc32(name.encode()), seed]).standard_normal(out[name].shape)
        drawn = base * np.exp(spread * noise) if base else spread * noise
        out[name] = jnp.asarray(drawn.astype(out[name].dtype))
    for name, factor in factors.items():
        out[name] = (out[name] * factor).astype(out[name].dtype)
    return out
```

```python
import concourse.bass as bass
from concourse import mybir
from contextlib import ExitStack

F32 = mybir.dt.float32
F16 = mybir.dt.float16
BF16 = mybir.dt.bfloat16
I32 = mybir.dt.int32
ALU = mybir.AluOpType
ACT = mybir.ActivationFunctionType
AX = mybir.AxisListType.X

P = 128
N = 100000
E = 50000
D = 64
A = 32
HID = 128
TB = 4
NB = -(-E // (P * TB))
NB += NB % 2
NT = NB * TB
EP = NT * P
TURNS = NB // 2
QT = NT // 4
LO = 256
HI = -(-N // LO)
PADKEY = HI * LO - 1
BIG = 1 << 20
ITEMS = 11
CHUNKS = N // P // ITEMS
PER = CHUNKS * ITEMS
TAIL = N - P * PER
HUGE = 3.0e38
EPS = 1e-5
SROW = A + 4
DROW = 4
R1 = D + 3
R2 = D + 1
assert PADKEY >= N and CHUNKS % 2 == 1 and TAIL <= 32


def turns(eng, body):
    body(0, True, False)
    with eng.Fori(1, TURNS - 1) as j:
        body(j, False, False)
    body(TURNS - 1, False, True)


def wait(eng, sem, value):
    if not (isinstance(value, int) and value <= 0):
        eng.wait_ge(sem, value)


def hold(eng, sem, value, tick):
    eng.wait_ge(sem, value)
    if not isinstance(value, int):
        eng.sem_inc(tick, 1)


class Chain:

    def __init__(self, eng, sem, per):
        self.eng, self.sem, self.per = eng, sem, per

    def step(self, k):
        self.base, self.n = k * self.per, 0

    def link(self, ins):
        ins.then_inc(self.sem, 1)
        self.n += 1
        self.eng.wait_ge(self.sem, self.base + self.n)

    def close(self):
        for _ in range(self.per - self.n):
            self.eng.sem_inc(self.sem, 1)
        self.n = self.per


class Build:
    def __init__(self, nc, ctx):
        self.nc, self.ctx, self.own = nc, ctx, []

    def sb(self, name, shape, dt, ctx=None):
        return (ctx or self.ctx).enter_context(self.nc.sbuf_tensor(name, shape, dt))

    def ps(self, name, shape, dt, ctx):
        return ctx.enter_context(self.nc.psum_tensor(name, shape, dt))

    def sem(self, name, ctx=None):
        sem = self.nc.alloc_semaphore(name)
        if ctx is not None:
            self.own.append(sem)
        return sem

    def clear(self):
        self.nc.clear_and_free_semaphores(self.own)
        self.own = []
        self.nc.all_engine_barrier()

    def dram(self, name, shape):
        return self.nc.dram_tensor(name, shape, F32, kind="Internal").ap()


def setup_phase(b, g, src, dst, w, weights):
    nc = b.nc
    with ExitStack() as c:
        rows_i = b.sb("rows_i", [QT, 2, 4, P], I32, c)
        rows_f = b.sb("rows_f", [QT, 3, 4, P], F32, c)
        iota_i = b.sb("iota_i", [P, NT], I32, c)
        pos_i = b.sb("pos_i", [P, NT], I32, c)
        digit_i = b.sb("digit_i", [P, 2, NT], I32, c)
        digit_j = b.sb("digit_j", [P, 4, NT], I32, c)
        w2t = b.sb("w2t", [D, D], F32, c)
        hbase = b.sb("hbase", [P, 1], F32, c)
        tr = b.ps("setup_tr", [P, 3, 512], F32, c)
        small = b.ps("setup_small", [P, 4, 512], F32, c)
        padded = b.sem("padded", c)
        loaded = b.sem("loaded", c)
        wloaded = b.sem("wloaded", c)
        made = b.sem("made", c)
        cast = b.sem("cast", c)
        columns = b.sem("columns", c)
        dv = b.sem("setup_dve", c)
        small_done = b.sem("small_done", c)
        rows_ready = b.sem("rows_ready", c)
        full = E // P
        rest = E - full * P
        with nc.Block() as block:
            @block.gpsimd
            def _(pool):
                for t, value in ((g.ident, 0.0), (g.before, 1.0), (g.since, 1.0)):
                    nc.gpsimd.memset(t[:, :], value).then_inc(made, 1)
                nc.gpsimd.iota(iota_i[:, :], [[1, NT]], base=0, channel_multiplier=0).then_inc(made, 1)
                nc.gpsimd.iota(pos_i[:, :], [[P, NT]], base=0, channel_multiplier=1).then_inc(made, 1)
                pool.wait_ge(made, 5)
                nc.gpsimd.affine_select(out=g.ident[:, :], in_=g.ident[:, :], compare_op=ALU.not_equal, fill=1.0,
                                        base=0, pattern=[[-1, P]], channel_multiplier=1).then_inc(made, 1)
                nc.gpsimd.affine_select(out=g.before[:, :], in_=g.before[:, :], compare_op=ALU.is_gt, fill=0.0,
                                        base=0, pattern=[[1, P]], channel_multiplier=-1).then_inc(made, 1)
                nc.gpsimd.affine_select(out=g.since[:, :], in_=g.since[:, :], compare_op=ALU.is_ge, fill=0.0,
                                        base=0, pattern=[[-1, P]], channel_multiplier=1).then_inc(made, 1)

            @block.sync
            def _(sp):
                hold(sp, padded, 4, g.sp_tick)
                for k, a in ((0, src), (1, dst), (2, w)):
                    to = rows_f[:, 2] if k == 2 else rows_i[:, k]
                    for q in range(4):
                        n = min(QT, full - q * QT)
                        sp.dma_start(to[0:n, q, :], a[q * QT * P:(q * QT + n) * P].rearrange("(t p) -> t p", p=P)
                                     ).then_inc(loaded, 16)
                    sp.dma_start(to[full - 3 * QT:full - 3 * QT + 1, 3, 0:rest],
                                 a[full * P:E].rearrange("(t p) -> t p", t=1)).then_inc(loaded, 16)

            @block.scalar
            def _(act):
                act.wait_ge(padded, 4)
                W = weights
                loads = [(g.w1[:, :], W["W1"][0:3 * A, :]), (g.w2[:, :], W["W2"]),
                         (g.b1[:, :], W["b1"].rearrange("(p a) -> p a", a=1)),
                         (g.w1u[:, :], W["W1"][3 * A:3 * A + 1, :]), (g.uval[:, :], W["u0"]),
                         (g.b2[:, :], W["b2"].rearrange("(p a) -> p a", p=1).broadcast_to([P, D])),
                         (g.conv_b[:, :], W["bias0"].rearrange("p k o -> p (k o)").broadcast_to([P, 2 * D])),
                         (g.l2b[:, :], W["l2b"].rearrange("(p a) -> p a", p=1).broadcast_to([P, D])),
                         (g.l3b[:, :], W["l3b"].rearrange("(p a) -> p a", p=1).broadcast_to([P, D])),
                         (w2t[:, :], W["l2W"]), (g.l3w[:, :], W["l3W"]),
                         (g.root1[D:D + 1, :], W["bias1"].rearrange("p k o -> p (k o)"))]
                for k in range(2):
                    o = slice(k * D, k * D + D)
                    loads += [(g.conv0[0:D, o], W["init"][k]), (g.conv0[D:2 * D, o], W["root"][0, k]),
                              (g.root1[0:D, o], W["root"][1, k]), (g.conv1[o, o], W["weight"][0, k])]
                for to, a in loads:
                    act.dma_start(to, a).then_inc(wloaded, 16)
                g.n_loads = len(loads)

            @block.vector
            def _(dve):
                ch = Chain(dve, dv, 0)
                ch.step(0)
                nc.vector.memset(rows_i[:, :, 3, :], PADKEY).then_inc(padded, 1)
                nc.vector.memset(rows_f[:, 2, 3, :], 0.0).then_inc(padded, 1)
                nc.vector.memset(g.conv1[:, :], 0.0).then_inc(padded, 1)
                nc.vector.memset(g.ones_f[:, :], 1.0).then_inc(padded, 1)
                ch.link(nc.vector.memset(g.ones_b[:, :], 1.0))
                dve.wait_ge(made, 5)
                nc.vector.tensor_copy(g.iota16[:, :], iota_i[:, :])
                nc.vector.tensor_copy(g.pos[:, :], pos_i[:, :])
                dve.wait_ge(loaded, 16 * 15)
                for k in range(2):
                    nc.vector.tensor_copy(rows_f[:, k], rows_i[:, k]).then_inc(cast, 1)
                for k, to in enumerate((g.src, g.dst, g.w)):
                    dve.wait_ge(columns, k + 1)
                    ch.link(nc.vector.tensor_copy(to[:, :], tr[:, k, 0:NT]))
                for k, key in enumerate((g.src, g.dst)):
                    ch.link(nc.vector.tensor_copy(digit_i[:, k], key[:, :]))
                    ch.link(nc.vector.tensor_scalar(digit_j[:, 2 * k], digit_i[:, k], LO - 1, None, ALU.bitwise_and))
                    ch.link(nc.vector.tensor_scalar(digit_j[:, 2 * k + 1], digit_i[:, k], 8, None,
                                                    ALU.logical_shift_right))
                    ch.link(nc.vector.tensor_copy(g.lo[k][:, :], digit_j[:, 2 * k]))
                    ch.link(nc.vector.tensor_copy(g.hi[k][:, :], digit_j[:, 2 * k + 1]))
                dve.wait_ge(small_done, 1)
                ch.link(nc.vector.tensor_tensor(g.hb[:, :], small[:, 0, 0:1], g.b1[:, :], ALU.add))
                nc.vector.tensor_scalar(hbase[:, :], g.hb[:, :], 0.0, None, ALU.max).then_inc(rows_ready, 1)
                dve.wait_ge(small_done, 2)
                ch.link(nc.vector.memset(g.fill_m[:, :, D:D + 1], 0.0))
                nc.vector.tensor_tensor(g.base[0:1, :], small[0:1, 1, 0:D], g.b2[0:1, :], ALU.add).then_inc(rows_ready, 1)
                dve.wait_ge(small_done, 3)
                ch.link(nc.vector.tensor_copy(g.base_all[:, :], small[:, 2, 0:D]))
                ch.link(nc.vector.tensor_copy(g.fill_m[:, :, 0:D],
                                              g.base_all[:, :].unsqueeze(1).broadcast_to([P, ITEMS, D])))
                ch.link(nc.vector.memset(g.fill_0[:, :], 0.0))
                ch.link(nc.vector.memset(g.fill_nd[:, :, 0:1], 0.0))
                ch.link(nc.vector.memset(g.fill_nd[:, :, 1:2], float(EP)))
                ch.link(nc.vector.tensor_copy(g.l2w[:, :], small[0:D, 3, 0:D]))
                for to, row in ((g.fill_2, g.l2b), (g.fill_3, g.l3b)):
                    ch.link(nc.vector.tensor_copy(to[:, :, :], row[:, :].unsqueeze(1).broadcast_to([P, ITEMS, D])))

            @block.tensor
            def _(pe):
                pe.wait_ge(made, 8)
                pe.wait_ge(loaded, 16 * 15)
                pe.wait_ge(cast, 2)
                for k in range(3):
                    for q in range(4):
                        last = nc.tensor.transpose(tr[:, k, q * QT:(q + 1) * QT], rows_f[:, k, q, :],
                                                   g.ident[0:QT, 0:QT])
                    last.then_inc(columns, 1)
                pe.wait_ge(wloaded, 16 * g.n_loads)
                nc.tensor.transpose(small[0:D, 3, 0:D], w2t[:, :], g.ident[0:D, 0:D])
                pe.wait_ge(padded, 4)
                nc.tensor.matmul(small[:, 0, 0:1], g.w1u[0:1, :], g.uval[0:1, :], start=True, stop=True
                                 ).then_inc(small_done, 1)
                pe.wait_ge(rows_ready, 1)
                nc.tensor.matmul(small[0:1, 1, 0:D], hbase[:, :], g.w2[:, :], start=True, stop=True
                                 ).then_inc(small_done, 1)
                pe.wait_ge(rows_ready, 2)
                nc.tensor.matmul(small[:, 2, 0:D], g.ones_f[0:1, 0:P], g.base[0:1, :], start=True, stop=True
                                 ).then_inc(small_done, 1)


def hist_phase(b, g):
    nc = b.nc
    keys = [(g.lo[0], LO, g.first[0]), (g.hi[0], HI, g.first[1]), (g.lo[1], LO, g.first[2]), (g.hi[1], HI, g.first[3])]
    with ExitStack() as c:
        hot = b.sb("hist_hot", [P, 2, TB, 4, HI], BF16, c)
        counts = b.sb("hist_counts", [P, 4, HI], F32, c)
        incl = b.sb("hist_incl", [P, 4, HI], F32, c)
        acc = b.ps("hist_acc", [P, 4, 512], F32, c)
        hot_ready = b.sem("hot_ready", c)
        hot_used = b.sem("hot_used", c)
        chain = b.sem("hist_chain", c)
        with nc.Block() as block:
            @block.vector
            def _(dve):
                def body(j, first, last):
                    for s in range(2):
                        if not first:
                            dve.wait_ge(hot_used, 2 * j + s - 1)
                        for i in range(TB):
                            for k, (digit, n, _) in enumerate(keys):
                                ins = nc.vector.tensor_scalar(hot[:, s, i, k, 0:n], g.iota16[:, 0:n],
                                                              digit[:, bass.ds((2 * j + s) * TB + i, 1)], None,
                                                              ALU.is_equal)
                        ins.then_inc(hot_ready, 1)
                turns(dve, body)
                ch = Chain(dve, chain, 0)
                ch.step(0)
                dve.wait_ge(hot_used, NB)
                for k, (_, n, start) in enumerate(keys):
                    ch.link(nc.vector.tensor_copy(counts[:, k, 0:n], acc[:, k, 0:n]))
                    ch.link(nc.vector.tensor_tensor_scan(incl[:, k, 0:n], g.ones_f[:, 0:n], counts[:, k, 0:n], 0.0,
                                                         ALU.mult, ALU.add))
                    ch.link(nc.vector.tensor_tensor(start[:, 0:n], incl[:, k, 0:n], counts[:, k, 0:n], ALU.subtract))

            @block.tensor
            def _(pe):
                def body(j, first, last):
                    for s in range(2):
                        wait(pe, hot_ready, 2 * j + s + 1)
                        for i in range(TB):
                            for k, (_, n, _) in enumerate(keys):
                                opens = first and s == 0 and i == 0
                                closes = last and s == 1 and i == TB - 1
                                ins = nc.tensor.matmul(acc[:, k, 0:n], g.ones_b[:, :], hot[:, s, i, k, 0:n],
                                                       start=opens, stop=closes, skip_group_check=True)
                        ins.then_inc(hot_used, 1)
                turns(pe, body)


def radix_phase(b, g, name, rows_in, make, width, digit, buckets, first_pos, out, fill):
    nc = b.nc
    loads_w = 0 if rows_in is None else rows_in.shape[1]
    with ExitStack() as c:
        rows = b.sb(name + "_rows", [P, 2, TB, width], F32, c)
        hot = b.sb(name + "_hot", [P, 2, TB, buckets], BF16, c)
        junk = b.sb(name + "_junk", [P, buckets], BF16, c)
        place_f = b.sb(name + "_place_f", [P, 2, TB], F32, c)
        place_i = b.sb(name + "_place_i", [P, 2, TB], I32, c)
        seen = b.ps(name + "_seen", [P, 512], F32, c)
        cleared = b.sem(name + "_cleared", c)
        loaded = [b.sem(f"{name}_loaded{s}", c) for s in range(2)]
        made = b.sem(name + "_made", c)
        hot_ready = b.sem(name + "_hot_ready", c)
        seen_ready = b.sem(name + "_seen_ready", c)
        summed = b.sem(name + "_summed", c)
        place_ready = b.sem(name + "_place_ready", c)
        sent = [b.sem(f"{name}_sent{s}", c) for s in range(2)]
        filled = b.sem(name + "_filled", c)
        tick = b.sem(name + "_tick", c)
        per_load = 16
        with nc.Block() as block:
            @block.sync
            def _(sp):
                if rows_in is None:
                    return

                def body(j, first, last):
                    for s in range(2):
                        blk = 2 * j + s
                        if first:
                            hold(sp, cleared, 1, g.sp_tick)
                        else:
                            hold(sp, sent[s], 16 * TB * j, g.sp_tick)
                        if last and s == 1 and E < EP and loads_w == A:
                            lo = (NB - 1) * TB * P
                            whole = (E - lo) // P
                            rest = E - lo - whole * P
                            sp.dma_start(rows[:, s, 0:whole, 0:A], rows_in[lo:lo + whole * P, :]
                                         .rearrange("(i p) c -> p i c", p=P)).then_inc(loaded[s], 16)
                            sp.dma_start(rows[0:rest, s, whole, 0:A], rows_in[lo + whole * P:E, :]
                                         ).then_inc(loaded[s], 16)
                        else:
                            sp.dma_start(rows[:, s, :, 0:loads_w], rows_in[bass.ds(blk * (TB * P), TB * P), :]
                                         .rearrange("(i p) c -> p i c", p=P)).then_inc(loaded[s], 16)
                turns(sp, body)

            @block.scalar
            def _(act):
                fill(act, filled)

            @block.gpsimd
            def _(pool):
                def body(j, first, last):
                    for s in range(2):
                        hold(pool, place_ready, 2 * j + s + 1, tick)
                        if loads_w:
                            extra = 1 if (last and s == 1 and loads_w == A) else 0
                            hold(pool, loaded[s], 16 * (j + 1 + extra), tick)
                        if make:
                            hold(pool, made, 2 * j + s + 1, tick)
                        for i in range(TB):
                            nc.gpsimd.indirect_dma_start(
                                out[:, :], bass.IndirectOffsetOnAxis(ap=place_i[:, s, i:i + 1], axis=0),
                                rows[:, s, i, :], None, bounds_check=g.lim_edges, oob_is_err=False
                            ).then_inc(sent[s], 16)
                g.lim_edges = pool.to_reg(EP - 1)
                turns(pool, body)
                for s in range(2):
                    pool.wait_ge(sent[s], 16 * TB * TURNS)

            @block.vector
            def _(dve):
                nc.vector.memset(rows[:, :, :, :], 0.0).then_inc(cleared, 1)
                dve.wait_ge(cleared, 1)

                def one_hot(j, s, i):
                    if digit is None:
                        if i == 0:
                            dve.wait_ge(loaded[s], 16 * (j + 1))
                        col = rows[:, s, i, width - 1:width]
                    else:
                        col = digit[:, bass.ds((2 * j + s) * TB + i, 1)]
                    nc.vector.tensor_scalar(hot[:, s, i, :], g.iota16[:, 0:buckets], col, None,
                                            ALU.is_equal).then_inc(hot_ready, 1)

                for i in range(TB):
                    one_hot(0, 0, i)

                def body(j, first, last):
                    for s in range(2):
                        blk = 2 * j + s
                        if not first:
                            dve.wait_ge(sent[s], 16 * TB * j)
                        for k, (at, table) in enumerate(make):
                            ins = nc.vector.tensor_scalar(rows[:, s, :, at], table[:, bass.ds(blk * TB, TB)], 1.0,
                                                          None, ALU.mult)
                        if make:
                            ins.then_inc(made, 1)
                        for i in range(TB):
                            dve.wait_ge(seen_ready, blk * TB + i + 1)
                            nc.vector.scalar_tensor_tensor(junk[:, :], seen[:, 0:buckets], 1.0, hot[:, s, i, :],
                                                           ALU.mult, ALU.mult, accum_out=place_f[:, s, i:i + 1]
                                                           ).then_inc(summed, 1)
                            if not (last and s == 1):
                                jn, sn = (j, 1) if s == 0 else (j + 1, 0)
                                one_hot(jn, sn, i)
                        dve.wait_ge(summed, (blk + 1) * TB)
                        nc.vector.tensor_scalar(place_i[:, s, :], place_f[:, s, :], 1.0, None, ALU.mult
                                                ).then_inc(place_ready, 1)
                turns(dve, body)

            @block.tensor
            def _(pe):
                nc.tensor.matmul(seen[:, 0:buckets], g.ident[:, :], first_pos[:, 0:buckets], start=True, stop=False,
                                 skip_group_check=True)

                def body(j, first, last):
                    for s in range(2):
                        for i in range(TB):
                            t = (2 * j + s) * TB + i
                            pe.wait_ge(hot_ready, t + 1)
                            nc.tensor.matmul(seen[:, 0:buckets], g.before[:, :], hot[:, s, i, :], start=False,
                                             stop=False, skip_group_check=True).then_inc(seen_ready, 1)
                            pe.wait_ge(summed, t + 1)
                            nc.tensor.matmul(seen[:, 0:buckets], g.since[:, :], hot[:, s, i, :], start=False,
                                             stop=last and s == 1 and i == TB - 1, skip_group_check=True)
                turns(pe, body)


def tables_phase(b, g, o, rows, cols):
    nc = b.nc
    key_at = 0 if o.name == "S" else 1
    with ExitStack() as c:
        cur = b.sb(o.name + "_cur", [P, NT, 4], F32, c)
        nxt = b.sb(o.name + "_nxt", [P, NT, 4], F32, c)
        same = b.sb(o.name + "_same", [P, NT], F32, c)
        flag_rows = b.sb(o.name + "_flag_rows", [QT, 4, P], F32, c)
        zero = b.sb(o.name + "_zero", [1, 1], F32, c)
        tr = b.ps(o.name + "_flag_tr", [QT, 4, P], F32, c)
        cleared = b.sem(o.name + "_cleared", c)
        loaded = b.sem(o.name + "_loaded", c)
        ch_sem = b.sem(o.name + "_chain", c)
        same_ready = b.sem(o.name + "_same_ready", c)
        turned = b.sem(o.name + "_turned", c)
        rows_ready = b.sem(o.name + "_rows_ready", c)
        stored = b.sem(o.name + "_stored", c)
        n_loads = 9
        with nc.Block() as block:
            @block.sync
            def _(sp):
                hold(sp, cleared, 1, g.sp_tick)
                for q in range(4):
                    a = q * QT
                    r = rows[a * P:(a + QT) * P, cols:cols + 4].rearrange("(t p) c -> p t c", p=P)
                    sp.dma_start(cur[:, a:a + QT, :], r).then_inc(loaded, 16)
                    k = QT if q < 3 else QT - 1
                    r = rows[a * P + 1:(a + k) * P + 1, cols:cols + 4].rearrange("(t p) c -> p t c", p=P)
                    sp.dma_start(nxt[:, a:a + k, :], r).then_inc(loaded, 16)
                sp.dma_start(nxt[0:P - 1, NT - 1, :], rows[EP - P + 1:EP, cols:cols + 4]).then_inc(loaded, 16)
                hold(sp, rows_ready, 1, g.sp_tick)
                for q in range(4):
                    k = QT if q < 3 else QT - 1
                    sp.dma_start(o.flags[q * QT * P + 1:(q * QT + k) * P + 1].rearrange("(t p) -> t p", p=P),
                                 flag_rows[0:k, q, :]).then_inc(stored, 16)
                sp.dma_start(o.flags[EP - P + 1:EP].rearrange("(t p) -> t p", t=1),
                             flag_rows[QT - 1:QT, 3, 0:P - 1]).then_inc(stored, 16)
                sp.dma_start(o.flags[0:1].rearrange("(t p) -> t p", t=1), zero[:, :]).then_inc(stored, 16)
                hold(sp, stored, 16 * 6, g.sp_tick)

            @block.vector
            def _(dve):
                ch = Chain(dve, ch_sem, 0)
                ch.step(0)
                nc.vector.memset(zero[:, :], 0.0)
                nc.vector.memset(nxt[:, NT - 1, :], -1.0).then_inc(cleared, 1)
                dve.wait_ge(loaded, 16 * n_loads)
                nc.vector.tensor_tensor(same[:, :], cur[:, :, key_at], nxt[:, :, key_at], ALU.is_equal
                                        ).then_inc(same_ready, 1)
                dve.wait_ge(same_ready, 1)
                ch.link(nc.vector.scalar_tensor_tensor(o.put[:, :], same[:, :], float(BIG), cur[:, :, key_at],
                                                       ALU.mult, ALU.add))
                ch.link(nc.vector.tensor_scalar(o.get[:, :], cur[:, :, 1 - key_at], float(N - 1), None, ALU.min))
                ch.link(nc.vector.tensor_copy(o.w[:, :], cur[:, :, 2]))
                dve.wait_ge(turned, 1)
                nc.vector.tensor_copy(flag_rows[:, :, :], tr[:, :, :]).then_inc(rows_ready, 1)

            @block.tensor
            def _(pe):
                pe.wait_ge(same_ready, 1)
                for q in range(4):
                    last = nc.tensor.transpose(tr[:, q, :], same[:, q * QT:(q + 1) * QT], g.ident[:, :])
                last.then_inc(turned, 1)


def load_flags(sp, g, o, ring, ready, used, j, s):
    if used is not None:
        hold(sp, used, 2 * j + s - 1, g.sp_tick)
    blk = 2 * j + s
    np_ = ring.shape[0]
    sp.dma_start(ring[:, s, :], o.flags[bass.ds(blk * (TB * P), TB * P)].rearrange("(a n) -> a n", a=1)
                 .broadcast_to([np_, TB * P])).then_inc(ready[s], 16)


def degree_phase(b, g, o, table):
    nc = b.nc
    with ExitStack() as c:
        flags = b.sb("deg_flags", [1, 2, TB * P], F32, c)
        deg = b.sb("deg_deg", [1, 2, TB * P], F32, c)
        low = b.sb("deg_low", [P, TB], F32, c)
        root = b.sb("deg_root", [P, 2, TB], F32, c)
        inv = b.sb("deg_inv", [P, TB], F32, c)
        some = b.sb("deg_some", [P, TB], F32, c)
        wring = b.sb("deg_wring", [P, 2, TB], F32, c)
        put = b.sb("deg_put", [P, 2, TB], I32, c)
        stage = b.sb("deg_stage", [P, 2, TB, 2], F32, c)
        wrow = b.ps("deg_wrow", [1, 2, TB * P], F32, c)
        col = b.ps("deg_col", [P, 2, 512], F32, c)
        flags_in = [b.sem(f"deg_flags_in{s}", c) for s in range(2)]
        wrow_ready = b.sem("deg_wrow_ready", c)
        scanned = b.sem("deg_scanned", c)
        col_ready = b.sem("deg_col_ready", c)
        low_ready = b.sem("deg_low_ready", c)
        root_ready = b.sem("deg_root_ready", c)
        chain = b.sem("deg_chain", c)
        stage_ready = b.sem("deg_stage_ready", c)
        sent = [b.sem(f"deg_sent{s}", c) for s in range(2)]
        zeroed = b.sem("deg_zeroed", c)
        wring_ready = b.sem("deg_wring_ready", c)
        with nc.Block() as block:
            @block.sync
            def _(sp):
                def body(j, first, last):
                    for s in range(2):
                        load_flags(sp, g, o, flags, flags_in, None if first else scanned, j, s)
                turns(sp, body)

            @block.tensor
            def _(pe):
                def body(j, first, last):
                    for s in range(2):
                        blk = 2 * j + s
                        pe.wait_ge(wring_ready, blk + 1)
                        if not first:
                            pe.wait_ge(scanned, blk - 1)
                        for i in range(TB):
                            ins = nc.tensor.matmul(wrow[0:1, s, i * P:(i + 1) * P], wring[:, s, i:i + 1],
                                                   g.ident[:, :], start=True, stop=True)
                        ins.then_inc(wrow_ready, 1)
                        pe.wait_ge(scanned, blk + 1)
                        if not first:
                            pe.wait_ge(stage_ready, blk - 1)
                        for i in range(TB):
                            ins = nc.tensor.matmul(col[:, s, i:i + 1], deg[0:1, s, i * P:(i + 1) * P],
                                                   g.ones_f[0:1, 0:1], start=True, stop=True)
                        ins.then_inc(col_ready, 1)
                turns(pe, body)

            @block.scalar
            def _(act):
                def body(j, first, last):
                    for s in range(2):
                        act.wait_ge(low_ready, 2 * j + s + 1)
                        nc.scalar.activation(root[:, s, :], low[:, :], ACT.Sqrt).then_inc(root_ready, 1)
                turns(act, body)

            @block.vector
            def _(dve):
                ch = Chain(dve, chain, 2)
                nc.vector.memset(deg[:, 1, :], 0.0).then_inc(zeroed, 1)
                dve.wait_ge(zeroed, 1)

                def body(j, first, last):
                    for s in range(2):
                        blk = 2 * j + s
                        ch.step(blk)
                        if not first:
                            dve.wait_ge(col_ready, blk - 1)
                            dve.wait_ge(sent[s], 16 * TB * j)
                        nc.vector.tensor_scalar(wring[:, s, :], o.w[:, bass.ds(blk * TB, TB)], 1.0, None, ALU.mult
                                                ).then_inc(wring_ready, 1)
                        nc.vector.tensor_scalar(put[:, s, :], o.put[:, bass.ds(blk * TB, TB)], 1.0, None, ALU.mult)
                        nc.vector.tensor_scalar(stage[:, s, :, 1], g.pos[:, bass.ds(blk * TB, TB)], 1.0, None,
                                                ALU.mult)
                        dve.wait_ge(flags_in[s], 16 * (j + 1))
                        dve.wait_ge(wrow_ready, blk + 1)
                        dve.wait_ge(scanned, blk) if not first or s else None
                        nc.vector.tensor_tensor_scan(deg[:, s, :], flags[:, s, :], wrow[:, s, :],
                                                     deg[:, 1 - s, TB * P - 1:TB * P], ALU.mult, ALU.add
                                                     ).then_inc(scanned, 1)
                        dve.wait_ge(col_ready, blk + 1)
                        nc.vector.tensor_scalar(low[:, :], col[:, s, 0:TB], 1e-12, None, ALU.max
                                                ).then_inc(low_ready, 1)
                        nc.vector.tensor_scalar(some[:, :], col[:, s, 0:TB], 0.0, None, ALU.is_gt)
                        dve.wait_ge(root_ready, blk + 1)
                        ch.link(nc.vector.reciprocal(inv[:, :], root[:, s, :]))
                        nc.vector.tensor_tensor(o.root[:, bass.ds(blk * TB, TB)], inv[:, :], some[:, :], ALU.mult)
                        nc.vector.tensor_tensor(stage[:, s, :, 0], inv[:, :], some[:, :], ALU.mult
                                                ).then_inc(stage_ready, 1)
                        dve.wait_ge(stage_ready, blk + 1)
                        ch.close()
                turns(dve, body)

            @block.gpsimd
            def _(pool):
                limit = pool.to_reg(N - 1)

                def body(j, first, last):
                    for s in range(2):
                        hold(pool, stage_ready, 2 * j + s + 1, g.pool_tick)
                        for i in range(TB):
                            nc.gpsimd.indirect_dma_start(
                                table[:, :], bass.IndirectOffsetOnAxis(ap=put[:, s, i:i + 1], axis=0),
                                stage[:, s, i, :], None, bounds_check=limit, oob_is_err=False
                            ).then_inc(sent[s], 16)
                turns(pool, body)
                for s in range(2):
                    pool.wait_ge(sent[s], 16 * TB * TURNS)


def edge_mlp_phase(b, g, o, rows, table):
    nc = b.nc
    with ExitStack() as c:
        attr = b.sb("mlp_attr", [P, 2, TB, A], F32, c)
        flags = b.sb("mlp_flags", [A, 2, TB * P], F32, c)
        cut = b.sb("mlp_cut", [A, TB * P], F32, c)
        cat = b.sb("mlp_cat", [3 * A, 2, TB * P], F32, c)
        most = b.sb("mlp_most", [A, 2, TB * P], F32, c)
        cnt = b.sb("mlp_cnt", [A, 2, TB * P], F32, c)
        rcnt = b.sb("mlp_rcnt", [A, TB * P], F32, c)
        hid = b.sb("mlp_hid", [P, TB * P], F32, c)
        stage = b.sb("mlp_stage", [P, 2, TB, D + 1], F32, c)
        root = b.sb("mlp_root", [P, TB], F32, c)
        put = b.sb("mlp_put", [P, 2, TB], I32, c)
        turned = b.ps("mlp_turned", [A, 2, TB * P], F32, c)
        hidden = b.ps("mlp_hidden", [P, 2, 512], F32, c)
        res = b.ps("mlp_res", [P, 2, 512], F32, c)
        cnt_col = b.ps("mlp_cnt_col", [P, 2, 512], F32, c)
        flags_in = [b.sem(f"mlp_flags_in{s}", c) for s in range(2)]
        attr_in = [b.sem(f"mlp_attr_in{s}", c) for s in range(2)]
        turned_ready = b.sem("mlp_turned_ready", c)
        chain = b.sem("mlp_chain", c)
        cat_ready = b.sem("mlp_cat_ready", c)
        hidden_ready = b.sem("mlp_hidden_ready", c)
        hid_ready = b.sem("mlp_hid_ready", c)
        res_ready = b.sem("mlp_res_ready", c)
        root_ready = b.sem("mlp_root_ready", c)
        stage_ready = b.sem("mlp_stage_ready", c)
        put_ready = b.sem("mlp_put_ready", c)
        zeroed = b.sem("mlp_zeroed", c)
        sent = [b.sem(f"mlp_sent{s}", c) for s in range(2)]
        with nc.Block() as block:
            @block.sync
            def _(sp):
                def body(j, first, last):
                    for s in range(2):
                        if not first:
                            hold(sp, turned_ready, 2 * j + s - 1, g.sp_tick)
                        sp.dma_start(attr[:, s, :, :], rows[bass.ds((2 * j + s) * (TB * P), TB * P), 0:A]
                                     .rearrange("(i p) c -> p i c", p=P)).then_inc(attr_in[s], 16)
                        load_flags(sp, g, o, flags, flags_in, None if first else cat_ready, j, s)
                turns(sp, body)

            @block.tensor
            def _(pe):
                def body(j, first, last):
                    for s in range(2):
                        blk = 2 * j + s
                        hold(pe, attr_in[s], 16 * (j + 1), g.pe_tick)
                        if not first:
                            hold(pe, cat_ready, blk - 1, g.pe_tick)
                        for i in range(TB):
                            ins = nc.tensor.transpose(turned[:, s, i * P:(i + 1) * P], attr[:, s, i, :],
                                                      g.ident[:, :])
                        ins.then_inc(turned_ready, 1)
                        hold(pe, cat_ready, blk + 1, g.pe_tick)
                        if not first:
                            hold(pe, hid_ready, blk - 1, g.pe_tick)
                        nc.tensor.matmul(hidden[:, s, :], g.w1[:, :], cat[:, s, :], start=True, stop=True
                                         ).then_inc(hidden_ready, 1)
                        hold(pe, hid_ready, blk + 1, g.pe_tick)
                        if not first:
                            hold(pe, stage_ready, blk - 1, g.pe_tick)
                        for i in range(TB):
                            nc.tensor.matmul(res[:, s, i * D:(i + 1) * D], hid[:, i * P:(i + 1) * P], g.w2[:, :],
                                             start=True, stop=True)
                            ins = nc.tensor.matmul(cnt_col[:, s, i:i + 1],
                                                   cnt[0:1, s, i * P:(i + 1) * P], g.ones_f[0:1, 0:1],
                                                   start=True, stop=True)
                        ins.then_inc(res_ready, 1)
                turns(pe, body)

            @block.scalar
            def _(act):
                def body(j, first, last):
                    for s in range(2):
                        blk = 2 * j + s
                        act.wait_ge(hidden_ready, blk + 1)
                        if not (first and s == 0):
                            act.wait_ge(res_ready, blk)
                        nc.scalar.activation(hid[:, :], hidden[:, s, :], ACT.Relu, bias=g.hb[:, 0:1]
                                             ).then_inc(hid_ready, 1)
                        act.wait_ge(res_ready, blk + 1)
                        if not (first and s == 0):
                            act.wait_ge(stage_ready, blk)
                        nc.scalar.activation(root[:, :], cnt_col[:, s, 0:TB], ACT.Sqrt
                                             ).then_inc(root_ready, 1)
                turns(act, body)

            @block.vector
            def _(dve):
                ch = Chain(dve, chain, 5)
                end = slice(TB * P - 1, TB * P)
                for t in (cat, most, cnt):
                    nc.vector.memset(t[:, 1, :], 0.0).then_inc(zeroed, 1)
                dve.wait_ge(zeroed, 3)

                def finish(j, s, first):
                    blk = 2 * j + s
                    dve.wait_ge(res_ready, blk + 1)
                    if not first:
                        dve.wait_ge(sent[s], 16 * TB * j)
                    nc.vector.tensor_scalar(put[:, s, :], o.put[:, bass.ds(blk * TB, TB)], 1.0, None, ALU.mult
                                            ).then_inc(put_ready, 1)
                    nc.vector.tensor_tensor(stage[:, s, :, 0:D],
                                            res[:, s, 0:TB * D].rearrange("p (i f) -> p i f", f=D),
                                            g.b2[:, :].unsqueeze(1).broadcast_to([P, TB, D]), ALU.add)
                    dve.wait_ge(root_ready, blk + 1)
                    nc.vector.reciprocal(o.root[:, bass.ds(blk * TB, TB)], root[:, :])
                    nc.vector.reciprocal(stage[:, s, :, D], root[:, :]).then_inc(stage_ready, 1)

                def body(j, first, last):
                    for s in range(2):
                        blk = 2 * j + s
                        ch.step(blk)
                        dve.wait_ge(flags_in[s], 16 * (j + 1))
                        dve.wait_ge(turned_ready, blk + 1)
                        if not first:
                            dve.wait_ge(res_ready, blk - 1)
                        ch.link(nc.vector.tensor_scalar(cut[:, :], flags[:, s, :], 1.0, HUGE, ALU.subtract,
                                                        ALU.mult))
                        ch.link(nc.vector.tensor_tensor_scan(cnt[:, s, :], flags[:, s, :], g.ones_f[0:A, :],
                                                             cnt[:, 1 - s, end], ALU.mult, ALU.add))
                        nc.vector.tensor_tensor_scan(cat[0:A, s, :], flags[:, s, :], turned[:, s, :],
                                                     cat[0:A, 1 - s, end], ALU.mult, ALU.add)
                        ch.link(nc.vector.tensor_tensor_scan(most[:, s, :], cut[:, :], turned[:, s, :],
                                                             most[:, 1 - s, end], ALU.add, ALU.max))
                        ch.link(nc.vector.reciprocal(rcnt[:, :], cnt[:, s, :]))
                        nc.vector.tensor_copy(cat[A:2 * A, s, :], most[:, s, :])
                        ch.link(nc.vector.tensor_tensor(cat[2 * A:3 * A, s, :], cat[0:A, s, :], rcnt[:, :], ALU.mult))
                        dve.sem_inc(cat_ready, 1)
                        finish(j, s, first)
                turns(dve, body)

            @block.gpsimd
            def _(pool):
                limit = pool.to_reg(N - 1)

                def body(j, first, last):
                    for s in range(2):
                        hold(pool, stage_ready, 2 * j + s + 1, g.pool_tick)
                        for i in range(TB):
                            nc.gpsimd.indirect_dma_start(
                                table[:, :], bass.IndirectOffsetOnAxis(ap=put[:, s, i:i + 1], axis=0),
                                stage[:, s, i, :], None, bounds_check=limit, oob_is_err=False
                            ).then_inc(sent[s], 16)
                turns(pool, body)
                for s in range(2):
                    pool.wait_ge(sent[s], 16 * TB * TURNS)


def message_phase(b, g, o, name, table, width, factor_at, weight, out, bias=None, scale_out=False, saved=None):
    nc = b.nc
    with ExitStack() as c:
        got = b.sb(name + "_got", [P, 2, TB, width], F32, c)
        msg = b.sb(name + "_msg", [P, 2, TB, D], F32, c)
        fac = b.sb(name + "_fac", [P, 2, TB], F32, c)
        get = b.sb(name + "_get", [P, 2, TB], I32, c)
        put = b.sb(name + "_put", [P, 2, TB], I32, c)
        flags = b.sb(name + "_flags", [D, 2, TB * P], F32, c)
        tot = b.sb(name + "_tot", [D, 2, TB * P], F32, c)
        stage = b.sb(name + "_stage", [P, 2, TB, D], F32, c)
        scaled = b.sb(name + "_scaled", [P, TB, D], F32, c)
        turned = b.ps(name + "_turned", [D, 2, TB * P], F32, c)
        res = b.ps(name + "_res", [P, 2, 512], F32, c)
        flags_in = [b.sem(f"{name}_flags_in{s}", c) for s in range(2)]
        got_in = [b.sem(f"{name}_got_in{s}", c) for s in range(2)]
        sent = [b.sem(f"{name}_sent{s}", c) for s in range(2)]
        kept = [b.sem(f"{name}_kept{s}", c) for s in range(2)]
        get_ready = b.sem(name + "_get_ready", c)
        put_ready = b.sem(name + "_put_ready", c)
        fac_ready = b.sem(name + "_fac_ready", c)
        msg_ready = b.sem(name + "_msg_ready", c)
        turned_ready = b.sem(name + "_turned_ready", c)
        scanned = b.sem(name + "_scanned", c)
        res_ready = b.sem(name + "_res_ready", c)
        scaled_ready = b.sem(name + "_scaled_ready", c)
        stage_ready = b.sem(name + "_stage_ready", c)
        zeroed = b.sem(name + "_zeroed", c)
        store = saved is not None
        slot_sent = 16 if store else 16 * TB
        with nc.Block() as block:
            @block.gpsimd
            def _(pool):
                limit = pool.to_reg(N - 1)

                def gather(blk, turn, s):
                    hold(pool, get_ready, blk + 1, g.pool_tick)
                    if not isinstance(blk, int) or blk >= 2:
                        hold(pool, msg_ready, blk - 1, g.pool_tick)
                        if store:
                            hold(pool, kept[s], 16 * turn, g.pool_tick)
                    for i in range(TB):
                        nc.gpsimd.indirect_dma_start(
                            got[:, s, i, :], None, table[:, :],
                            bass.IndirectOffsetOnAxis(ap=get[:, s, i:i + 1], axis=0),
                            bounds_check=limit, oob_is_err=False).then_inc(got_in[s], 16)

                for s in range(2):
                    gather(s, 0, s)

                def body(j, first, last):
                    for s in range(2):
                        if not last:
                            gather(2 * j + 2 + s, j + 1, s)
                        if not store:
                            hold(pool, stage_ready, 2 * j + s + 1, g.pool_tick)
                            hold(pool, put_ready, 2 * j + s + 1, g.pool_tick)
                            for i in range(TB):
                                nc.gpsimd.indirect_dma_start(
                                    out[:, :], bass.IndirectOffsetOnAxis(ap=put[:, s, i:i + 1], axis=0),
                                    stage[:, s, i, :], None, bounds_check=limit, oob_is_err=False
                                ).then_inc(sent[s], 16)
                turns(pool, body)
                for s in range(2):
                    pool.wait_ge(got_in[s], 16 * TB * TURNS)
                    if not store:
                        pool.wait_ge(sent[s], slot_sent * TURNS)

            @block.sync
            def _(sp):
                def body(j, first, last):
                    for s in range(2):
                        load_flags(sp, g, o, flags, flags_in, None if first else scanned, j, s)
                turns(sp, body)

            @block.scalar
            def _(act):
                if not store:
                    return

                def body(j, first, last):
                    for s in range(2):
                        at = bass.ds((2 * j + s) * (TB * P), TB * P)
                        act.wait_ge(got_in[s], 16 * TB * (j + 1))
                        act.dma_start(saved[at, :].rearrange("(i p) c -> p i c", p=P), got[:, s]
                                      ).then_inc(kept[s], 16)
                        act.wait_ge(stage_ready, 2 * j + s + 1)
                        act.dma_start(out[at, :].rearrange("(i p) c -> p i c", p=P), stage[:, s]
                                      ).then_inc(sent[s], 16)
                turns(act, body)
                for s in range(2):
                    act.wait_ge(kept[s], 16 * TURNS)
                    act.wait_ge(sent[s], 16 * TURNS)

            @block.tensor
            def _(pe):
                def body(j, first, last):
                    for s in range(2):
                        blk = 2 * j + s
                        hold(pe, msg_ready, blk + 1, g.pe_tick)
                        if not first:
                            hold(pe, scanned, blk - 1, g.pe_tick)
                        for i in range(TB):
                            ins = nc.tensor.transpose(turned[:, s, i * P:(i + 1) * P], msg[:, s, i, :],
                                                      g.ident[:, :])
                        ins.then_inc(turned_ready, 1)
                        hold(pe, scanned, blk + 1, g.pe_tick)
                        if not first:
                            hold(pe, stage_ready, blk - 1, g.pe_tick)
                        for i in range(TB):
                            if weight is None:
                                ins = nc.tensor.transpose(res[:, s, i * D:(i + 1) * D], tot[:, s, i * P:(i + 1) * P],
                                                          g.ident[0:D, 0:D])
                            else:
                                ins = nc.tensor.matmul(res[:, s, i * D:(i + 1) * D], tot[:, s, i * P:(i + 1) * P],
                                                       weight[:, :], start=True, stop=True)
                        ins.then_inc(res_ready, 1)
                turns(pe, body)

            @block.vector
            def _(dve):
                def places(blk, s):
                    nc.vector.tensor_scalar(get[:, s, :], o.get[:, bass.ds(blk * TB, TB)], 1.0, None, ALU.mult
                                            ).then_inc(get_ready, 1)
                nc.vector.memset(tot[:, 1, :], 0.0).then_inc(zeroed, 1)
                for s in range(2):
                    places(s, s)
                dve.wait_ge(zeroed, 1)

                def body(j, first, last):
                    for s in range(2):
                        blk = 2 * j + s
                        at = bass.ds(blk * TB, TB)
                        dve.wait_ge(got_in[s], 16 * TB * (j + 1))
                        if not last:
                            places(blk + 2, s)
                        if not first:
                            dve.wait_ge(turned_ready, blk - 1)
                        if factor_at is None:
                            nc.vector.tensor_scalar(fac[:, s, :], o.w[:, at], 1.0, None, ALU.mult
                                                    ).then_inc(fac_ready, 1)
                        else:
                            nc.vector.tensor_tensor(fac[:, s, :], got[:, s, :, factor_at], o.w[:, at], ALU.mult
                                                    ).then_inc(fac_ready, 1)
                        dve.wait_ge(fac_ready, blk + 1)
                        nc.vector.tensor_tensor(msg[:, s], got[:, s, :, 0:D],
                                                fac[:, s, :].unsqueeze(2).broadcast_to([P, TB, D]), ALU.mult
                                                ).then_inc(msg_ready, 1)
                        dve.wait_ge(flags_in[s], 16 * (j + 1))
                        dve.wait_ge(turned_ready, blk + 1)
                        if not first:
                            dve.wait_ge(res_ready, blk - 1)
                        if not (first and s == 0):
                            dve.wait_ge(scanned, blk)
                        nc.vector.tensor_tensor_scan(tot[:, s, :], flags[:, s, :], turned[:, s, :],
                                                     tot[:, 1 - s, TB * P - 1:TB * P], ALU.mult, ALU.add
                                                     ).then_inc(scanned, 1)
                        if not first:
                            dve.wait_ge(sent[s], slot_sent * j)
                        if not store:
                            nc.vector.tensor_scalar(put[:, s, :], o.put[:, at], 1.0, None, ALU.mult
                                                    ).then_inc(put_ready, 1)
                        dve.wait_ge(res_ready, blk + 1)
                        r = res[:, s, 0:TB * D].rearrange("p (i f) -> p i f", f=D)
                        if scale_out:
                            nc.vector.tensor_tensor(scaled[:, :, :], r, o.root[:, at].unsqueeze(2)
                                                    .broadcast_to([P, TB, D]), ALU.mult).then_inc(scaled_ready, 1)
                            dve.wait_ge(scaled_ready, blk + 1)
                            r = scaled[:, :, :]
                        if bias is None:
                            nc.vector.tensor_copy(stage[:, s], r).then_inc(stage_ready, 1)
                        else:
                            nc.vector.tensor_tensor(stage[:, s], r, bias[:, :].unsqueeze(1).broadcast_to([P, TB, D]),
                                                    ALU.add).then_inc(stage_ready, 1)
                turns(dve, body)


def conv_phase(b, g, o, rows, table, out):
    nc = b.nc
    W2 = 2 * D
    with ExitStack() as c:
        pair = b.sb("conv_pair", [P, 2, TB, W2], F32, c)
        aux = b.sb("conv_aux", [P, 2, TB, R1 - D], F32, c)
        get = b.sb("conv_get", [P, 2, TB], I32, c)
        put = b.sb("conv_put", [P, 2, TB], I32, c)
        fac = b.sb("conv_fac", [P, TB], F32, c)
        lhs = b.sb("conv_lhs", [P, 2, TB * P], F32, c)
        hid = b.sb("conv_hid", [P, TB, W2], F32, c)
        msg = b.sb("conv_msg", [P, 2, TB, W2], F32, c)
        flags = b.sb("conv_flags", [P, 2, TB * P], F32, c)
        tot = b.sb("conv_tot", [P, 2, TB * P], F32, c)
        stage = b.sb("conv_stage", [P, 2, TB, W2], F32, c)
        pt = b.ps("conv_pt", [P, 2, 512], F32, c)
        pre = b.ps("conv_pre", [P, 2, 512], F32, c)
        turned = b.ps("conv_turned", [P, 2, 512], F32, c)
        res = b.ps("conv_res", [P, 2, 512], F32, c)
        flags_in = [b.sem(f"conv_flags_in{s}", c) for s in range(2)]
        aux_in = [b.sem(f"conv_aux_in{s}", c) for s in range(2)]
        x_in = [b.sem(f"conv_x_in{s}", c) for s in range(2)]
        got_in = [b.sem(f"conv_got_in{s}", c) for s in range(2)]
        sent = [b.sem(f"conv_sent{s}", c) for s in range(2)]
        get_ready = b.sem("conv_get_ready", c)
        put_ready = b.sem("conv_put_ready", c)
        pair_ready = b.sem("conv_pair_ready", c)
        pt_ready = b.sem("conv_pt_ready", c)
        lhs_ready = b.sem("conv_lhs_ready", c)
        pre_ready = b.sem("conv_pre_ready", c)
        hid_ready = b.sem("conv_hid_ready", c)
        fac_ready = b.sem("conv_fac_ready", c)
        msg_ready = b.sem("conv_msg_ready", c)
        turned_ready = b.sem("conv_turned_ready", c)
        scanned = b.sem("conv_scanned", c)
        res_ready = b.sem("conv_res_ready", c)
        stage_ready = b.sem("conv_stage_ready", c)
        zeroed = b.sem("conv_zeroed", c)
        with nc.Block() as block:
            @block.gpsimd
            def _(pool):
                limit_edges = pool.to_reg(EP)
                limit_nodes = pool.to_reg(N - 1)

                def gather(blk, s):
                    hold(pool, get_ready, blk + 1, g.pool_tick)
                    if not isinstance(blk, int) or blk >= 2:
                        hold(pool, pt_ready, blk - 1, g.pool_tick)
                    for i in range(TB):
                        nc.gpsimd.indirect_dma_start(
                            pair[:, s, i, 0:D], None, table[:, :],
                            bass.IndirectOffsetOnAxis(ap=get[:, s, i:i + 1], axis=0),
                            bounds_check=limit_edges, oob_is_err=False).then_inc(got_in[s], 16)

                for s in range(2):
                    gather(s, s)

                def body(j, first, last):
                    for s in range(2):
                        if not last:
                            gather(2 * j + 2 + s, s)
                        hold(pool, stage_ready, 2 * j + s + 1, g.pool_tick)
                        hold(pool, put_ready, 2 * j + s + 1, g.pool_tick)
                        for i in range(TB):
                            nc.gpsimd.indirect_dma_start(
                                out[:, :], bass.IndirectOffsetOnAxis(ap=put[:, s, i:i + 1], axis=0),
                                stage[:, s, i, :], None, bounds_check=limit_nodes, oob_is_err=False
                            ).then_inc(sent[s], 16)
                turns(pool, body)
                for s in range(2):
                    pool.wait_ge(got_in[s], 16 * TB * TURNS)
                    pool.wait_ge(sent[s], 16 * TB * TURNS)

            @block.sync
            def _(sp):
                def body(j, first, last):
                    for s in range(2):
                        blk = 2 * j + s
                        if not first:
                            hold(sp, fac_ready, blk - 1, g.sp_tick)
                            hold(sp, pt_ready, blk - 1, g.sp_tick)
                        r = rows[bass.ds(blk * (TB * P), TB * P), :].rearrange("(i p) c -> p i c", p=P)
                        sp.dma_start(aux[:, s], r[:, :, D:R1]).then_inc(aux_in[s], 16)
                        sp.dma_start(pair[:, s, :, D:W2], r[:, :, 0:D]).then_inc(x_in[s], 16)
                        load_flags(sp, g, o, flags, flags_in, None if first else scanned, j, s)
                turns(sp, body)

            @block.scalar
            def _(act):
                def body(j, first, last):
                    for s in range(2):
                        blk = 2 * j + s
                        act.wait_ge(pt_ready, blk + 1)
                        if not first:
                            act.wait_ge(pre_ready, blk - 1)
                        nc.scalar.activation(lhs[:, s, :], pt[:, s, :], ACT.Copy).then_inc(lhs_ready, 1)
                turns(act, body)

            @block.tensor
            def _(pe):
                def body(j, first, last):
                    for s in range(2):
                        blk = 2 * j + s
                        hold(pe, pair_ready, blk + 1, g.pe_tick)
                        hold(pe, x_in[s], 16 * (j + 1), g.pe_tick)
                        if not first:
                            hold(pe, lhs_ready, blk - 1, g.pe_tick)
                        for i in range(TB):
                            ins = nc.tensor.transpose(pt[:, s, i * P:(i + 1) * P], pair[:, s, i, :], g.ident[:, :])
                        ins.then_inc(pt_ready, 1)
                        hold(pe, lhs_ready, blk + 1, g.pe_tick)
                        if not first:
                            hold(pe, hid_ready, blk - 1, g.pe_tick)
                        for i in range(TB):
                            ins = nc.tensor.matmul(pre[:, s, i * P:(i + 1) * P], lhs[:, s, i * P:(i + 1) * P],
                                                   g.conv0[:, :], start=True, stop=True)
                        ins.then_inc(pre_ready, 1)
                        hold(pe, msg_ready, blk + 1, g.pe_tick)
                        if not first:
                            hold(pe, scanned, blk - 1, g.pe_tick)
                        for i in range(TB):
                            ins = nc.tensor.transpose(turned[:, s, i * P:(i + 1) * P], msg[:, s, i, :],
                                                      g.ident[:, :])
                        ins.then_inc(turned_ready, 1)
                        hold(pe, scanned, blk + 1, g.pe_tick)
                        if not first:
                            hold(pe, stage_ready, blk - 1, g.pe_tick)
                        for i in range(TB):
                            ins = nc.tensor.matmul(res[:, s, i * P:(i + 1) * P], tot[:, s, i * P:(i + 1) * P],
                                                   g.conv1[:, :], start=True, stop=True)
                        ins.then_inc(res_ready, 1)
                turns(pe, body)

            @block.vector
            def _(dve):
                def places(j, s):
                    dve.wait_ge(aux_in[s], 16 * (j + 1))
                    nc.vector.tensor_scalar(get[:, s, :], aux[:, s, :, 1], 1.0, None, ALU.mult
                                            ).then_inc(get_ready, 1)
                nc.vector.memset(tot[:, 1, :], 0.0).then_inc(zeroed, 1)
                for s in range(2):
                    places(0, s)
                dve.wait_ge(zeroed, 1)

                def body(j, first, last):
                    for s in range(2):
                        blk = 2 * j + s
                        at = bass.ds(blk * TB, TB)
                        dve.wait_ge(got_in[s], 16 * TB * (j + 1))
                        nc.vector.tensor_tensor(pair[:, s, :, 0:D], pair[:, s, :, 0:D],
                                                aux[:, s, :, 0:1].broadcast_to([P, TB, D]), ALU.mult
                                                ).then_inc(pair_ready, 1)
                        if not (first and s == 0):
                            dve.wait_ge(msg_ready, blk)
                        nc.vector.tensor_tensor(fac[:, :], aux[:, s, :, 0], o.w[:, at], ALU.mult
                                                ).then_inc(fac_ready, 1)
                        dve.wait_ge(pre_ready, blk + 1)
                        nc.vector.tensor_tensor(hid[:, :, :], pre[:, s, :].rearrange("p (i f) -> p i f", f=W2),
                                                g.conv_b[:, :].unsqueeze(1).broadcast_to([P, TB, W2]), ALU.add
                                                ).then_inc(hid_ready, 1)
                        dve.wait_ge(hid_ready, blk + 1)
                        dve.wait_ge(fac_ready, blk + 1)
                        if not first:
                            dve.wait_ge(turned_ready, blk - 1)
                        nc.vector.scalar_tensor_tensor(msg[:, s], hid[:, :, :], 0.0,
                                                       fac[:, :].unsqueeze(2).broadcast_to([P, TB, W2]),
                                                       ALU.max, ALU.mult).then_inc(msg_ready, 1)
                        dve.wait_ge(flags_in[s], 16 * (j + 1))
                        dve.wait_ge(turned_ready, blk + 1)
                        if not first:
                            dve.wait_ge(res_ready, blk - 1)
                        if not (first and s == 0):
                            dve.wait_ge(scanned, blk)
                        nc.vector.tensor_tensor_scan(tot[:, s, :], flags[:, s, :], turned[:, s, :],
                                                     tot[:, 1 - s, TB * P - 1:TB * P], ALU.mult, ALU.add
                                                     ).then_inc(scanned, 1)
                        if not last:
                            places(j + 1, s)
                        if not first:
                            dve.wait_ge(sent[s], 16 * TB * j)
                        nc.vector.tensor_scalar(put[:, s, :], o.put[:, at], 1.0, None, ALU.mult
                                                ).then_inc(put_ready, 1)
                        dve.wait_ge(res_ready, blk + 1)
                        nc.vector.tensor_tensor(stage[:, s], res[:, s, :].rearrange("p (i f) -> p i f", f=W2),
                                                o.root[:, at].unsqueeze(2).broadcast_to([P, TB, W2]), ALU.mult
                                                ).then_inc(stage_ready, 1)
                turns(dve, body)


def node_rows(table, k, tail, lo=0, hi=None):
    hi = table.shape[1] if hi is None else hi
    if tail:
        return table[P * PER:N, lo:hi].rearrange("(p n) f -> p n f", n=1)
    return table[0:P * PER, lo:hi].rearrange("(p n) f -> p n f", p=P)[:, bass.ds(k * ITEMS, ITEMS), :]


def arrived(k, s):
    return 8 * (k - s) + 16


def chunks(eng, first_half, second_half):
    first_half(0, 0, False)
    for k in (1, 2):
        first_half(k, k % 2, False)
        second_half(k - 1, (k - 1) % 2, False)
    with eng.Fori(1, (CHUNKS - 1) // 2) as h:
        for k in (1, 2):
            first_half(2 * h + k, k % 2, False)
            second_half(2 * h + (k - 1), (k - 1) % 2, False)
    first_half(CHUNKS, CHUNKS % 2, True)
    second_half(CHUNKS - 1, (CHUNKS - 1) % 2, False)
    second_half(CHUNKS, CHUNKS % 2, True)


def dense_phase(b, g, name, x, msgs, out, extra=None, aux=(), root=False):
    nc = b.nc
    wx, wm, wo = x.shape[1], msgs.shape[1], out.shape[1]
    we = extra.shape[1] if extra is not None else 1
    with ExitStack() as c:
        xs = b.sb(name + "_x", [P, 2, ITEMS, wx], F32, c)
        ms = b.sb(name + "_m", [P, 2, ITEMS, wm], F32, c)
        es = b.sb(name + "_e", [P, 2, ITEMS, we], F32, c)
        pre = b.sb(name + "_pre", [P, 2, ITEMS, D], F32, c)
        cen = b.sb(name + "_cen", [P, 2, ITEMS, D], F32, c)
        sq = b.sb(name + "_sq", [P, 2, ITEMS, D], F32, c)
        row = b.sb(name + "_row", [P, 2, ITEMS, wo], F32, c)
        stat = b.sb(name + "_stat", [P, 6, 2, ITEMS], F32, c)
        total, neg, total2, var, dev, inv = (stat[:, k] for k in range(6))
        x_in = [b.sem(f"{name}_x_in{s}", c) for s in range(2)]
        m_in = [b.sem(f"{name}_m_in{s}", c) for s in range(2)]
        e_in = [b.sem(f"{name}_e_in{s}", c) for s in range(2)]
        pre_ready = b.sem(name + "_pre_ready", c)
        cen_ready = b.sem(name + "_cen_ready", c)
        sq_ready = b.sem(name + "_sq_ready", c)
        var_ready = b.sem(name + "_var_ready", c)
        dev_ready = b.sem(name + "_dev_ready", c)
        inv_ready = b.sem(name + "_inv_ready", c)
        aux_ready = b.sem(name + "_aux_ready", c)
        row_ready = b.sem(name + "_row_ready", c)
        chain_a = b.sem(name + "_chain_a", c)
        chain_b = b.sem(name + "_chain_b", c)
        stored = [b.sem(f"{name}_stored{s}", c) for s in range(2)]
        if root:
            xt = b.sb(name + "_xt", [D + 1, 2, ITEMS * P], F32, c)
            z = b.sb(name + "_z", [P, ITEMS, 2 * D], F32, c)
            act_z = b.sb(name + "_act_z", [P, ITEMS, 2 * D], F32, c)
            both = b.sb(name + "_both", [P, ITEMS, D], F32, c)
            xt_ps = b.ps(name + "_xt_ps", [D, 3 * 512], F32, c)
            root_ps = b.ps(name + "_root_ps", [P, 3 * 512], F32, c)
            xt_ps_ready = b.sem(name + "_xt_ps_ready", c)
            xt_ready = b.sem(name + "_xt_ready", c)
            root_ready = b.sem(name + "_root_ready", c)
            z_ready = b.sem(name + "_z_ready", c)
            act_ready = b.sem(name + "_act_ready", c)
            both_ready = b.sem(name + "_both_ready", c)
            ones_ready = b.sem(name + "_ones_ready", c)

        def sizes(tail):
            return (TAIL, 1) if tail else (P, ITEMS)

        with nc.Block() as block:
            @block.sync
            def _(sp):
                def load(k, s, tail):
                    p, n = sizes(tail)
                    if not isinstance(k, int) or k >= 2:
                        hold(sp, pre_ready, k - 1, g.sp_tick)
                        if aux:
                            hold(sp, aux_ready, k - 1, g.sp_tick)
                        if root:
                            hold(sp, xt_ps_ready, k - 1, g.sp_tick)
                            hold(sp, z_ready, k - 1, g.sp_tick)
                    sp.dma_start(xs[0:p, s, 0:n, :], node_rows(x, k, tail)).then_inc(x_in[s], 16)
                    sp.dma_start(ms[0:p, s, 0:n, :], node_rows(msgs, k, tail)).then_inc(m_in[s], 16)
                    if extra is not None:
                        sp.dma_start(es[0:p, s, 0:n, :], node_rows(extra, k, tail)).then_inc(e_in[s], 16)

                def store(k, s, tail):
                    p, n = sizes(tail)
                    hold(sp, row_ready, k + 1, g.sp_tick)
                    if aux:
                        hold(sp, aux_ready, k + 1, g.sp_tick)
                    sp.dma_start(node_rows(out, k, tail), row[0:p, s, 0:n, :]).then_inc(stored[s], 16)
                chunks(sp, load, store)
                for s in range(2):
                    hold(sp, stored[s], 16 * (CHUNKS + 1) // 2, g.sp_tick)

            @block.gpsimd
            def _(pool):
                def sums(k, s, tail):
                    p, n = sizes(tail)
                    hold(pool, x_in[s], arrived(k, s), g.pool_tick)
                    if root:
                        hold(pool, act_ready, k + 1, g.pool_tick)
                        nc.gpsimd.tensor_tensor(both[0:p, 0:n], act_z[0:p, 0:n, 0:D], act_z[0:p, 0:n, D:2 * D],
                                                ALU.add).then_inc(both_ready, 1)
                        hold(pool, both_ready, k + 1, g.pool_tick)
                        m = both[0:p, 0:n]
                    else:
                        hold(pool, m_in[s], arrived(k, s), g.pool_tick)
                        m = ms[0:p, s, 0:n, 0:D]
                    if not isinstance(k, int) or k >= 2:
                        hold(pool, cen_ready, k - 1, g.pool_tick)
                    nc.gpsimd.tensor_tensor(pre[0:p, s, 0:n], xs[0:p, s, 0:n, 0:D], m, ALU.add
                                            ).then_inc(pre_ready, 1)

                def rows(k, s, tail):
                    p, n = sizes(tail)
                    hold(pool, inv_ready, k + 1, g.pool_tick)
                    if not isinstance(k, int) or k >= 2:
                        hold(pool, stored[s], arrived(k, s) - 16, g.pool_tick)
                    nc.gpsimd.tensor_tensor(row[0:p, s, 0:n, 0:D], cen[0:p, s, 0:n],
                                            inv[0:p, s, 0:n].unsqueeze(2).broadcast_to([p, n, D]), ALU.mult
                                            ).then_inc(row_ready, 1)
                chunks(pool, sums, rows)

            @block.vector
            def _(dve):
                a, bb = Chain(dve, chain_a, 2), Chain(dve, chain_b, 1)
                if root:
                    nc.vector.memset(xt[D:D + 1, :, :], 1.0).then_inc(ones_ready, 1)

                def center(k, s, tail):
                    p, n = sizes(tail)
                    a.step(k)
                    if root:
                        dve.wait_ge(root_ready, k + 1)
                        dve.wait_ge(m_in[s], arrived(k, s))
                        if not (isinstance(k, int) and k == 0):
                            dve.wait_ge(act_ready, k)
                        nc.vector.tensor_tensor(z[0:p, 0:n], root_ps[0:p, 0:n * 2 * D]
                                                .rearrange("p (n f) -> p n f", f=2 * D), ms[0:p, s, 0:n], ALU.add
                                                ).then_inc(z_ready, 1)
                    dve.wait_ge(pre_ready, k + 1)
                    a.link(nc.vector.reduce_sum(total[0:p, s, 0:n], pre[0:p, s, 0:n], axis=AX))
                    a.link(nc.vector.tensor_scalar(neg[0:p, s, 0:n], total[0:p, s, 0:n], -1.0 / D, None, ALU.mult))
                    if not isinstance(k, int) or k >= 2:
                        dve.wait_ge(row_ready, k - 1)
                        dve.wait_ge(sq_ready, k - 1)
                    nc.vector.tensor_tensor(cen[0:p, s, 0:n], pre[0:p, s, 0:n],
                                            neg[0:p, s, 0:n].unsqueeze(2).broadcast_to([p, n, D]), ALU.add
                                            ).then_inc(cen_ready, 1)

                def scale(k, s, tail):
                    p, n = sizes(tail)
                    bb.step(k)
                    dve.wait_ge(sq_ready, k + 1)
                    bb.link(nc.vector.reduce_sum(total2[0:p, s, 0:n], sq[0:p, s, 0:n], axis=AX))
                    nc.vector.tensor_scalar(var[0:p, s, 0:n], total2[0:p, s, 0:n], 1.0 / D, EPS, ALU.mult, ALU.add
                                            ).then_inc(var_ready, 1)
                    dve.wait_ge(dev_ready, k + 1)
                    nc.vector.reciprocal(inv[0:p, s, 0:n], dev[0:p, s, 0:n]).then_inc(inv_ready, 1)
                chunks(dve, center, scale)

            @block.scalar
            def _(act):
                def square(k, s, tail):
                    p, n = sizes(tail)
                    if root:
                        act.wait_ge(xt_ps_ready, k + 1)
                        if not isinstance(k, int) or k >= 2:
                            act.wait_ge(root_ready, k - 1)
                        w = ITEMS * P if not tail else P
                        cols = w if not tail else TAIL
                        nc.scalar.activation(xt[0:D, s, 0:cols], xt_ps[:, 0:cols], ACT.Copy).then_inc(xt_ready, 1)
                        act.wait_ge(z_ready, k + 1)
                        if not (isinstance(k, int) and k == 0):
                            act.wait_ge(both_ready, k)
                        nc.scalar.activation(act_z[0:p, 0:n], z[0:p, 0:n], ACT.Relu, scale=0.5
                                             ).then_inc(act_ready, 1)
                    act.wait_ge(cen_ready, k + 1)
                    if not isinstance(k, int) or k >= 2:
                        act.wait_ge(inv_ready, k - 1)
                    nc.scalar.activation(sq[0:p, s, 0:n], cen[0:p, s, 0:n], ACT.Square).then_inc(sq_ready, 1)

                def deviation(k, s, tail):
                    p, n = sizes(tail)
                    act.wait_ge(var_ready, k + 1)
                    nc.scalar.activation(dev[0:p, s, 0:n], var[0:p, s, 0:n], ACT.Sqrt).then_inc(dev_ready, 1)
                    if aux:
                        if not isinstance(k, int) or k >= 2:
                            act.wait_ge(stored[s], arrived(k, s) - 16)
                        act.wait_ge(x_in[s], arrived(k, s))
                        act.wait_ge(m_in[s], arrived(k, s))
                        if extra is not None:
                            act.wait_ge(e_in[s], arrived(k, s))
                        for at, which, place, w in aux:
                            ins = nc.scalar.activation(row[0:p, s, 0:n, at:at + w],
                                                       {"x": xs, "m": ms, "e": es}[which][0:p, s, 0:n, place:place + w],
                                                       ACT.Copy)
                        ins.then_inc(aux_ready, 1)
                chunks(act, square, deviation)

            if root:
                @block.tensor
                def _(pe):
                    pe.wait_ge(ones_ready, 1)

                    def products(k, s, tail):
                        p, n = sizes(tail)
                        hold(pe, x_in[s], arrived(k, s), g.pe_tick)
                        if not (isinstance(k, int) and k == 0):
                            hold(pe, xt_ready, k, g.pe_tick)
                        for i in range(n):
                            ins = nc.tensor.transpose(xt_ps[:, i * p:(i + 1) * p], xs[0:p, s, i, 0:D],
                                                      g.ident[0:p, 0:p])
                        ins.then_inc(xt_ps_ready, 1)
                        hold(pe, xt_ready, k + 1, g.pe_tick)
                        if not (isinstance(k, int) and k == 0):
                            hold(pe, z_ready, k, g.pe_tick)
                        for i in range(n):
                            ins = nc.tensor.matmul(root_ps[0:p, i * 2 * D:(i + 1) * 2 * D],
                                                   xt[:, s, i * p:(i + 1) * p], g.root1[:, :], start=True, stop=True)
                        ins.then_inc(root_ready, 1)
                    chunks(pe, products, lambda k, s, tail: None)


class Globals:
    pass


class Order:

    def __init__(self, b, name):
        self.name = name
        self.put = b.sb(name + "_put_table", [P, NT], F32)
        self.get = b.sb(name + "_get_table", [P, NT], F32)
        self.w = b.sb(name + "_w_table", [P, NT], F32)
        self.root = b.sb(name + "_root_table", [P, NT], F32)
        self.flags = b.dram(name + "_flags_dram", [EP])


def fill_table(act, table, tile, done):
    with act.Fori(0, CHUNKS) as k:
        act.dma_start(node_rows(table, k, False), tile).then_inc(done, 16)
    act.dma_start(node_rows(table, CHUNKS, True), tile[0:TAIL, 0:1, :]).then_inc(done, 16)
    act.wait_ge(done, 16 * (CHUNKS + 1))


def build(nc, x, src, dst, attr, w, u, W1, b1, W2, b2, init, weight, root, bias, l2W, l2b, l3W, l3b, out):
    with ExitStack() as ctx:
        b = Build(nc, ctx)
        g = Globals()
        g.pool_tick = b.sem("pool_tick")
        g.pe_tick = b.sem("pe_tick")
        g.sp_tick = b.sem("sp_tick")
        g.ident = b.sb("ident", [P, P], F32)
        g.before = b.sb("before", [P, P], BF16)
        g.since = b.sb("since", [P, P], BF16)
        g.ones_b = b.sb("ones_b", [P, P], BF16)
        g.ones_f = b.sb("ones_f", [P, TB * P], F32)
        g.iota16 = b.sb("iota16", [P, NT], F16)
        g.pos = b.sb("pos", [P, NT], F32)
        g.src = b.sb("src_table", [P, NT], F32)
        g.dst = b.sb("dst_table", [P, NT], F32)
        g.w = b.sb("w_table", [P, NT], F32)
        g.lo = [b.sb(f"lo{k}", [P, NT], F32) for k in range(2)]
        g.hi = [b.sb(f"hi{k}", [P, NT], F32) for k in range(2)]
        g.first = [b.sb(f"first{k}", [P, HI], F32) for k in range(4)]
        g.w1 = b.sb("w1", [3 * A, HID], F32)
        g.w1u = b.sb("w1u", [1, HID], F32)
        g.uval = b.sb("uval", [1, 1], F32)
        g.w2 = b.sb("w2", [HID, D], F32)
        g.b1 = b.sb("b1", [HID, 1], F32)
        g.hb = b.sb("hb", [HID, 1], F32)
        g.b2 = b.sb("b2", [P, D], F32)
        g.conv0 = b.sb("conv0", [2 * D, 2 * D], F32)
        g.conv1 = b.sb("conv1", [2 * D, 2 * D], F32)
        g.conv_b = b.sb("conv_b", [P, 2 * D], F32)
        g.root1 = b.sb("root1", [D + 1, 2 * D], F32)
        g.l2w = b.sb("l2w", [D, D], F32)
        g.l2b = b.sb("l2b", [P, D], F32)
        g.l3w = b.sb("l3w", [D, D], F32)
        g.l3b = b.sb("l3b", [P, D], F32)
        g.base = b.sb("base", [1, D], F32)
        g.base_all = b.sb("base_all", [P, D], F32)
        g.fill_m = b.sb("fill_m", [P, ITEMS, D + 1], F32)
        g.fill_nd = b.sb("fill_nd", [P, ITEMS, 2], F32)
        g.fill_0 = b.sb("fill_0", [P, ITEMS * 2 * D], F32)
        g.fill_2 = b.sb("fill_2", [P, ITEMS, D], F32)
        g.fill_3 = b.sb("fill_3", [P, ITEMS, D], F32)
        order_d, order_s = Order(b, "D"), Order(b, "S")

        s_half = b.dram("s_half", [EP, SROW])
        s_rows = b.dram("s_rows", [EP, SROW])
        d_half = b.dram("d_half", [EP, DROW])
        d_rows = b.dram("d_rows", [EP, DROW])
        m0 = b.dram("m0", [N, D + 1])
        nd = b.dram("nd", [N, 2])
        x1 = b.dram("x1", [N, R1])
        x1_edges = b.dram("x1_edges", [EP, R1])
        sums1 = b.dram("sums1", [EP + 1, D])
        m1 = b.dram("m1", [N, 2 * D])
        x2 = b.dram("x2", [N, R2])
        m2 = b.dram("m2", [N, D])
        x3 = b.dram("x3", [N, R2])
        m3 = b.dram("m3", [N, D])

        setup_phase(b, g, src, dst, w, {
            "W1": W1, "u0": u[0:1, :], "W2": W2, "b1": b1, "b2": b2, "init": init, "weight": weight, "root": root,
            "bias0": bias[0:1], "bias1": bias[1:2], "l2W": l2W, "l2b": l2b, "l3W": l3W, "l3b": l3b})
        b.clear()
        hist_phase(b, g)
        b.clear()

        def fill_sums(act, done):
            fill_table(act, m0, g.fill_m[:, :, :], done)

        def fill_last(act, done):
            act.dma_start(sums1[EP:EP + 1, :], g.fill_0[0:1, 0:D]).then_inc(done, 16)
            act.dma_start(nd[P * PER:N, :], g.fill_nd[0:TAIL, 0, :]).then_inc(done, 16)
            with act.Fori(0, CHUNKS) as k:
                act.dma_start(node_rows(nd, k, False), g.fill_nd[:, :, :]).then_inc(done, 16)
            act.wait_ge(done, 16 * (CHUNKS + 2))

        def fill_m1(act, done):
            fill_table(act, m1, g.fill_0[:, :].rearrange("p (n f) -> p n f", f=2 * D), done)

        def fill_m23(act, done):
            fill_table(act, m2, g.fill_2[:, :, :], done)
            with act.Fori(0, CHUNKS) as k:
                act.dma_start(node_rows(m3, k, False), g.fill_3[:, :, :]).then_inc(done, 16)
            act.dma_start(node_rows(m3, CHUNKS, True), g.fill_3[0:TAIL, 0:1, :]).then_inc(done, 16)
            act.wait_ge(done, 32 * (CHUNKS + 1))

        radix_phase(b, g, "s1", attr, [(A, g.src), (A + 1, g.dst), (A + 2, g.w), (A + 3, g.hi[0])], SROW,
                    g.lo[0], LO, g.first[0], s_half, fill_sums)
        b.clear()
        radix_phase(b, g, "s2", s_half, [], SROW, None, HI, g.first[1], s_rows, fill_last)
        b.clear()
        radix_phase(b, g, "d1", None, [(0, g.src), (1, g.dst), (2, g.w), (3, g.hi[1])], DROW,
                    g.lo[1], LO, g.first[2], d_half, fill_m1)
        b.clear()
        radix_phase(b, g, "d2", d_half, [], DROW, None, HI, g.first[3], d_rows, fill_m23)
        b.clear()
        tables_phase(b, g, order_s, s_rows, A)
        b.clear()
        tables_phase(b, g, order_d, d_rows, 0)
        b.clear()
        degree_phase(b, g, order_d, nd)
        b.clear()
        edge_mlp_phase(b, g, order_s, s_rows, m0)
        b.clear()
        dense_phase(b, g, "l0", x, m0, x1, extra=nd, aux=((D, "e", 0, 2), (D + 2, "m", D, 1)))
        b.clear()
        message_phase(b, g, order_d, "p1", x1, R1, D, None, sums1, saved=x1_edges)
        b.clear()
        conv_phase(b, g, order_d, x1_edges, sums1, m1)
        b.clear()
        dense_phase(b, g, "l1", x1, m1, x2, aux=((D, "x", D + 2, 1),), root=True)
        b.clear()
        message_phase(b, g, order_s, "p3", x2, R2, None, g.l2w, m2, bias=g.l2b)
        b.clear()
        dense_phase(b, g, "l2", x2, m2, x3, aux=((D, "x", D, 1),))
        b.clear()
        message_phase(b, g, order_s, "p4", x3, R2, D, g.l3w, m3, bias=g.l3b, scale_out=True)
        b.clear()
        dense_phase(b, g, "l3", x3, m3, out)
        b.clear()


_INS = ["x", "src", "dst", "edge_attr_32", "edge_weight", "L0_gnn_u", "L0_gnn_W1", "L0_gnn_b1", "L0_gnn_W2",
        "L0_gnn_b2", "L1_gnn_init_weight", "L1_gnn_weight", "L1_gnn_root_weight", "L1_gnn_bias", "L2_gnn_W",
        "L2_gnn_b", "L3_gnn_weight", "L3_gnn_bias"]


def kernel(**inputs):
    import numpy as _np
    import concourse.bacc as _bacc
    from concourse import mybir as _mybir
    from concourse.bass_utils import run_bass_kernel_spmd as _run

    nc = _bacc.Bacc("TRN2", target_bir_lowering=False, num_devices=1)
    arrays, args = {}, []
    for name in _INS:
        a = _np.ascontiguousarray(inputs[name])
        arrays[f"in_{name}_dram"] = a
        args.append(nc.dram_tensor(f"in_{name}_dram", a.shape, _mybir.dt.from_np(a.dtype), kind="ExternalInput").ap())
    out = nc.dram_tensor("out_0_dram", (N, D), _mybir.dt.float32, kind="ExternalOutput").ap()
    build(nc, *args, out)
    r = _run(nc, [arrays], core_ids=[0])
    return r.results[0]["out_0_dram"]
```

```python
import concourse.bass as bass
from concourse import mybir
from contextlib import ExitStack

F32 = mybir.dt.float32
F16 = mybir.dt.float16
BF16 = mybir.dt.bfloat16
I32 = mybir.dt.int32
ALU = mybir.AluOpType
ACT = mybir.ActivationFunctionType
AX = mybir.AxisListType.X

P = 128
N = 100000
E = 50000
D = 64
A = 32
HID = 128
TB = 4
NB = -(-E // (P * TB))
NB += NB % 2
NT = NB * TB
EP = NT * P
TURNS = NB // 2
QT = NT // 4
LO = 256
HI = -(-N // LO)
PADKEY = HI * LO - 1
BIG = 1 << 20
ITEMS = 13
RING = 4
CHUNKS = N // P // ITEMS // RING * RING
PER = CHUNKS * ITEMS
TAIL = N - P * PER
TAIL_P = 32
TAIL_ITEMS = TAIL // TAIL_P
HUGE = 3.0e38
EPS = 1e-5
SROW = A + 4
DROW = 4
R1 = D + 3
R2 = D + 1
assert PADKEY >= N and TAIL_P * TAIL_ITEMS == TAIL and TAIL_ITEMS <= ITEMS and 16 % RING == 0


def turns(eng, body):
    body(0, True, False)
    with eng.Fori(1, TURNS - 1) as j:
        body(j, False, False)
    body(TURNS - 1, False, True)


def wait(eng, sem, value):
    if not (isinstance(value, int) and value <= 0):
        eng.wait_ge(sem, value)


def hold(eng, sem, value, tick):
    eng.wait_ge(sem, value)
    if not isinstance(value, int):
        eng.sem_inc(tick, 1)


class Chain:

    def __init__(self, eng, sem, per):
        self.eng, self.sem, self.per = eng, sem, per

    def step(self, k):
        self.base, self.n = k * self.per, 0

    def link(self, ins):
        ins.then_inc(self.sem, 1)
        self.n += 1
        self.eng.wait_ge(self.sem, self.base + self.n)

    def close(self):
        for _ in range(self.per - self.n):
            self.eng.sem_inc(self.sem, 1)
        self.n = self.per


class Build:
    def __init__(self, nc, ctx):
        self.nc, self.ctx, self.own = nc, ctx, []

    def sb(self, name, shape, dt, ctx=None):
        return (ctx or self.ctx).enter_context(self.nc.sbuf_tensor(name, shape, dt))

    def ps(self, name, shape, dt, ctx):
        return ctx.enter_context(self.nc.psum_tensor(name, shape, dt))

    def sem(self, name, ctx=None):
        sem = self.nc.alloc_semaphore(name)
        if ctx is not None:
            self.own.append(sem)
        return sem

    def clear(self):
        self.nc.clear_and_free_semaphores(self.own)
        self.own = []
        self.nc.all_engine_barrier()

    def dram(self, name, shape):
        return self.nc.dram_tensor(name, shape, F32, kind="Internal").ap()


def setup_phase(b, g, src, dst, w, weights):
    nc = b.nc
    with ExitStack() as c:
        rows_i = b.sb("rows_i", [QT, 2, 4, P], I32, c)
        rows_f = b.sb("rows_f", [QT, 3, 4, P], F32, c)
        next_i = b.sb("next_i", [QT, 4, P], I32, c)
        next_f = b.sb("next_f", [QT, 4, P], F32, c)
        falls = b.sb("falls", [QT, 4 * P], F32, c)
        fall = b.sb("fall", [QT, 1], F32, c)
        fall_all = b.sb("fall_all", [1, 1], F32, c)
        iota_i = b.sb("iota_i", [P, NT], I32, c)
        pos_i = b.sb("pos_i", [P, NT], I32, c)
        digit_i = b.sb("digit_i", [P, 2, NT], I32, c)
        digit_j = b.sb("digit_j", [P, 4, NT], I32, c)
        w2t = b.sb("w2t", [D, D], F32, c)
        hbase = b.sb("hbase", [P, 1], F32, c)
        tr = b.ps("setup_tr", [P, 3, 512], F32, c)
        small = b.ps("setup_small", [P, 4, 512], F32, c)
        fall_ps = b.ps("fall_ps", [P, 512], F32, c)
        fall_ready = b.sem("fall_ready", c)
        padded = b.sem("padded", c)
        loaded = b.sem("loaded", c)
        wloaded = b.sem("wloaded", c)
        made = b.sem("made", c)
        cast = b.sem("cast", c)
        columns = b.sem("columns", c)
        dv = b.sem("setup_dve", c)
        small_done = b.sem("small_done", c)
        rows_ready = b.sem("rows_ready", c)
        full = E // P
        rest = E - full * P
        with nc.Block() as block:
            @block.gpsimd
            def _(pool):
                for t, value in ((g.ident, 0.0), (g.before, 1.0), (g.since, 1.0)):
                    nc.gpsimd.memset(t[:, :], value).then_inc(made, 1)
                nc.gpsimd.iota(iota_i[:, :], [[1, NT]], base=0, channel_multiplier=0).then_inc(made, 1)
                nc.gpsimd.iota(pos_i[:, :], [[P, NT]], base=0, channel_multiplier=1).then_inc(made, 1)
                pool.wait_ge(made, 5)
                nc.gpsimd.affine_select(out=g.ident[:, :], in_=g.ident[:, :], compare_op=ALU.not_equal, fill=1.0,
                                        base=0, pattern=[[-1, P]], channel_multiplier=1).then_inc(made, 1)
                nc.gpsimd.affine_select(out=g.before[:, :], in_=g.before[:, :], compare_op=ALU.is_gt, fill=0.0,
                                        base=0, pattern=[[1, P]], channel_multiplier=-1).then_inc(made, 1)
                nc.gpsimd.affine_select(out=g.since[:, :], in_=g.since[:, :], compare_op=ALU.is_ge, fill=0.0,
                                        base=0, pattern=[[-1, P]], channel_multiplier=1).then_inc(made, 1)

            @block.sync
            def _(sp):
                hold(sp, padded, 6, g.sp_tick)
                for k, a in ((0, src), (1, dst), (2, w)):
                    to = rows_f[:, 2] if k == 2 else rows_i[:, k]
                    for q in range(4):
                        n = min(QT, full - q * QT)
                        sp.dma_start(to[0:n, q, :], a[q * QT * P:(q * QT + n) * P].rearrange("(t p) -> t p", p=P)
                                     ).then_inc(loaded, 16)
                    sp.dma_start(to[full - 3 * QT:full - 3 * QT + 1, 3, 0:rest],
                                 a[full * P:E].rearrange("(t p) -> t p", t=1)).then_inc(loaded, 16)
                for q in range(4):
                    n = min(QT, full - q * QT)
                    sp.dma_start(next_i[0:n, q, :], dst[q * QT * P + 1:(q * QT + n) * P + 1]
                                 .rearrange("(t p) -> t p", p=P)).then_inc(loaded, 16)
                sp.dma_start(next_i[full - 3 * QT:full - 3 * QT + 1, 3, 0:rest - 1],
                             dst[full * P + 1:E].rearrange("(t p) -> t p", t=1)).then_inc(loaded, 16)

            @block.scalar
            def _(act):
                act.wait_ge(padded, 6)
                W = weights
                loads = [(g.w1[:, :], W["W1"][0:3 * A, :]), (g.w2[:, :], W["W2"]),
                         (g.b1[:, :], W["b1"].rearrange("(p a) -> p a", a=1)),
                         (g.w1u[:, :], W["W1"][3 * A:3 * A + 1, :]), (g.uval[:, :], W["u0"]),
                         (g.b2[:, :], W["b2"].rearrange("(p a) -> p a", p=1).broadcast_to([P, D])),
                         (g.conv_b[:, :], W["bias0"].rearrange("p k o -> p (k o)").broadcast_to([P, 2 * D])),
                         (g.l2b[:, :], W["l2b"].rearrange("(p a) -> p a", p=1).broadcast_to([P, D])),
                         (g.l3b[:, :], W["l3b"].rearrange("(p a) -> p a", p=1).broadcast_to([P, D])),
                         (w2t[:, :], W["l2W"]), (g.l3w[:, :], W["l3W"]),
                         (g.root1_b[:, :], W["bias1"].rearrange("p k o -> p (k o)").broadcast_to([P, 2 * D]))]
                for k in range(2):
                    o = slice(k * D, k * D + D)
                    loads += [(g.conv0[0:D, o], W["init"][k]), (g.conv0[D:2 * D, o], W["root"][0, k]),
                              (g.root1[0:D, o], W["root"][1, k]),
                              (g.root1[D:2 * D, 2 * D + k * D:3 * D + k * D], W["root"][1, k]), (g.conv1[o, o], W["weight"][0, k])]
                for to, a in loads:
                    act.dma_start(to, a).then_inc(wloaded, 16)
                g.n_loads = len(loads)

            @block.vector
            def _(dve):
                ch = Chain(dve, dv, 0)
                ch.step(0)
                nc.vector.memset(rows_i[:, :, 3, :], PADKEY).then_inc(padded, 1)
                nc.vector.memset(next_i[:, 3, :], PADKEY).then_inc(padded, 1)
                nc.vector.memset(rows_f[:, 2, 3, :], 0.0).then_inc(padded, 1)
                nc.vector.memset(g.conv1[:, :], 0.0).then_inc(padded, 1)
                nc.vector.memset(g.root1[:, :], 0.0).then_inc(padded, 1)
                nc.vector.memset(g.ones_f[:, :], 1.0).then_inc(padded, 1)
                ch.link(nc.vector.memset(g.ones_b[:, :], 1.0))
                dve.wait_ge(made, 5)
                nc.vector.tensor_copy(g.iota16[:, :], iota_i[:, :])
                nc.vector.tensor_copy(g.pos[:, :], pos_i[:, :])
                dve.wait_ge(loaded, 16 * 20)
                for k in range(2):
                    nc.vector.tensor_copy(rows_f[:, k], rows_i[:, k]).then_inc(cast, 1)
                ch.link(nc.vector.tensor_copy(next_f[:, :, :], next_i[:, :, :]))
                dve.wait_ge(cast, 2)
                ch.link(nc.vector.tensor_tensor(falls[:, :].rearrange("t (q p) -> t q p", p=P), rows_f[:, 1],
                                                next_f[:, :, :], ALU.is_gt))
                nc.vector.reduce_max(fall[:, :], falls[:, :], axis=AX).then_inc(fall_ready, 1)
                dve.wait_ge(fall_ready, 2)
                ch.link(nc.vector.tensor_scalar(fall_all[:, :], fall_ps[0:1, 0:1], 1.0, None, ALU.min))
                ch.link(nc.vector.tensor_copy(g.unsorted[0:1, 0:1], fall_all[:, :]))
                for k, to in enumerate((g.src, g.dst, g.w)):
                    dve.wait_ge(columns, k + 1)
                    ch.link(nc.vector.tensor_copy(to[:, :], tr[:, k, 0:NT]))
                for k, key in enumerate((g.src, g.dst)):
                    ch.link(nc.vector.tensor_copy(digit_i[:, k], key[:, :]))
                    ch.link(nc.vector.tensor_scalar(digit_j[:, 2 * k], digit_i[:, k], LO - 1, None, ALU.bitwise_and))
                    ch.link(nc.vector.tensor_scalar(digit_j[:, 2 * k + 1], digit_i[:, k], 8, None,
                                                    ALU.logical_shift_right))
                    ch.link(nc.vector.tensor_copy(g.lo[k][:, :], digit_j[:, 2 * k]))
                    ch.link(nc.vector.tensor_copy(g.hi[k][:, :], digit_j[:, 2 * k + 1]))
                dve.wait_ge(small_done, 1)
                ch.link(nc.vector.tensor_tensor(g.hb[:, :], small[:, 0, 0:1], g.b1[:, :], ALU.add))
                nc.vector.tensor_scalar(hbase[:, :], g.hb[:, :], 0.0, None, ALU.max).then_inc(rows_ready, 1)
                dve.wait_ge(small_done, 2)
                ch.link(nc.vector.memset(g.fill_m[:, :, D:D + 1], 0.0))
                nc.vector.tensor_tensor(g.base[0:1, :], small[0:1, 1, 0:D], g.b2[0:1, :], ALU.add).then_inc(rows_ready, 1)
                dve.wait_ge(small_done, 3)
                ch.link(nc.vector.tensor_copy(g.base_all[:, :], small[:, 2, 0:D]))
                ch.link(nc.vector.tensor_copy(g.fill_m[:, :, 0:D],
                                              g.base_all[:, :].unsqueeze(1).broadcast_to([P, ITEMS, D])))
                ch.link(nc.vector.memset(g.zero_row[:, :], 0.0))
                ch.link(nc.vector.memset(g.fill_nd[:, :, 0:1], 0.0))
                ch.link(nc.vector.memset(g.fill_nd[:, :, 1:2], float(EP)))
                ch.link(nc.vector.tensor_copy(g.l2w[:, :], small[0:D, 3, 0:D]))
                for to, row in ((g.fill_1, g.root1_b), (g.fill_2, g.l2b), (g.fill_3, g.l3b)):
                    ch.link(nc.vector.tensor_copy(to[:, :, :], row[:, :].unsqueeze(1).broadcast_to(list(to.shape))))

            @block.tensor
            def _(pe):
                pe.wait_ge(made, 8)
                pe.wait_ge(loaded, 16 * 20)
                pe.wait_ge(cast, 2)
                pe.wait_ge(fall_ready, 1)
                nc.tensor.matmul(fall_ps[0:1, 0:1], fall[:, :], g.ones_f[0:QT, 0:1], start=True, stop=True
                                 ).then_inc(fall_ready, 1)
                for k in range(3):
                    for q in range(4):
                        last = nc.tensor.transpose(tr[:, k, q * QT:(q + 1) * QT], rows_f[:, k, q, :],
                                                   g.ident[0:QT, 0:QT])
                    last.then_inc(columns, 1)
                pe.wait_ge(wloaded, 16 * g.n_loads)
                nc.tensor.transpose(small[0:D, 3, 0:D], w2t[:, :], g.ident[0:D, 0:D])
                pe.wait_ge(padded, 6)
                nc.tensor.matmul(small[:, 0, 0:1], g.w1u[0:1, :], g.uval[0:1, :], start=True, stop=True
                                 ).then_inc(small_done, 1)
                pe.wait_ge(rows_ready, 1)
                nc.tensor.matmul(small[0:1, 1, 0:D], hbase[:, :], g.w2[:, :], start=True, stop=True
                                 ).then_inc(small_done, 1)
                pe.wait_ge(rows_ready, 2)
                nc.tensor.matmul(small[:, 2, 0:D], g.ones_f[0:1, 0:P], g.base[0:1, :], start=True, stop=True
                                 ).then_inc(small_done, 1)


def guarded(eng, body, flag, wanted):
    if flag is None:
        body()
    else:
        with eng.If(eng.value_load(flag) == wanted):
            body()


def hist_phase(b, g, name, digit, buckets, first_pos, flag=None):
    nc = b.nc
    with ExitStack() as c:
        hot = b.sb(name + "_hot", [P, 2, TB, buckets], BF16, c)
        counts = b.sb(name + "_counts", [P, buckets], F32, c)
        incl = b.sb(name + "_incl", [P, buckets], F32, c)
        acc = b.ps(name + "_acc", [P, 512], F32, c)
        hot_ready = b.sem(name + "_hot_ready", c)
        hot_used = b.sem(name + "_hot_used", c)
        chain = b.sem(name + "_chain", c)
        with nc.Block() as block:
            @block.vector
            def _(dve):
                def body(j, first, last):
                    for s in range(2):
                        if not first:
                            dve.wait_ge(hot_used, 2 * j + s - 1)
                        for i in range(TB):
                            ins = nc.vector.tensor_scalar(hot[:, s, i, :], g.iota16[:, 0:buckets],
                                                          digit[:, bass.ds((2 * j + s) * TB + i, 1)], None,
                                                          ALU.is_equal)
                        ins.then_inc(hot_ready, 1)

                def program():
                    turns(dve, body)
                    dve.wait_ge(hot_used, NB)
                    first_places(nc, dve, g, chain, acc, counts, incl, first_pos, buckets)
                guarded(dve, program, flag, 1)

            @block.tensor
            def _(pe):
                def body(j, first, last):
                    for s in range(2):
                        hold(pe, hot_ready, 2 * j + s + 1, g.pe_tick)
                        for i in range(TB):
                            ins = nc.tensor.matmul(acc[:, 0:buckets], g.ones_b[:, :], hot[:, s, i, :],
                                                   start=first and s == 0 and i == 0,
                                                   stop=last and s == 1 and i == TB - 1, skip_group_check=True)
                        ins.then_inc(hot_used, 1)
                guarded(pe, lambda: turns(pe, body), flag, 1)


def first_places(nc, dve, g, sem, acc, counts, incl, first_pos, buckets):
    ch = Chain(dve, sem, 0)
    ch.step(0)
    ch.link(nc.vector.tensor_copy(counts[:, 0:buckets], acc[:, 0:buckets]))
    ch.link(nc.vector.tensor_tensor_scan(incl[:, 0:buckets], g.ones_f[:, 0:buckets], counts[:, 0:buckets], 0.0,
                                         ALU.mult, ALU.add))
    ch.link(nc.vector.tensor_tensor(first_pos[:, 0:buckets], incl[:, 0:buckets], counts[:, 0:buckets],
                                    ALU.subtract))


def radix_phase(b, g, name, rows_in, loads_w, make, width, digit, buckets, first_pos, out, fill=None, then=None,
                flag=None):
    nc = b.nc
    parts = 7
    with ExitStack() as c:
        whole = b.sb(name + "_whole", [P, NT, max(loads_w, 1)], F32, c)
        rows = b.sb(name + "_rows", [P, 2, TB, width], F32, c)
        hot = b.sb(name + "_hot", [P, 2, TB, buckets], BF16, c)
        junk = b.sb(name + "_junk", [P, buckets], BF16, c)
        place_f = b.sb(name + "_place_f", [P, 2, TB], F32, c)
        place_i = b.sb(name + "_place_i", [P, 2, TB], I32, c)
        seen = b.ps(name + "_seen", [P, 512], F32, c)
        if then:
            hot2 = b.sb(name + "_hot2", [P, 2, TB, then[1]], BF16, c)
            counts = b.sb(name + "_counts", [P, then[1]], F32, c)
            incl = b.sb(name + "_incl", [P, then[1]], F32, c)
            acc = b.ps(name + "_acc", [P, 512], F32, c)
            hot2_ready = b.sem(name + "_hot2_ready", c)
            hot2_used = b.sem(name + "_hot2_used", c)
            chain = b.sem(name + "_chain", c)
        cleared = b.sem(name + "_cleared", c)
        loaded = b.sem(name + "_loaded", c)
        copied = b.sem(name + "_copied", c)
        made = b.sem(name + "_made", c)
        hot_ready = b.sem(name + "_hot_ready", c)
        seen_ready = b.sem(name + "_seen_ready", c)
        summed = b.sem(name + "_summed", c)
        place_ready = b.sem(name + "_place_ready", c)
        sent = [b.sem(f"{name}_sent{s}", c) for s in range(2)]
        filled = b.sem(name + "_filled", c)
        partial = rows_in is not None and rows_in.shape[0] < EP
        n_loads = parts + 1 if partial else parts
        with nc.Block() as block:
            @block.sync
            def _(sp):
                def program():
                    if partial:
                        sp.wait_ge(cleared, 1)
                    full = rows_in.shape[0] // P
                    step = NT // parts
                    for a in range(0, NT, step):
                        n = min(step, full - a)
                        sp.dma_start(whole[:, a:a + n, :], rows_in[a * P:(a + n) * P, 0:loads_w]
                                     .rearrange("(t p) c -> p t c", p=P)).then_inc(loaded, 16)
                    if partial:
                        sp.dma_start(whole[0:rows_in.shape[0] - full * P, full, :], rows_in[full * P:, 0:loads_w]
                                     ).then_inc(loaded, 16)
                if loads_w:
                    guarded(sp, program, flag, 1)
                if fill:
                    fill(sp, filled)

            @block.scalar
            def _(act):
                def body(j, first, last):
                    for s in range(2):
                        if not first:
                            act.wait_ge(sent[s], 16 * TB * j)
                        nc.scalar.activation(rows[:, s, :, 0:loads_w],
                                             whole[:, bass.ds((2 * j + s) * TB, TB), :], ACT.Copy
                                             ).then_inc(copied, 1)

                def program():
                    act.wait_ge(loaded, 16 * n_loads)
                    turns(act, body)
                if loads_w:
                    guarded(act, program, flag, 1)

            @block.gpsimd
            def _(pool):
                limit = pool.to_reg(EP - 1)

                def body(j, first, last):
                    for s in range(2):
                        hold(pool, place_ready, 2 * j + s + 1, g.pool_tick)
                        if loads_w:
                            hold(pool, copied, 2 * j + s + 1, g.pool_tick)
                        if make:
                            hold(pool, made, 2 * j + s + 1, g.pool_tick)
                        for i in range(TB):
                            nc.gpsimd.indirect_dma_start(
                                out[:, :], bass.IndirectOffsetOnAxis(ap=place_i[:, s, i:i + 1], axis=0),
                                rows[:, s, i, :], None, bounds_check=limit, oob_is_err=False
                            ).then_inc(sent[s], 16)

                def program():
                    turns(pool, body)
                    for s in range(2):
                        pool.wait_ge(sent[s], 16 * TB * TURNS)
                guarded(pool, program, flag, 1)

            @block.vector
            def _(dve):
                def one_hot(j, s, i):
                    t = (2 * j + s) * TB + i
                    col = digit[:, bass.ds(t, 1)] if digit is not None else whole[:, bass.ds(t, 1), width - 1]
                    nc.vector.tensor_scalar(hot[:, s, i, :], g.iota16[:, 0:buckets], col, None,
                                            ALU.is_equal).then_inc(hot_ready, 1)

                def body(j, first, last):
                    for s in range(2):
                        blk = 2 * j + s
                        if not first:
                            dve.wait_ge(sent[s], 16 * TB * j)
                        for k, (at, table) in enumerate(make):
                            ins = nc.vector.tensor_scalar(rows[:, s, :, at], table[:, bass.ds(blk * TB, TB)], 1.0,
                                                          None, ALU.mult)
                        if make:
                            ins.then_inc(made, 1)
                        if then and not first:
                            dve.wait_ge(hot2_used, blk - 1)
                        for i in range(TB):
                            dve.wait_ge(seen_ready, blk * TB + i + 1)
                            nc.vector.scalar_tensor_tensor(junk[:, :], seen[:, 0:buckets], 1.0, hot[:, s, i, :],
                                                           ALU.mult, ALU.mult, accum_out=place_f[:, s, i:i + 1]
                                                           ).then_inc(summed, 1)
                            if not (last and s == 1):
                                jn, sn = (j, 1) if s == 0 else (j + 1, 0)
                                one_hot(jn, sn, i)
                            if then:
                                ins = nc.vector.tensor_scalar(hot2[:, s, i, :], g.iota16[:, 0:then[1]],
                                                              then[0][:, bass.ds(blk * TB + i, 1)], None,
                                                              ALU.is_equal)
                        if then:
                            ins.then_inc(hot2_ready, 1)
                        dve.wait_ge(summed, (blk + 1) * TB)
                        nc.vector.tensor_scalar(place_i[:, s, :], place_f[:, s, :], 1.0, None, ALU.mult
                                                ).then_inc(place_ready, 1)

                def program():
                    if partial:
                        nc.vector.memset(whole[:, rows_in.shape[0] // P:NT, :], 0.0).then_inc(cleared, 1)
                    if digit is None:
                        dve.wait_ge(loaded, 16 * n_loads)
                    for i in range(TB):
                        one_hot(0, 0, i)
                    turns(dve, body)
                    if then:
                        dve.wait_ge(hot2_used, NB)
                        first_places(nc, dve, g, chain, acc, counts, incl, then[2], then[1])
                guarded(dve, program, flag, 1)

            @block.tensor
            def _(pe):
                def body(j, first, last):
                    for s in range(2):
                        for i in range(TB):
                            t = (2 * j + s) * TB + i
                            pe.wait_ge(hot_ready, t + 1)
                            nc.tensor.matmul(seen[:, 0:buckets], g.before[:, :], hot[:, s, i, :], start=False,
                                             stop=False, skip_group_check=True).then_inc(seen_ready, 1)
                            pe.wait_ge(summed, t + 1)
                            nc.tensor.matmul(seen[:, 0:buckets], g.since[:, :], hot[:, s, i, :], start=False,
                                             stop=last and s == 1 and i == TB - 1, skip_group_check=True)
                        if then:
                            hold(pe, hot2_ready, 2 * j + s + 1, g.pe_tick)
                            for i in range(TB):
                                ins = nc.tensor.matmul(acc[:, 0:then[1]], g.ones_b[:, :], hot2[:, s, i, :],
                                                       start=first and s == 0 and i == 0,
                                                       stop=last and s == 1 and i == TB - 1, skip_group_check=True)
                            ins.then_inc(hot2_used, 1)

                def program():
                    nc.tensor.matmul(seen[:, 0:buckets], g.ident[:, :], first_pos[:, 0:buckets], start=True,
                                     stop=False, skip_group_check=True)
                    turns(pe, body)
                guarded(pe, program, flag, 1)


def keep_phase(b, g, out):
    nc = b.nc
    with ExitStack() as c:
        rows = b.sb("keep_rows", [P, NT, DROW], F32, c)
        made = b.sem("keep_made", c)
        stored = b.sem("keep_stored", c)
        with nc.Block() as block:
            @block.vector
            def _(dve):
                def program():
                    for k, table in enumerate((g.src, g.dst, g.w, g.hi[1])):
                        nc.vector.tensor_copy(rows[:, :, k], table[:, :]).then_inc(made, 1)
                guarded(dve, program, g.unsorted[0:1, 0:1], 0)

            @block.sync
            def _(sp):
                def program():
                    sp.wait_ge(made, 4)
                    for q in range(4):
                        sp.dma_start(out[q * QT * P:(q + 1) * QT * P, :].rearrange("(t p) c -> p t c", p=P),
                                     rows[:, q * QT:(q + 1) * QT, :]).then_inc(stored, 16)
                    sp.wait_ge(stored, 16 * 4)
                guarded(sp, program, g.unsorted[0:1, 0:1], 0)


def tables_phase(b, g, o, rows, cols):
    nc = b.nc
    key_at = 0 if o.name == "S" else 1
    with ExitStack() as c:
        cur = b.sb(o.name + "_cur", [P, NT, 4], F32, c)
        nxt = b.sb(o.name + "_nxt", [P, NT, 4], F32, c)
        same = b.sb(o.name + "_same", [P, NT], F32, c)
        flag_rows = b.sb(o.name + "_flag_rows", [QT, 4, P], F32, c)
        zero = b.sb(o.name + "_zero", [1, 1], F32, c)
        tr = b.ps(o.name + "_flag_tr", [QT, 4, P], F32, c)
        cleared = b.sem(o.name + "_cleared", c)
        loaded = b.sem(o.name + "_loaded", c)
        ch_sem = b.sem(o.name + "_chain", c)
        same_ready = b.sem(o.name + "_same_ready", c)
        turned = b.sem(o.name + "_turned", c)
        rows_ready = b.sem(o.name + "_rows_ready", c)
        stored = b.sem(o.name + "_stored", c)
        n_loads = 9
        with nc.Block() as block:
            @block.sync
            def _(sp):
                hold(sp, cleared, 1, g.sp_tick)
                for q in range(4):
                    a = q * QT
                    r = rows[a * P:(a + QT) * P, cols:cols + 4].rearrange("(t p) c -> p t c", p=P)
                    sp.dma_start(cur[:, a:a + QT, :], r).then_inc(loaded, 16)
                    k = QT if q < 3 else QT - 1
                    r = rows[a * P + 1:(a + k) * P + 1, cols:cols + 4].rearrange("(t p) c -> p t c", p=P)
                    sp.dma_start(nxt[:, a:a + k, :], r).then_inc(loaded, 16)
                sp.dma_start(nxt[0:P - 1, NT - 1, :], rows[EP - P + 1:EP, cols:cols + 4]).then_inc(loaded, 16)
                hold(sp, rows_ready, 1, g.sp_tick)
                for q in range(4):
                    k = QT if q < 3 else QT - 1
                    sp.dma_start(o.flags[q * QT * P + 1:(q * QT + k) * P + 1].rearrange("(t p) -> t p", p=P),
                                 flag_rows[0:k, q, :]).then_inc(stored, 16)
                sp.dma_start(o.flags[EP - P + 1:EP].rearrange("(t p) -> t p", t=1),
                             flag_rows[QT - 1:QT, 3, 0:P - 1]).then_inc(stored, 16)
                sp.dma_start(o.flags[0:1].rearrange("(t p) -> t p", t=1), zero[:, :]).then_inc(stored, 16)
                hold(sp, stored, 16 * 6, g.sp_tick)

            @block.vector
            def _(dve):
                ch = Chain(dve, ch_sem, 0)
                ch.step(0)
                nc.vector.memset(zero[:, :], 0.0)
                nc.vector.memset(nxt[:, NT - 1, :], -1.0).then_inc(cleared, 1)
                dve.wait_ge(loaded, 16 * n_loads)
                nc.vector.tensor_tensor(same[:, :], cur[:, :, key_at], nxt[:, :, key_at], ALU.is_equal
                                        ).then_inc(same_ready, 1)
                dve.wait_ge(same_ready, 1)
                ch.link(nc.vector.scalar_tensor_tensor(o.put[:, :], same[:, :], float(BIG), cur[:, :, key_at],
                                                       ALU.mult, ALU.add))
                ch.link(nc.vector.tensor_scalar(o.get[:, :], cur[:, :, 1 - key_at], float(N - 1), None, ALU.min))
                ch.link(nc.vector.tensor_copy(o.w[:, :], cur[:, :, 2]))
                dve.wait_ge(turned, 1)
                nc.vector.tensor_copy(flag_rows[:, :, :], tr[:, :, :]).then_inc(rows_ready, 1)

            @block.tensor
            def _(pe):
                pe.wait_ge(same_ready, 1)
                for q in range(4):
                    last = nc.tensor.transpose(tr[:, q, :], same[:, q * QT:(q + 1) * QT], g.ident[:, :])
                last.then_inc(turned, 1)


def load_flags(sp, g, o, ring, ready, used, j, s):
    if used is not None:
        hold(sp, used, 2 * j + s - 1, g.sp_tick)
    blk = 2 * j + s
    np_ = ring.shape[0]
    sp.dma_start(ring[:, s, :], o.flags[bass.ds(blk * (TB * P), TB * P)].rearrange("(a n) -> a n", a=1)
                 .broadcast_to([np_, TB * P])).then_inc(ready[s], 16)


def degree_phase(b, g, o, table):
    nc = b.nc
    with ExitStack() as c:
        flags = b.sb("deg_flags", [1, 2, TB * P], F32, c)
        deg = b.sb("deg_deg", [1, 2, TB * P], F32, c)
        low = b.sb("deg_low", [P, TB], F32, c)
        root = b.sb("deg_root", [P, 2, TB], F32, c)
        inv = b.sb("deg_inv", [P, TB], F32, c)
        some = b.sb("deg_some", [P, TB], F32, c)
        wring = b.sb("deg_wring", [P, 2, TB], F32, c)
        put = b.sb("deg_put", [P, 2, TB], I32, c)
        stage = b.sb("deg_stage", [P, 2, TB, 2], F32, c)
        wrow = b.ps("deg_wrow", [1, 2, TB * P], F32, c)
        col = b.ps("deg_col", [P, 2, 512], F32, c)
        flags_in = [b.sem(f"deg_flags_in{s}", c) for s in range(2)]
        wrow_ready = b.sem("deg_wrow_ready", c)
        scanned = b.sem("deg_scanned", c)
        col_ready = b.sem("deg_col_ready", c)
        low_ready = b.sem("deg_low_ready", c)
        root_ready = b.sem("deg_root_ready", c)
        chain = b.sem("deg_chain", c)
        stage_ready = b.sem("deg_stage_ready", c)
        sent = [b.sem(f"deg_sent{s}", c) for s in range(2)]
        zeroed = b.sem("deg_zeroed", c)
        wring_ready = b.sem("deg_wring_ready", c)
        with nc.Block() as block:
            @block.sync
            def _(sp):
                def body(j, first, last):
                    for s in range(2):
                        load_flags(sp, g, o, flags, flags_in, None if first else scanned, j, s)
                turns(sp, body)

            @block.tensor
            def _(pe):
                def body(j, first, last):
                    for s in range(2):
                        blk = 2 * j + s
                        pe.wait_ge(wring_ready, blk + 1)
                        if not first:
                            pe.wait_ge(scanned, blk - 1)
                        for i in range(TB):
                            ins = nc.tensor.matmul(wrow[0:1, s, i * P:(i + 1) * P], wring[:, s, i:i + 1],
                                                   g.ident[:, :], start=True, stop=True)
                        ins.then_inc(wrow_ready, 1)
                        pe.wait_ge(scanned, blk + 1)
                        if not first:
                            pe.wait_ge(stage_ready, blk - 1)
                        for i in range(TB):
                            ins = nc.tensor.matmul(col[:, s, i:i + 1], deg[0:1, s, i * P:(i + 1) * P],
                                                   g.ones_f[0:1, 0:1], start=True, stop=True)
                        ins.then_inc(col_ready, 1)
                turns(pe, body)

            @block.scalar
            def _(act):
                def body(j, first, last):
                    for s in range(2):
                        act.wait_ge(low_ready, 2 * j + s + 1)
                        nc.scalar.activation(root[:, s, :], low[:, :], ACT.Sqrt).then_inc(root_ready, 1)
                turns(act, body)

            @block.vector
            def _(dve):
                ch = Chain(dve, chain, 2)
                nc.vector.memset(deg[:, 1, :], 0.0).then_inc(zeroed, 1)
                dve.wait_ge(zeroed, 1)

                def body(j, first, last):
                    for s in range(2):
                        blk = 2 * j + s
                        ch.step(blk)
                        if not first:
                            dve.wait_ge(col_ready, blk - 1)
                            dve.wait_ge(sent[s], 16 * TB * j)
                        nc.vector.tensor_scalar(wring[:, s, :], o.w[:, bass.ds(blk * TB, TB)], 1.0, None, ALU.mult
                                                ).then_inc(wring_ready, 1)
                        nc.vector.tensor_scalar(put[:, s, :], o.put[:, bass.ds(blk * TB, TB)], 1.0, None, ALU.mult)
                        nc.vector.tensor_scalar(stage[:, s, :, 1], g.pos[:, bass.ds(blk * TB, TB)], 1.0, None,
                                                ALU.mult)
                        dve.wait_ge(flags_in[s], 16 * (j + 1))
                        dve.wait_ge(wrow_ready, blk + 1)
                        dve.wait_ge(scanned, blk) if not first or s else None
                        nc.vector.tensor_tensor_scan(deg[:, s, :], flags[:, s, :], wrow[:, s, :],
                                                     deg[:, 1 - s, TB * P - 1:TB * P], ALU.mult, ALU.add
                                                     ).then_inc(scanned, 1)
                        dve.wait_ge(col_ready, blk + 1)
                        nc.vector.tensor_scalar(low[:, :], col[:, s, 0:TB], 1e-12, None, ALU.max
                                                ).then_inc(low_ready, 1)
                        nc.vector.tensor_scalar(some[:, :], col[:, s, 0:TB], 0.0, None, ALU.is_gt)
                        dve.wait_ge(root_ready, blk + 1)
                        ch.link(nc.vector.reciprocal(inv[:, :], root[:, s, :]))
                        nc.vector.tensor_tensor(o.root[:, bass.ds(blk * TB, TB)], inv[:, :], some[:, :], ALU.mult)
                        nc.vector.tensor_tensor(stage[:, s, :, 0], inv[:, :], some[:, :], ALU.mult
                                                ).then_inc(stage_ready, 1)
                        dve.wait_ge(stage_ready, blk + 1)
                        ch.close()
                turns(dve, body)

            @block.gpsimd
            def _(pool):
                limit = pool.to_reg(N - 1)

                def body(j, first, last):
                    for s in range(2):
                        hold(pool, stage_ready, 2 * j + s + 1, g.pool_tick)
                        for i in range(TB):
                            nc.gpsimd.indirect_dma_start(
                                table[:, :], bass.IndirectOffsetOnAxis(ap=put[:, s, i:i + 1], axis=0),
                                stage[:, s, i, :], None, bounds_check=limit, oob_is_err=False
                            ).then_inc(sent[s], 16)
                turns(pool, body)
                for s in range(2):
                    pool.wait_ge(sent[s], 16 * TB * TURNS)


def edge_mlp_phase(b, g, o, rows, table):
    nc = b.nc
    with ExitStack() as c:
        attr = b.sb("mlp_attr", [P, 2, TB, A], F32, c)
        flags = b.sb("mlp_flags", [A, 2, TB * P], F32, c)
        cut = b.sb("mlp_cut", [A, TB * P], F32, c)
        cat = b.sb("mlp_cat", [3 * A, 2, TB * P], F32, c)
        most = b.sb("mlp_most", [A, 2, TB * P], F32, c)
        cnt = b.sb("mlp_cnt", [A, 2, TB * P], F32, c)
        rcnt = b.sb("mlp_rcnt", [A, TB * P], F32, c)
        hid = b.sb("mlp_hid", [P, TB * P], F32, c)
        stage = b.sb("mlp_stage", [P, 2, TB, D + 1], F32, c)
        root = b.sb("mlp_root", [P, TB], F32, c)
        put = b.sb("mlp_put", [P, 2, TB], I32, c)
        turned = b.ps("mlp_turned", [A, 2, TB * P], F32, c)
        hidden = b.ps("mlp_hidden", [P, 2, 512], F32, c)
        res = b.ps("mlp_res", [P, 2, 512], F32, c)
        cnt_col = b.ps("mlp_cnt_col", [P, 2, 512], F32, c)
        flags_in = [b.sem(f"mlp_flags_in{s}", c) for s in range(2)]
        attr_in = [b.sem(f"mlp_attr_in{s}", c) for s in range(2)]
        turned_ready = b.sem("mlp_turned_ready", c)
        chain = b.sem("mlp_chain", c)
        cat_ready = b.sem("mlp_cat_ready", c)
        hidden_ready = b.sem("mlp_hidden_ready", c)
        hid_ready = b.sem("mlp_hid_ready", c)
        res_ready = b.sem("mlp_res_ready", c)
        root_ready = b.sem("mlp_root_ready", c)
        stage_ready = b.sem("mlp_stage_ready", c)
        put_ready = b.sem("mlp_put_ready", c)
        zeroed = b.sem("mlp_zeroed", c)
        sent = [b.sem(f"mlp_sent{s}", c) for s in range(2)]
        with nc.Block() as block:
            @block.sync
            def _(sp):
                def body(j, first, last):
                    for s in range(2):
                        if not first:
                            hold(sp, turned_ready, 2 * j + s - 1, g.sp_tick)
                        sp.dma_start(attr[:, s, :, :], rows[bass.ds((2 * j + s) * (TB * P), TB * P), 0:A]
                                     .rearrange("(i p) c -> p i c", p=P)).then_inc(attr_in[s], 16)
                        load_flags(sp, g, o, flags, flags_in, None if first else cat_ready, j, s)
                turns(sp, body)

            @block.tensor
            def _(pe):
                def body(j, first, last):
                    for s in range(2):
                        blk = 2 * j + s
                        hold(pe, attr_in[s], 16 * (j + 1), g.pe_tick)
                        if not first:
                            hold(pe, cat_ready, blk - 1, g.pe_tick)
                        for i in range(TB):
                            ins = nc.tensor.transpose(turned[:, s, i * P:(i + 1) * P], attr[:, s, i, :],
                                                      g.ident[:, :])
                        ins.then_inc(turned_ready, 1)
                        hold(pe, cat_ready, blk + 1, g.pe_tick)
                        if not first:
                            hold(pe, hid_ready, blk - 1, g.pe_tick)
                        nc.tensor.matmul(hidden[:, s, :], g.w1[:, :], cat[:, s, :], start=True, stop=True
                                         ).then_inc(hidden_ready, 1)
                        hold(pe, hid_ready, blk + 1, g.pe_tick)
                        if not first:
                            hold(pe, stage_ready, blk - 1, g.pe_tick)
                        for i in range(TB):
                            nc.tensor.matmul(res[:, s, i * D:(i + 1) * D], hid[:, i * P:(i + 1) * P], g.w2[:, :],
                                             start=True, stop=True)
                            ins = nc.tensor.matmul(cnt_col[:, s, i:i + 1],
                                                   cnt[0:1, s, i * P:(i + 1) * P], g.ones_f[0:1, 0:1],
                                                   start=True, stop=True)
                        ins.then_inc(res_ready, 1)
                turns(pe, body)

            @block.scalar
            def _(act):
                def body(j, first, last):
                    for s in range(2):
                        blk = 2 * j + s
                        act.wait_ge(hidden_ready, blk + 1)
                        if not (first and s == 0):
                            act.wait_ge(res_ready, blk)
                        nc.scalar.activation(hid[:, :], hidden[:, s, :], ACT.Relu, bias=g.hb[:, 0:1]
                                             ).then_inc(hid_ready, 1)
                        act.wait_ge(res_ready, blk + 1)
                        if not (first and s == 0):
                            act.wait_ge(stage_ready, blk)
                        nc.scalar.activation(root[:, :], cnt_col[:, s, 0:TB], ACT.Sqrt
                                             ).then_inc(root_ready, 1)
                turns(act, body)

            @block.vector
            def _(dve):
                ch = Chain(dve, chain, 5)
                end = slice(TB * P - 1, TB * P)
                for t in (cat, most, cnt):
                    nc.vector.memset(t[:, 1, :], 0.0).then_inc(zeroed, 1)
                dve.wait_ge(zeroed, 3)

                def finish(j, s, first):
                    blk = 2 * j + s
                    dve.wait_ge(res_ready, blk + 1)
                    if not first:
                        dve.wait_ge(sent[s], 16 * TB * j)
                    nc.vector.tensor_scalar(put[:, s, :], o.put[:, bass.ds(blk * TB, TB)], 1.0, None, ALU.mult
                                            ).then_inc(put_ready, 1)
                    nc.vector.tensor_tensor(stage[:, s, :, 0:D],
                                            res[:, s, 0:TB * D].rearrange("p (i f) -> p i f", f=D),
                                            g.b2[:, :].unsqueeze(1).broadcast_to([P, TB, D]), ALU.add)
                    dve.wait_ge(root_ready, blk + 1)
                    nc.vector.reciprocal(o.root[:, bass.ds(blk * TB, TB)], root[:, :])
                    nc.vector.reciprocal(stage[:, s, :, D], root[:, :]).then_inc(stage_ready, 1)

                def body(j, first, last):
                    for s in range(2):
                        blk = 2 * j + s
                        ch.step(blk)
                        dve.wait_ge(flags_in[s], 16 * (j + 1))
                        dve.wait_ge(turned_ready, blk + 1)
                        if not first:
                            dve.wait_ge(res_ready, blk - 1)
                        ch.link(nc.vector.tensor_scalar(cut[:, :], flags[:, s, :], 1.0, HUGE, ALU.subtract,
                                                        ALU.mult))
                        ch.link(nc.vector.tensor_tensor_scan(cnt[:, s, :], flags[:, s, :], g.ones_f[0:A, :],
                                                             cnt[:, 1 - s, end], ALU.mult, ALU.add))
                        nc.vector.tensor_tensor_scan(cat[0:A, s, :], flags[:, s, :], turned[:, s, :],
                                                     cat[0:A, 1 - s, end], ALU.mult, ALU.add)
                        ch.link(nc.vector.tensor_tensor_scan(most[:, s, :], cut[:, :], turned[:, s, :],
                                                             most[:, 1 - s, end], ALU.add, ALU.max))
                        ch.link(nc.vector.reciprocal(rcnt[:, :], cnt[:, s, :]))
                        nc.vector.tensor_copy(cat[A:2 * A, s, :], most[:, s, :])
                        ch.link(nc.vector.tensor_tensor(cat[2 * A:3 * A, s, :], cat[0:A, s, :], rcnt[:, :], ALU.mult))
                        dve.sem_inc(cat_ready, 1)
                        finish(j, s, first)
                turns(dve, body)

            @block.gpsimd
            def _(pool):
                limit = pool.to_reg(N - 1)

                def body(j, first, last):
                    for s in range(2):
                        hold(pool, stage_ready, 2 * j + s + 1, g.pool_tick)
                        for i in range(TB):
                            nc.gpsimd.indirect_dma_start(
                                table[:, :], bass.IndirectOffsetOnAxis(ap=put[:, s, i:i + 1], axis=0),
                                stage[:, s, i, :], None, bounds_check=limit, oob_is_err=False
                            ).then_inc(sent[s], 16)
                turns(pool, body)
                for s in range(2):
                    pool.wait_ge(sent[s], 16 * TB * TURNS)


def message_phase(b, g, o, name, table, width, factor_at, weight, out, bias=None, scale_out=False, saved=None):
    nc = b.nc
    with ExitStack() as c:
        got = b.sb(name + "_got", [P, 2, TB, width], F32, c)
        msg = b.sb(name + "_msg", [P, 2, TB, D], F32, c)
        fac = b.sb(name + "_fac", [P, 2, TB], F32, c)
        get = b.sb(name + "_get", [P, 2, TB], I32, c)
        put = b.sb(name + "_put", [P, 2, TB], I32, c)
        flags = b.sb(name + "_flags", [D, 2, TB * P], F32, c)
        tot = b.sb(name + "_tot", [D, 2, TB * P], F32, c)
        stage = b.sb(name + "_stage", [P, 2, TB, D], F32, c)
        scaled = b.sb(name + "_scaled", [P, TB, D], F32, c)
        turned = b.ps(name + "_turned", [D, 2, TB * P], F32, c)
        res = b.ps(name + "_res", [P, 2, 512], F32, c)
        flags_in = [b.sem(f"{name}_flags_in{s}", c) for s in range(2)]
        got_in = [b.sem(f"{name}_got_in{s}", c) for s in range(2)]
        sent = [b.sem(f"{name}_sent{s}", c) for s in range(2)]
        kept = [b.sem(f"{name}_kept{s}", c) for s in range(2)]
        get_ready = b.sem(name + "_get_ready", c)
        put_ready = b.sem(name + "_put_ready", c)
        fac_ready = b.sem(name + "_fac_ready", c)
        msg_ready = b.sem(name + "_msg_ready", c)
        turned_ready = b.sem(name + "_turned_ready", c)
        scanned = b.sem(name + "_scanned", c)
        res_ready = b.sem(name + "_res_ready", c)
        scaled_ready = b.sem(name + "_scaled_ready", c)
        stage_ready = b.sem(name + "_stage_ready", c)
        zeroed = b.sem(name + "_zeroed", c)
        store = saved is not None
        slot_sent = 16 if store else 16 * TB
        with nc.Block() as block:
            @block.gpsimd
            def _(pool):
                limit = pool.to_reg(N - 1)

                def gather(blk, turn, s):
                    hold(pool, get_ready, blk + 1, g.pool_tick)
                    if not isinstance(blk, int) or blk >= 2:
                        hold(pool, msg_ready, blk - 1, g.pool_tick)
                        if store:
                            hold(pool, kept[s], 16 * turn, g.pool_tick)
                    for i in range(TB):
                        nc.gpsimd.indirect_dma_start(
                            got[:, s, i, :], None, table[:, :],
                            bass.IndirectOffsetOnAxis(ap=get[:, s, i:i + 1], axis=0),
                            bounds_check=limit, oob_is_err=False).then_inc(got_in[s], 16)

                for s in range(2):
                    gather(s, 0, s)

                def body(j, first, last):
                    for s in range(2):
                        if not last:
                            gather(2 * j + 2 + s, j + 1, s)
                        if not store:
                            hold(pool, stage_ready, 2 * j + s + 1, g.pool_tick)
                            hold(pool, put_ready, 2 * j + s + 1, g.pool_tick)
                            for i in range(TB):
                                nc.gpsimd.indirect_dma_start(
                                    out[:, :], bass.IndirectOffsetOnAxis(ap=put[:, s, i:i + 1], axis=0),
                                    stage[:, s, i, :], None, bounds_check=limit, oob_is_err=False
                                ).then_inc(sent[s], 16)
                turns(pool, body)
                for s in range(2):
                    pool.wait_ge(got_in[s], 16 * TB * TURNS)
                    if not store:
                        pool.wait_ge(sent[s], slot_sent * TURNS)

            @block.sync
            def _(sp):
                def body(j, first, last):
                    for s in range(2):
                        load_flags(sp, g, o, flags, flags_in, None if first else scanned, j, s)
                turns(sp, body)

            @block.scalar
            def _(act):
                if not store:
                    return

                def body(j, first, last):
                    for s in range(2):
                        at = bass.ds((2 * j + s) * (TB * P), TB * P)
                        act.wait_ge(got_in[s], 16 * TB * (j + 1))
                        act.dma_start(saved[at, :].rearrange("(i p) c -> p i c", p=P), got[:, s]
                                      ).then_inc(kept[s], 16)
                        act.wait_ge(stage_ready, 2 * j + s + 1)
                        act.dma_start(out[at, :].rearrange("(i p) c -> p i c", p=P), stage[:, s]
                                      ).then_inc(sent[s], 16)
                turns(act, body)
                for s in range(2):
                    act.wait_ge(kept[s], 16 * TURNS)
                    act.wait_ge(sent[s], 16 * TURNS)

            @block.tensor
            def _(pe):
                def body(j, first, last):
                    for s in range(2):
                        blk = 2 * j + s
                        hold(pe, msg_ready, blk + 1, g.pe_tick)
                        if not first:
                            hold(pe, scanned, blk - 1, g.pe_tick)
                        for i in range(TB):
                            ins = nc.tensor.transpose(turned[:, s, i * P:(i + 1) * P], msg[:, s, i, :],
                                                      g.ident[:, :])
                        ins.then_inc(turned_ready, 1)
                        hold(pe, scanned, blk + 1, g.pe_tick)
                        if not first:
                            hold(pe, stage_ready, blk - 1, g.pe_tick)
                        for i in range(TB):
                            if weight is None:
                                ins = nc.tensor.transpose(res[:, s, i * D:(i + 1) * D], tot[:, s, i * P:(i + 1) * P],
                                                          g.ident[0:D, 0:D])
                            else:
                                ins = nc.tensor.matmul(res[:, s, i * D:(i + 1) * D], tot[:, s, i * P:(i + 1) * P],
                                                       weight[:, :], start=True, stop=True)
                        ins.then_inc(res_ready, 1)
                turns(pe, body)

            @block.vector
            def _(dve):
                def places(blk, s):
                    nc.vector.tensor_scalar(get[:, s, :], o.get[:, bass.ds(blk * TB, TB)], 1.0, None, ALU.mult
                                            ).then_inc(get_ready, 1)
                nc.vector.memset(tot[:, 1, :], 0.0).then_inc(zeroed, 1)
                for s in range(2):
                    places(s, s)
                dve.wait_ge(zeroed, 1)

                def body(j, first, last):
                    for s in range(2):
                        blk = 2 * j + s
                        at = bass.ds(blk * TB, TB)
                        dve.wait_ge(got_in[s], 16 * TB * (j + 1))
                        if not last:
                            places(blk + 2, s)
                        if not first:
                            dve.wait_ge(turned_ready, blk - 1)
                        if factor_at is None:
                            nc.vector.tensor_scalar(fac[:, s, :], o.w[:, at], 1.0, None, ALU.mult
                                                    ).then_inc(fac_ready, 1)
                        else:
                            nc.vector.tensor_tensor(fac[:, s, :], got[:, s, :, factor_at], o.w[:, at], ALU.mult
                                                    ).then_inc(fac_ready, 1)
                        dve.wait_ge(fac_ready, blk + 1)
                        nc.vector.tensor_tensor(msg[:, s], got[:, s, :, 0:D],
                                                fac[:, s, :].unsqueeze(2).broadcast_to([P, TB, D]), ALU.mult
                                                ).then_inc(msg_ready, 1)
                        dve.wait_ge(flags_in[s], 16 * (j + 1))
                        dve.wait_ge(turned_ready, blk + 1)
                        if not first:
                            dve.wait_ge(res_ready, blk - 1)
                        if not (first and s == 0):
                            dve.wait_ge(scanned, blk)
                        nc.vector.tensor_tensor_scan(tot[:, s, :], flags[:, s, :], turned[:, s, :],
                                                     tot[:, 1 - s, TB * P - 1:TB * P], ALU.mult, ALU.add
                                                     ).then_inc(scanned, 1)
                        if not first:
                            dve.wait_ge(sent[s], slot_sent * j)
                        if not store:
                            nc.vector.tensor_scalar(put[:, s, :], o.put[:, at], 1.0, None, ALU.mult
                                                    ).then_inc(put_ready, 1)
                        dve.wait_ge(res_ready, blk + 1)
                        r = res[:, s, 0:TB * D].rearrange("p (i f) -> p i f", f=D)
                        if scale_out:
                            nc.vector.tensor_tensor(scaled[:, :, :], r, o.root[:, at].unsqueeze(2)
                                                    .broadcast_to([P, TB, D]), ALU.mult).then_inc(scaled_ready, 1)
                            dve.wait_ge(scaled_ready, blk + 1)
                            r = scaled[:, :, :]
                        if bias is None:
                            nc.vector.tensor_copy(stage[:, s], r).then_inc(stage_ready, 1)
                        else:
                            nc.vector.tensor_tensor(stage[:, s], r, bias[:, :].unsqueeze(1).broadcast_to([P, TB, D]),
                                                    ALU.add).then_inc(stage_ready, 1)
                turns(dve, body)


def conv_phase(b, g, o, rows, table, out):
    nc = b.nc
    W2 = 2 * D
    with ExitStack() as c:
        pair = b.sb("conv_pair", [P, 2, TB, W2], F32, c)
        aux = b.sb("conv_aux", [P, 2, TB, R1 - D], F32, c)
        get = b.sb("conv_get", [P, 2, TB], I32, c)
        put = b.sb("conv_put", [P, 2, TB], I32, c)
        fac = b.sb("conv_fac", [P, TB], F32, c)
        lhs = b.sb("conv_lhs", [P, 2, TB * P], F32, c)
        hid = b.sb("conv_hid", [P, TB, W2], F32, c)
        msg = b.sb("conv_msg", [P, 2, TB, W2], F32, c)
        flags = b.sb("conv_flags", [P, 2, TB * P], F32, c)
        tot = b.sb("conv_tot", [P, 2, TB * P], F32, c)
        stage = b.sb("conv_stage", [P, 2, TB, W2], F32, c)
        scaled = b.sb("conv_scaled", [P, TB, W2], F32, c)
        scaled_ready = b.sem("conv_scaled_ready", c)
        pt = b.ps("conv_pt", [P, 2, 512], F32, c)
        pre = b.ps("conv_pre", [P, 2, 512], F32, c)
        turned = b.ps("conv_turned", [P, 2, 512], F32, c)
        res = b.ps("conv_res", [P, 2, 512], F32, c)
        flags_in = [b.sem(f"conv_flags_in{s}", c) for s in range(2)]
        aux_in = [b.sem(f"conv_aux_in{s}", c) for s in range(2)]
        x_in = [b.sem(f"conv_x_in{s}", c) for s in range(2)]
        got_in = [b.sem(f"conv_got_in{s}", c) for s in range(2)]
        sent = [b.sem(f"conv_sent{s}", c) for s in range(2)]
        get_ready = b.sem("conv_get_ready", c)
        put_ready = b.sem("conv_put_ready", c)
        pair_ready = b.sem("conv_pair_ready", c)
        pt_ready = b.sem("conv_pt_ready", c)
        lhs_ready = b.sem("conv_lhs_ready", c)
        pre_ready = b.sem("conv_pre_ready", c)
        hid_ready = b.sem("conv_hid_ready", c)
        fac_ready = b.sem("conv_fac_ready", c)
        msg_ready = b.sem("conv_msg_ready", c)
        turned_ready = b.sem("conv_turned_ready", c)
        scanned = b.sem("conv_scanned", c)
        res_ready = b.sem("conv_res_ready", c)
        stage_ready = b.sem("conv_stage_ready", c)
        zeroed = b.sem("conv_zeroed", c)
        with nc.Block() as block:
            @block.gpsimd
            def _(pool):
                limit_edges = pool.to_reg(EP)
                limit_nodes = pool.to_reg(N - 1)

                def gather(blk, s):
                    hold(pool, get_ready, blk + 1, g.pool_tick)
                    if not isinstance(blk, int) or blk >= 2:
                        hold(pool, pt_ready, blk - 1, g.pool_tick)
                    for i in range(TB):
                        nc.gpsimd.indirect_dma_start(
                            pair[:, s, i, 0:D], None, table[:, :],
                            bass.IndirectOffsetOnAxis(ap=get[:, s, i:i + 1], axis=0),
                            bounds_check=limit_edges, oob_is_err=False).then_inc(got_in[s], 16)

                for s in range(2):
                    gather(s, s)

                def body(j, first, last):
                    for s in range(2):
                        if not last:
                            gather(2 * j + 2 + s, s)
                        hold(pool, stage_ready, 2 * j + s + 1, g.pool_tick)
                        hold(pool, put_ready, 2 * j + s + 1, g.pool_tick)
                        for i in range(TB):
                            nc.gpsimd.indirect_dma_start(
                                out[:, :], bass.IndirectOffsetOnAxis(ap=put[:, s, i:i + 1], axis=0),
                                stage[:, s, i, :], None, bounds_check=limit_nodes, oob_is_err=False
                            ).then_inc(sent[s], 16)
                turns(pool, body)
                for s in range(2):
                    pool.wait_ge(got_in[s], 16 * TB * TURNS)
                    pool.wait_ge(sent[s], 16 * TB * TURNS)

            @block.sync
            def _(sp):
                def body(j, first, last):
                    for s in range(2):
                        blk = 2 * j + s
                        if not first:
                            hold(sp, fac_ready, blk - 1, g.sp_tick)
                            hold(sp, pt_ready, blk - 1, g.sp_tick)
                        r = rows[bass.ds(blk * (TB * P), TB * P), :].rearrange("(i p) c -> p i c", p=P)
                        sp.dma_start(aux[:, s], r[:, :, D:R1]).then_inc(aux_in[s], 16)
                        sp.dma_start(pair[:, s, :, D:W2], r[:, :, 0:D]).then_inc(x_in[s], 16)
                        load_flags(sp, g, o, flags, flags_in, None if first else scanned, j, s)
                turns(sp, body)

            @block.scalar
            def _(act):
                def body(j, first, last):
                    for s in range(2):
                        blk = 2 * j + s
                        act.wait_ge(pt_ready, blk + 1)
                        if not first:
                            act.wait_ge(pre_ready, blk - 1)
                        nc.scalar.activation(lhs[:, s, :], pt[:, s, :], ACT.Copy).then_inc(lhs_ready, 1)
                turns(act, body)

            @block.tensor
            def _(pe):
                def body(j, first, last):
                    for s in range(2):
                        blk = 2 * j + s
                        hold(pe, pair_ready, blk + 1, g.pe_tick)
                        hold(pe, x_in[s], 16 * (j + 1), g.pe_tick)
                        if not first:
                            hold(pe, lhs_ready, blk - 1, g.pe_tick)
                        for i in range(TB):
                            ins = nc.tensor.transpose(pt[:, s, i * P:(i + 1) * P], pair[:, s, i, :], g.ident[:, :])
                        ins.then_inc(pt_ready, 1)
                        hold(pe, lhs_ready, blk + 1, g.pe_tick)
                        if not first:
                            hold(pe, hid_ready, blk - 1, g.pe_tick)
                        for i in range(TB):
                            ins = nc.tensor.matmul(pre[:, s, i * P:(i + 1) * P], lhs[:, s, i * P:(i + 1) * P],
                                                   g.conv0[:, :], start=True, stop=True)
                        ins.then_inc(pre_ready, 1)
                        hold(pe, msg_ready, blk + 1, g.pe_tick)
                        if not first:
                            hold(pe, scanned, blk - 1, g.pe_tick)
                        for i in range(TB):
                            ins = nc.tensor.transpose(turned[:, s, i * P:(i + 1) * P], msg[:, s, i, :],
                                                      g.ident[:, :])
                        ins.then_inc(turned_ready, 1)
                        hold(pe, scanned, blk + 1, g.pe_tick)
                        if not first:
                            hold(pe, stage_ready, blk - 1, g.pe_tick)
                        for i in range(TB):
                            ins = nc.tensor.matmul(res[:, s, i * P:(i + 1) * P], tot[:, s, i * P:(i + 1) * P],
                                                   g.conv1[:, :], start=True, stop=True)
                        ins.then_inc(res_ready, 1)
                turns(pe, body)

            @block.vector
            def _(dve):
                def places(j, s):
                    dve.wait_ge(aux_in[s], 16 * (j + 1))
                    nc.vector.tensor_scalar(get[:, s, :], aux[:, s, :, 1], 1.0, None, ALU.mult
                                            ).then_inc(get_ready, 1)
                nc.vector.memset(tot[:, 1, :], 0.0).then_inc(zeroed, 1)
                for s in range(2):
                    places(0, s)
                dve.wait_ge(zeroed, 1)

                def body(j, first, last):
                    for s in range(2):
                        blk = 2 * j + s
                        at = bass.ds(blk * TB, TB)
                        dve.wait_ge(got_in[s], 16 * TB * (j + 1))
                        nc.vector.tensor_tensor(pair[:, s, :, 0:D], pair[:, s, :, 0:D],
                                                aux[:, s, :, 0:1].broadcast_to([P, TB, D]), ALU.mult
                                                ).then_inc(pair_ready, 1)
                        if not (first and s == 0):
                            dve.wait_ge(msg_ready, blk)
                        nc.vector.tensor_tensor(fac[:, :], aux[:, s, :, 0], o.w[:, at], ALU.mult
                                                ).then_inc(fac_ready, 1)
                        dve.wait_ge(pre_ready, blk + 1)
                        nc.vector.tensor_tensor(hid[:, :, :], pre[:, s, :].rearrange("p (i f) -> p i f", f=W2),
                                                g.conv_b[:, :].unsqueeze(1).broadcast_to([P, TB, W2]), ALU.add
                                                ).then_inc(hid_ready, 1)
                        dve.wait_ge(hid_ready, blk + 1)
                        dve.wait_ge(fac_ready, blk + 1)
                        if not first:
                            dve.wait_ge(turned_ready, blk - 1)
                        nc.vector.scalar_tensor_tensor(msg[:, s], hid[:, :, :], 0.0,
                                                       fac[:, :].unsqueeze(2).broadcast_to([P, TB, W2]),
                                                       ALU.max, ALU.mult).then_inc(msg_ready, 1)
                        dve.wait_ge(flags_in[s], 16 * (j + 1))
                        dve.wait_ge(turned_ready, blk + 1)
                        if not first:
                            dve.wait_ge(res_ready, blk - 1)
                        if not (first and s == 0):
                            dve.wait_ge(scanned, blk)
                        nc.vector.tensor_tensor_scan(tot[:, s, :], flags[:, s, :], turned[:, s, :],
                                                     tot[:, 1 - s, TB * P - 1:TB * P], ALU.mult, ALU.add
                                                     ).then_inc(scanned, 1)
                        if not last:
                            places(j + 1, s)
                        if not first:
                            dve.wait_ge(sent[s], 16 * TB * j)
                        nc.vector.tensor_scalar(put[:, s, :], o.put[:, at], 1.0, None, ALU.mult
                                                ).then_inc(put_ready, 1)
                        dve.wait_ge(res_ready, blk + 1)
                        nc.vector.tensor_tensor(scaled[:, :, :], res[:, s, :].rearrange("p (i f) -> p i f", f=W2),
                                                o.root[:, at].unsqueeze(2).broadcast_to([P, TB, W2]), ALU.mult
                                                ).then_inc(scaled_ready, 1)
                        dve.wait_ge(scaled_ready, blk + 1)
                        nc.vector.tensor_tensor(stage[:, s], scaled[:, :, :], g.root1_b[:, :].unsqueeze(1)
                                                .broadcast_to([P, TB, W2]), ALU.add).then_inc(stage_ready, 1)
                turns(dve, body)


def node_rows(table, k, tail):
    if tail:
        return table[P * PER:N, :].rearrange("(p n) f -> p n f", n=TAIL_ITEMS)
    return table[0:P * PER, :].rearrange("(p n) f -> p n f", p=P)[:, bass.ds(k * ITEMS, ITEMS), :]


def arrived(k, s):
    return (k - s) * (16 // RING) + 16


def chunks(eng, *stages):
    def step(at, slot_of, lowest, highest):
        for n, stage in enumerate(stages):
            if stage is not None and lowest <= n <= highest:
                stage(at(n), slot_of(n), False)
    for k in range(2 * RING):
        step(lambda n: k - n, lambda n: (k - n) % RING, 0, k)
    with eng.Fori(2, CHUNKS // RING) as h:
        for k in range(RING):
            step(lambda n: h * RING + (k - n), lambda n: (k - n) % RING, 0, len(stages))
    for k in range(CHUNKS, CHUNKS + len(stages)):
        for n, stage in enumerate(stages):
            if stage is not None and k - n <= CHUNKS:
                stage(k - n, (k - n) % RING, k - n == CHUNKS)


def old(k, lag=None):
    return not isinstance(k, int) or k >= (RING if lag is None else lag)


def dense_phase(b, g, name, x, msgs, out, extra=None, aux=(), root=False):
    nc = b.nc
    wx, wm, wo = x.shape[1], msgs.shape[1], out.shape[1]
    we = extra.shape[1] if extra is not None else 1
    pairs = (ITEMS + 1) // 2
    with ExitStack() as c:
        xs = b.sb(name + "_x", [P, RING, ITEMS, wx], F32, c)
        ms = b.sb(name + "_m", [P, RING, ITEMS, wm], F32, c)
        es = b.sb(name + "_e", [P, RING, ITEMS, we], F32, c)
        pre = b.sb(name + "_pre", [P, RING, ITEMS, D], F32, c)
        cen = b.sb(name + "_cen", [P, RING, ITEMS, D], F32, c)
        sq = b.sb(name + "_sq", [P, RING, ITEMS, D], F32, c)
        row = b.sb(name + "_row", [P, RING, ITEMS, wo], F32, c)
        stat = b.sb(name + "_stat", [P, 6, RING, ITEMS], F32, c)
        total, neg, total2, var, dev, inv = (stat[:, k] for k in range(6))
        x_in = [b.sem(f"{name}_x_in{s}", c) for s in range(RING)]
        m_in = [b.sem(f"{name}_m_in{s}", c) for s in range(RING)]
        e_in = [b.sem(f"{name}_e_in{s}", c) for s in range(RING)]
        pre_ready = b.sem(name + "_pre_ready", c)
        total_ready = b.sem(name + "_total_ready", c)
        neg_ready = b.sem(name + "_neg_ready", c)
        cen_ready = b.sem(name + "_cen_ready", c)
        sq_ready = b.sem(name + "_sq_ready", c)
        total2_ready = b.sem(name + "_total2_ready", c)
        var_ready = b.sem(name + "_var_ready", c)
        dev_ready = b.sem(name + "_dev_ready", c)
        inv_ready = b.sem(name + "_inv_ready", c)
        aux_ready = b.sem(name + "_aux_ready", c)
        row_ready = b.sem(name + "_row_ready", c)
        stored = [b.sem(f"{name}_stored{s}", c) for s in range(RING)]
        if root:
            packed = b.sb(name + "_packed", [P, 2, ITEMS * D], F32, c)
            packed_ready = b.sem(name + "_packed_ready", c)
            xt = b.sb(name + "_xt", [P, 2, pairs * P], F32, c)
            z = b.sb(name + "_z", [P, 2, ITEMS, 2 * D], F32, c)
            both = b.sb(name + "_both", [P, 2, ITEMS, D], F32, c)
            xt_ps = b.ps(name + "_xt_ps", [P, 1024], F32, c)
            root_ps = b.ps(name + "_root_ps", [P, 4 * 512], F32, c)
            xt_ps_ready = b.sem(name + "_xt_ps_ready", c)
            xt_ready = b.sem(name + "_xt_ready", c)
            root_ready = b.sem(name + "_root_ready", c)
            z_ready = b.sem(name + "_z_ready", c)
            act_ready = b.sem(name + "_act_ready", c)
            both_ready = b.sem(name + "_both_ready", c)

        def sizes(tail):
            return (TAIL_P, TAIL_ITEMS) if tail else (P, ITEMS)

        def spans(p, n):
            whole = n // 2
            yield 0, whole * p, P
            if n % 2:
                yield whole * p, (whole + 1) * p, D

        with nc.Block() as block:
            @block.sync
            def _(sp):
                def load(k, s, tail):
                    p, n = sizes(tail)
                    if old(k):
                        hold(sp, pre_ready, k - RING + 1, g.sp_tick)
                        if aux:
                            hold(sp, aux_ready, k - RING + 1, g.sp_tick)
                        if root:
                            hold(sp, packed_ready, k - RING + 1, g.sp_tick)
                            hold(sp, z_ready, k - RING + 1, g.sp_tick)
                    sp.dma_start(xs[0:p, s, 0:n, :], node_rows(x, k, tail)).then_inc(x_in[s], 16)
                    sp.dma_start(ms[0:p, s, 0:n, :], node_rows(msgs, k, tail)).then_inc(m_in[s], 16)
                    if extra is not None:
                        sp.dma_start(es[0:p, s, 0:n, :], node_rows(extra, k, tail)).then_inc(e_in[s], 16)

                def store(k, s, tail):
                    p, n = sizes(tail)
                    hold(sp, row_ready, k + 1, g.sp_tick)
                    if aux:
                        hold(sp, aux_ready, k + 1, g.sp_tick)
                    sp.dma_start(node_rows(out, k, tail), row[0:p, s, 0:n, :]).then_inc(stored[s], 16)
                chunks(sp, load, *[None] * (4 if root else 3), store)
                for s in range(RING):
                    sp.wait_ge(stored[s], 16 * (CHUNKS // RING + (s == CHUNKS % RING)))

            @block.gpsimd
            def _(pool):
                def sums(k, s, tail):
                    p, n = sizes(tail)
                    hold(pool, x_in[s], arrived(k, s), g.pool_tick)
                    if root:
                        t = s % 2
                        hold(pool, act_ready, k + 1, g.pool_tick)
                        nc.gpsimd.tensor_tensor(both[0:p, t, 0:n], z[0:p, t, 0:n, 0:D], z[0:p, t, 0:n, D:2 * D],
                                                ALU.add).then_inc(both_ready, 1)
                        hold(pool, both_ready, k + 1, g.pool_tick)
                        m = both[0:p, t, 0:n]
                    else:
                        hold(pool, m_in[s], arrived(k, s), g.pool_tick)
                        m = ms[0:p, s, 0:n, 0:D]
                    if old(k):
                        hold(pool, cen_ready, k - RING + 1, g.pool_tick)
                    nc.gpsimd.tensor_tensor(pre[0:p, s, 0:n], xs[0:p, s, 0:n, 0:D], m, ALU.add
                                            ).then_inc(pre_ready, 1)

                def rows(k, s, tail):
                    p, n = sizes(tail)
                    hold(pool, inv_ready, k + 1, g.pool_tick)
                    if old(k):
                        hold(pool, stored[s], arrived(k, s) - 16, g.pool_tick)
                    nc.gpsimd.tensor_tensor(row[0:p, s, 0:n, 0:D], cen[0:p, s, 0:n],
                                            inv[0:p, s, 0:n].unsqueeze(2).broadcast_to([p, n, D]), ALU.mult
                                            ).then_inc(row_ready, 1)
                chunks(pool, sums, None, None, rows)

            @block.vector
            def _(dve):
                def root_sum(k, s, tail):
                    p, n = sizes(tail)
                    t = s % 2
                    dve.wait_ge(root_ready, k + 1)
                    dve.wait_ge(m_in[s], arrived(k, s))
                    if old(k, 2):
                        dve.wait_ge(both_ready, k - 1)
                    nc.vector.tensor_tensor(z[0:p, t, 0:n], root_ps[0:p, 0:n * 2 * D]
                                            .rearrange("p (n f) -> p n f", f=2 * D), ms[0:p, s, 0:n], ALU.add
                                            ).then_inc(z_ready, 1)

                def center(k, s, tail):
                    p, n = sizes(tail)
                    dve.wait_ge(pre_ready, k + 1)
                    nc.vector.reduce_sum(total[0:p, s, 0:n], pre[0:p, s, 0:n], axis=AX).then_inc(total_ready, 1)
                    dve.wait_ge(total_ready, k + 1)
                    nc.vector.tensor_scalar(neg[0:p, s, 0:n], total[0:p, s, 0:n], -1.0 / D, None, ALU.mult
                                            ).then_inc(neg_ready, 1)
                    dve.wait_ge(neg_ready, k + 1)
                    if old(k):
                        dve.wait_ge(row_ready, k - RING + 1)
                        dve.wait_ge(sq_ready, k - RING + 1)
                    nc.vector.tensor_tensor(cen[0:p, s, 0:n], pre[0:p, s, 0:n],
                                            neg[0:p, s, 0:n].unsqueeze(2).broadcast_to([p, n, D]), ALU.add
                                            ).then_inc(cen_ready, 1)

                def variance(k, s, tail):
                    p, n = sizes(tail)
                    dve.wait_ge(sq_ready, k + 1)
                    nc.vector.reduce_sum(total2[0:p, s, 0:n], sq[0:p, s, 0:n], axis=AX).then_inc(total2_ready, 1)
                    dve.wait_ge(total2_ready, k + 1)
                    nc.vector.tensor_scalar(var[0:p, s, 0:n], total2[0:p, s, 0:n], 1.0 / D, EPS, ALU.mult, ALU.add
                                            ).then_inc(var_ready, 1)

                def inverse(k, s, tail):
                    p, n = sizes(tail)
                    dve.wait_ge(dev_ready, k + 1)
                    if old(k):
                        dve.wait_ge(row_ready, k - RING + 1)
                    nc.vector.reciprocal(inv[0:p, s, 0:n], dev[0:p, s, 0:n]).then_inc(inv_ready, 1)
                if root:
                    chunks(dve, root_sum, center, variance, inverse)
                else:
                    chunks(dve, center, variance, inverse)

            @block.scalar
            def _(act):
                def turned_rows(k, s, tail):
                    p, n = sizes(tail)
                    t = s % 2
                    act.wait_ge(xt_ps_ready, k + 1)
                    if old(k, 2):
                        act.wait_ge(root_ready, k - 1)
                    for lo, hi, rows in spans(p, n):
                        ins = nc.scalar.activation(xt[0:rows, t, lo:hi], xt_ps[0:rows, lo:hi], ACT.Copy)
                    ins.then_inc(xt_ready, 1)

                def pack(k, s, tail):
                    p, n = sizes(tail)
                    act.wait_ge(x_in[s], arrived(k, s))
                    if old(k, 2):
                        act.wait_ge(xt_ps_ready, k - 1)
                    nc.scalar.activation(packed[0:p, s % 2, 0:n * D].rearrange("p (n f) -> p n f", f=D),
                                         xs[0:p, s, 0:n, 0:D], ACT.Copy).then_inc(packed_ready, 1)

                def relu(k, s, tail):
                    p, n = sizes(tail)
                    act.wait_ge(z_ready, k + 1)
                    nc.scalar.activation(z[0:p, s % 2, 0:n], z[0:p, s % 2, 0:n], ACT.Relu, scale=0.5
                                         ).then_inc(act_ready, 1)

                def square(k, s, tail):
                    p, n = sizes(tail)
                    act.wait_ge(cen_ready, k + 1)
                    if old(k):
                        act.wait_ge(total2_ready, k - RING + 1)
                    nc.scalar.activation(sq[0:p, s, 0:n], cen[0:p, s, 0:n], ACT.Square).then_inc(sq_ready, 1)
                    if aux:
                        if old(k):
                            act.wait_ge(stored[s], arrived(k, s) - 16)
                        act.wait_ge(x_in[s], arrived(k, s))
                        act.wait_ge(m_in[s], arrived(k, s))
                        if extra is not None:
                            act.wait_ge(e_in[s], arrived(k, s))
                        for at, which, place, w in aux:
                            ins = nc.scalar.activation(row[0:p, s, 0:n, at:at + w],
                                                       {"x": xs, "m": ms, "e": es}[which][0:p, s, 0:n, place:place + w],
                                                       ACT.Copy)
                        ins.then_inc(aux_ready, 1)

                def deviation(k, s, tail):
                    p, n = sizes(tail)
                    act.wait_ge(var_ready, k + 1)
                    if old(k):
                        act.wait_ge(inv_ready, k - RING + 1)
                    nc.scalar.activation(dev[0:p, s, 0:n], var[0:p, s, 0:n], ACT.Sqrt).then_inc(dev_ready, 1)
                if root:
                    def turned_and_relu(k, s, tail):
                        turned_rows(k, s, tail)
                        relu(k, s, tail)
                    chunks(act, pack, turned_and_relu, square, deviation)
                else:
                    chunks(act, square, deviation)

            if root:
                @block.tensor
                def _(pe):
                    def turn(k, s, tail):
                        p, n = sizes(tail)
                        hold(pe, packed_ready, k + 1, g.pe_tick)
                        if old(k, 1):
                            hold(pe, xt_ready, k, g.pe_tick)
                        for i in range(0, n, 2):
                            m = min(2, n - i)
                            ins = nc.tensor.transpose(xt_ps[0:m * D, i // 2 * p:(i // 2 + 1) * p],
                                                      packed[0:p, s % 2, i * D:(i + m) * D], g.ident[0:p, 0:p])
                        ins.then_inc(xt_ps_ready, 1)

                    def product(k, s, tail):
                        p, n = sizes(tail)
                        hold(pe, xt_ready, k + 1, g.pe_tick)
                        if old(k, 1):
                            hold(pe, z_ready, k, g.pe_tick)
                        for i in range(0, n, 2):
                            m = min(2, n - i)
                            ins = nc.tensor.matmul(root_ps[0:p, i * 2 * D:(i + m) * 2 * D],
                                                   xt[0:m * D, s % 2, i // 2 * p:(i // 2 + 1) * p],
                                                   g.root1[0:m * D, 0:m * 2 * D], start=True, stop=True)
                        ins.then_inc(root_ready, 1)

                    def turn_and_product(k, s, tail):
                        turn(k, s, tail)
                        product(k, s, tail)
                    chunks(pe, turn_and_product)


class Globals:
    pass


class Order:

    def __init__(self, b, name):
        self.name = name
        self.put = b.sb(name + "_put_table", [P, NT], F32)
        self.get = b.sb(name + "_get_table", [P, NT], F32)
        self.w = b.sb(name + "_w_table", [P, NT], F32)
        self.root = b.sb(name + "_root_table", [P, NT], F32)
        self.flags = b.dram(name + "_flags_dram", [EP])


def fill_tables(eng, done, tables, before=0):
    for table, tile in tables:
        with eng.Fori(0, CHUNKS) as k:
            eng.dma_start(node_rows(table, k, False), tile).then_inc(done, 16)
        eng.dma_start(node_rows(table, CHUNKS, True), tile[0:TAIL_P, 0:TAIL_ITEMS, :]).then_inc(done, 16)
    eng.wait_ge(done, 16 * (before + len(tables) * (CHUNKS + 1)))


def build(nc, x, src, dst, attr, w, u, W1, b1, W2, b2, init, weight, root, bias, l2W, l2b, l3W, l3b, out):
    with ExitStack() as ctx:
        b = Build(nc, ctx)
        g = Globals()
        g.pool_tick = b.sem("pool_tick")
        g.pe_tick = b.sem("pe_tick")
        g.sp_tick = b.sem("sp_tick")
        g.unsorted = b.sb("unsorted", [1, 2], I32)
        g.ident = b.sb("ident", [P, P], F32)
        g.before = b.sb("before", [P, P], BF16)
        g.since = b.sb("since", [P, P], BF16)
        g.ones_b = b.sb("ones_b", [P, P], BF16)
        g.ones_f = b.sb("ones_f", [P, TB * P], F32)
        g.iota16 = b.sb("iota16", [P, NT], F16)
        g.pos = b.sb("pos", [P, NT], F32)
        g.src = b.sb("src_table", [P, NT], F32)
        g.dst = b.sb("dst_table", [P, NT], F32)
        g.w = b.sb("w_table", [P, NT], F32)
        g.lo = [b.sb(f"lo{k}", [P, NT], F32) for k in range(2)]
        g.hi = [b.sb(f"hi{k}", [P, NT], F32) for k in range(2)]
        g.first = [b.sb(f"first{k}", [P, HI], F32) for k in range(4)]
        g.w1 = b.sb("w1", [3 * A, HID], F32)
        g.w1u = b.sb("w1u", [1, HID], F32)
        g.uval = b.sb("uval", [1, 1], F32)
        g.w2 = b.sb("w2", [HID, D], F32)
        g.b1 = b.sb("b1", [HID, 1], F32)
        g.hb = b.sb("hb", [HID, 1], F32)
        g.b2 = b.sb("b2", [P, D], F32)
        g.conv0 = b.sb("conv0", [2 * D, 2 * D], F32)
        g.conv1 = b.sb("conv1", [2 * D, 2 * D], F32)
        g.conv_b = b.sb("conv_b", [P, 2 * D], F32)
        g.root1 = b.sb("root1", [2 * D, 4 * D], F32)
        g.root1_b = b.sb("root1_b", [P, 2 * D], F32)
        g.l2w = b.sb("l2w", [D, D], F32)
        g.l2b = b.sb("l2b", [P, D], F32)
        g.l3w = b.sb("l3w", [D, D], F32)
        g.l3b = b.sb("l3b", [P, D], F32)
        g.base = b.sb("base", [1, D], F32)
        g.base_all = b.sb("base_all", [P, D], F32)
        g.fill_m = b.sb("fill_m", [P, ITEMS, D + 1], F32)
        g.fill_nd = b.sb("fill_nd", [P, ITEMS, 2], F32)
        g.fill_1 = b.sb("fill_1", [P, ITEMS, 2 * D], F32)
        g.zero_row = b.sb("zero_row", [1, D], F32)
        g.fill_2 = b.sb("fill_2", [P, ITEMS, D], F32)
        g.fill_3 = b.sb("fill_3", [P, ITEMS, D], F32)
        order_d, order_s = Order(b, "D"), Order(b, "S")

        s_half = b.dram("s_half", [EP, SROW])
        s_rows = b.dram("s_rows", [EP, SROW])
        d_half = b.dram("d_half", [EP, DROW])
        d_rows = b.dram("d_rows", [EP, DROW])
        m0 = b.dram("m0", [N, D + 1])
        nd = b.dram("nd", [N, 2])
        x1 = b.dram("x1", [N, R1])
        x1_edges = b.dram("x1_edges", [EP, R1])
        sums1 = b.dram("sums1", [EP + 1, D])
        m1 = b.dram("m1", [N, 2 * D])
        x2 = b.dram("x2", [N, R2])
        m2 = b.dram("m2", [N, D])
        x3 = b.dram("x3", [N, R2])
        m3 = b.dram("m3", [N, D])

        setup_phase(b, g, src, dst, w, {
            "W1": W1, "u0": u[0:1, :], "W2": W2, "b1": b1, "b2": b2, "init": init, "weight": weight, "root": root,
            "bias0": bias[0:1], "bias1": bias[1:2], "l2W": l2W, "l2b": l2b, "l3W": l3W, "l3b": l3b})
        b.clear()
        hist_phase(b, g, "s0", g.lo[0], LO, g.first[0])
        b.clear()

        def fill_1(eng, done):
            fill_tables(eng, done, [(m0, g.fill_m[:, :, :]), (m2, g.fill_2[:, :, :])])

        def fill_2(eng, done):
            eng.dma_start(sums1[EP:EP + 1, :], g.zero_row[:, :]).then_inc(done, 16)
            fill_tables(eng, done, [(nd, g.fill_nd[:, :, :]), (m1, g.fill_1[:, :, :]), (m3, g.fill_3[:, :, :])], 1)

        radix_phase(b, g, "s1", attr, A, [(A, g.src), (A + 1, g.dst), (A + 2, g.w), (A + 3, g.hi[0])], SROW,
                    g.lo[0], LO, g.first[0], s_half, fill=fill_1, then=(g.hi[0], HI, g.first[1]))
        b.clear()
        radix_phase(b, g, "s2", s_half, SROW, [], SROW, None, HI, g.first[1], s_rows, fill=fill_2)
        b.clear()
        unsorted = g.unsorted[0:1, 0:1]
        hist_phase(b, g, "d0", g.lo[1], LO, g.first[2], flag=unsorted)
        b.clear()
        radix_phase(b, g, "d1", None, 0, [(0, g.src), (1, g.dst), (2, g.w), (3, g.hi[1])], DROW,
                    g.lo[1], LO, g.first[2], d_half, then=(g.hi[1], HI, g.first[3]), flag=unsorted)
        b.clear()
        radix_phase(b, g, "d2", d_half, DROW, [], DROW, None, HI, g.first[3], d_rows, flag=unsorted)
        b.clear()
        keep_phase(b, g, d_rows)
        b.clear()
        tables_phase(b, g, order_s, s_rows, A)
        b.clear()
        tables_phase(b, g, order_d, d_rows, 0)
        b.clear()
        degree_phase(b, g, order_d, nd)
        b.clear()
        edge_mlp_phase(b, g, order_s, s_rows, m0)
        b.clear()
        dense_phase(b, g, "l0", x, m0, x1, extra=nd, aux=((D, "e", 0, 2), (D + 2, "m", D, 1)))
        b.clear()
        message_phase(b, g, order_d, "p1", x1, R1, D, None, sums1, saved=x1_edges)
        b.clear()
        conv_phase(b, g, order_d, x1_edges, sums1, m1)
        b.clear()
        dense_phase(b, g, "l1", x1, m1, x2, aux=((D, "x", D + 2, 1),), root=True)
        b.clear()
        message_phase(b, g, order_s, "p3", x2, R2, None, g.l2w, m2, bias=g.l2b)
        b.clear()
        dense_phase(b, g, "l2", x2, m2, x3, aux=((D, "x", D, 1),))
        b.clear()
        message_phase(b, g, order_s, "p4", x3, R2, D, g.l3w, m3, bias=g.l3b, scale_out=True)
        b.clear()
        dense_phase(b, g, "l3", x3, m3, out)
        b.clear()


_INS = ["x", "src", "dst", "edge_attr_32", "edge_weight", "L0_gnn_u", "L0_gnn_W1", "L0_gnn_b1", "L0_gnn_W2",
        "L0_gnn_b2", "L1_gnn_init_weight", "L1_gnn_weight", "L1_gnn_root_weight", "L1_gnn_bias", "L2_gnn_W",
        "L2_gnn_b", "L3_gnn_weight", "L3_gnn_bias"]


def kernel(**inputs):
    import numpy as _np
    import concourse.bacc as _bacc
    from concourse import mybir as _mybir
    from concourse.bass_utils import run_bass_kernel_spmd as _run

    nc = _bacc.Bacc("TRN2", target_bir_lowering=False, num_devices=1)
    arrays, args = {}, []
    for name in _INS:
        a = _np.ascontiguousarray(inputs[name])
        arrays[f"in_{name}_dram"] = a
        args.append(nc.dram_tensor(f"in_{name}_dram", a.shape, _mybir.dt.from_np(a.dtype), kind="ExternalInput").ap())
    out = nc.dram_tensor("out_0_dram", (N, D), _mybir.dt.float32, kind="ExternalOutput").ap()
    build(nc, *args, out)
    r = _run(nc, [arrays], core_ids=[0])
    return r.results[0]["out_0_dram"]
```

```python
import concourse.bass as bass
from concourse import mybir
from contextlib import ExitStack

F32 = mybir.dt.float32
F16 = mybir.dt.float16
BF16 = mybir.dt.bfloat16
I32 = mybir.dt.int32
ALU = mybir.AluOpType
ACT = mybir.ActivationFunctionType
AX = mybir.AxisListType.X

P = 128
N = 100000
E = 50000
D = 64
A = 32
HID = 128
TB = 4
NB = -(-E // (P * TB))
NB += NB % 2
NT = NB * TB
EP = NT * P
TURNS = NB // 2
QT = NT // 4
LO = 256
HI = -(-N // LO)
PADKEY = HI * LO - 1
BIG = 1 << 20
ITEMS = 13
RING = 4
CHUNKS = N // P // ITEMS // RING * RING
PER = CHUNKS * ITEMS
TAIL = N - P * PER
TAIL_P = 32
TAIL_ITEMS = TAIL // TAIL_P
ND_P = 125
HUGE = 3.0e38
EPS = 1e-5
SROW = A + 4
DROW = 4
R1 = D + 3
R2 = D + 1
assert PADKEY >= N and TAIL_P * TAIL_ITEMS == TAIL and TAIL_ITEMS <= ITEMS and 16 % RING == 0




def turns(eng, body):
    body(0, True, False)
    with eng.Fori(1, TURNS - 1) as j:
        body(j, False, False)
    body(TURNS - 1, False, True)


def lagged(eng, *stages):
    most = max(lag for lag, _ in stages)
    peeled = 3
    assert most <= 2 * peeled - 2
    for k in range(2 * peeled):
        for lag, stage in stages:
            if k >= lag:
                stage(k - lag, (k - lag) % 2, (k - lag) // 2)
    with eng.Fori(peeled, TURNS) as j:
        for k in range(2):
            for lag, stage in stages:
                stage(2 * j + (k - lag), (k - lag) % 2, j + (k - lag) // 2)
    for k in range(NB, NB + most):
        for lag, stage in stages:
            if k - lag < NB:
                stage(k - lag, (k - lag) % 2, (k - lag) // 2)


def had(blk, before=2):
    return not isinstance(blk, int) or blk >= before


def hold(eng, sem, value, tick):
    eng.wait_ge(sem, value)
    if not isinstance(value, int):
        eng.sem_inc(tick, 1)


class Chain:

    def __init__(self, eng, sem, per):
        self.eng, self.sem, self.per = eng, sem, per

    def step(self, k):
        self.base, self.n = k * self.per, 0

    def link(self, ins):
        ins.then_inc(self.sem, 1)
        self.n += 1
        self.eng.wait_ge(self.sem, self.base + self.n)


class Build:
    def __init__(self, nc, ctx):
        self.nc, self.ctx, self.own = nc, ctx, []

    def sb(self, name, shape, dt, ctx=None):
        return (ctx or self.ctx).enter_context(self.nc.sbuf_tensor(name, shape, dt))

    def ps(self, name, shape, dt, ctx):
        return ctx.enter_context(self.nc.psum_tensor(name, shape, dt))

    def sem(self, name, ctx=None):
        sem = self.nc.alloc_semaphore(name)
        if ctx is not None:
            self.own.append(sem)
        return sem

    def clear(self):
        self.nc.clear_and_free_semaphores(self.own)
        self.own = []
        self.nc.all_engine_barrier()

    def dram(self, name, shape):
        return self.nc.dram_tensor(name, shape, F32, kind="Internal").ap()


def setup_phase(b, g, src, dst, w, weights):
    nc = b.nc
    with ExitStack() as c:
        rows_i = b.sb("rows_i", [QT, 2, 4, P], I32, c)
        rows_f = b.sb("rows_f", [QT, 3, 4, P], F32, c)
        next_i = b.sb("next_i", [QT, 4, P], I32, c)
        next_f = b.sb("next_f", [QT, 4, P], F32, c)
        falls = b.sb("falls", [QT, 4 * P], F32, c)
        fall = b.sb("fall", [QT, 1], F32, c)
        fall_all = b.sb("fall_all", [1, 1], F32, c)
        iota_i = b.sb("iota_i", [P, NT], I32, c)
        pos_i = b.sb("pos_i", [P, NT], I32, c)
        digit_i = b.sb("digit_i", [P, 2, NT], I32, c)
        digit_j = b.sb("digit_j", [P, 4, NT], I32, c)
        w2t = b.sb("w2t", [D, D], F32, c)
        hbase = b.sb("hbase", [P, 1], F32, c)
        tr = b.ps("setup_tr", [P, 3, 512], F32, c)
        small = b.ps("setup_small", [P, 4, 512], F32, c)
        fall_ps = b.ps("fall_ps", [P, 512], F32, c)
        fall_ready = b.sem("fall_ready", c)
        padded = b.sem("padded", c)
        loaded = b.sem("loaded", c)
        wloaded = b.sem("wloaded", c)
        made = b.sem("made", c)
        cast = b.sem("cast", c)
        columns = b.sem("columns", c)
        dv = b.sem("setup_dve", c)
        small_done = b.sem("small_done", c)
        rows_ready = b.sem("rows_ready", c)
        full = E // P
        rest = E - full * P
        W = weights

        def spread(row, width):
            return row.broadcast_to([P, width])
        loads = [(g.w1[:, :], W["W1"][0:3 * A, :]), (g.w2[:, :], W["W2"]),
                 (g.b1[:, :], W["b1"].rearrange("(p a) -> p a", a=1)),
                 (g.w1u[:, :], W["W1"][3 * A:3 * A + 1, :]), (g.uval[:, :], W["u0"]),
                 (g.b2[:, :], spread(W["b2"].rearrange("(p a) -> p a", p=1), D)),
                 (g.conv_b[:, :], spread(W["bias0"].rearrange("p k o -> p (k o)"), 2 * D)),
                 (g.l2b[:, :], spread(W["l2b"].rearrange("(p a) -> p a", p=1), D)),
                 (g.l3b[:, :], spread(W["l3b"].rearrange("(p a) -> p a", p=1), D)),
                 (w2t[:, :], W["l2W"]), (g.l3w[:, :], W["l3W"]),
                 (g.root1_b[:, :], spread(W["bias1"].rearrange("p k o -> p (k o)"), 2 * D))]
        for k in range(2):
            o = slice(k * D, k * D + D)
            far = slice(2 * D + k * D, 3 * D + k * D)
            loads += [(g.conv0[0:D, o], W["init"][k]), (g.conv0[D:2 * D, o], W["root"][0, k]),
                      (g.root1[0:D, o], W["root"][1, k]), (g.root1[D:2 * D, far], W["root"][1, k]),
                      (g.conv1[o, o], W["weight"][0, k])]
        with nc.Block() as block:
            @block.gpsimd
            def _(pool):
                for t, value in ((g.ident, 0.0), (g.before, 1.0), (g.since, 1.0), (g.down, 0.0), (g.around, 0.0)):
                    nc.gpsimd.memset(t[:, :], value).then_inc(made, 1)
                nc.gpsimd.iota(iota_i[:, :], [[1, NT]], base=0, channel_multiplier=0).then_inc(made, 1)
                nc.gpsimd.iota(pos_i[:, :], [[P, NT]], base=0, channel_multiplier=1).then_inc(made, 1)
                pool.wait_ge(made, 7)
                for t, base in ((g.ident, 0), (g.down, -1), (g.around, P - 1)):
                    nc.gpsimd.affine_select(out=t[:, :], in_=t[:, :], compare_op=ALU.not_equal, fill=1.0,
                                            base=base, pattern=[[-1, P]], channel_multiplier=1).then_inc(made, 1)
                nc.gpsimd.affine_select(out=g.before[:, :], in_=g.before[:, :], compare_op=ALU.is_gt, fill=0.0,
                                        base=0, pattern=[[1, P]], channel_multiplier=-1).then_inc(made, 1)
                nc.gpsimd.affine_select(out=g.since[:, :], in_=g.since[:, :], compare_op=ALU.is_ge, fill=0.0,
                                        base=0, pattern=[[-1, P]], channel_multiplier=1).then_inc(made, 1)

            @block.sync
            def _(sp):
                hold(sp, padded, 6, g.sp_tick)
                for k, a in ((0, src), (1, dst), (2, w)):
                    to = rows_f[:, 2] if k == 2 else rows_i[:, k]
                    for q in range(4):
                        n = min(QT, full - q * QT)
                        sp.dma_start(to[0:n, q, :], a[q * QT * P:(q * QT + n) * P].rearrange("(t p) -> t p", p=P)
                                     ).then_inc(loaded, 16)
                    sp.dma_start(to[full - 3 * QT:full - 3 * QT + 1, 3, 0:rest],
                                 a[full * P:E].rearrange("(t p) -> t p", t=1)).then_inc(loaded, 16)
                for q in range(4):
                    n = min(QT, full - q * QT)
                    sp.dma_start(next_i[0:n, q, :], dst[q * QT * P + 1:(q * QT + n) * P + 1]
                                 .rearrange("(t p) -> t p", p=P)).then_inc(loaded, 16)
                sp.dma_start(next_i[full - 3 * QT:full - 3 * QT + 1, 3, 0:rest - 1],
                             dst[full * P + 1:E].rearrange("(t p) -> t p", t=1)).then_inc(loaded, 16)

            @block.scalar
            def _(act):
                act.wait_ge(padded, 6)
                for to, a in loads:
                    act.dma_start(to, a).then_inc(wloaded, 16)

            @block.vector
            def _(dve):
                ch = Chain(dve, dv, 0)
                ch.step(0)
                nc.vector.memset(rows_i[:, :, 3, :], PADKEY).then_inc(padded, 1)
                nc.vector.memset(next_i[:, 3, :], PADKEY).then_inc(padded, 1)
                nc.vector.memset(rows_f[:, 2, 3, :], 0.0).then_inc(padded, 1)
                nc.vector.memset(g.conv1[:, :], 0.0).then_inc(padded, 1)
                nc.vector.memset(g.root1[:, :], 0.0).then_inc(padded, 1)
                nc.vector.memset(g.ones_f[:, :], 1.0).then_inc(padded, 1)
                ch.link(nc.vector.memset(g.ones_b[:, :], 1.0))
                dve.wait_ge(made, 7)
                nc.vector.tensor_copy(g.iota16[:, :], iota_i[:, :])
                nc.vector.tensor_copy(g.pos[:, :], pos_i[:, :])
                dve.wait_ge(loaded, 16 * 20)
                for k in range(2):
                    nc.vector.tensor_copy(rows_f[:, k], rows_i[:, k]).then_inc(cast, 1)
                ch.link(nc.vector.tensor_copy(next_f[:, :, :], next_i[:, :, :]))
                dve.wait_ge(cast, 2)
                ch.link(nc.vector.tensor_tensor(falls[:, :].rearrange("t (q p) -> t q p", p=P), rows_f[:, 1],
                                                next_f[:, :, :], ALU.is_gt))
                nc.vector.reduce_max(fall[:, :], falls[:, :], axis=AX).then_inc(fall_ready, 1)
                dve.wait_ge(fall_ready, 2)
                ch.link(nc.vector.tensor_scalar(fall_all[:, :], fall_ps[0:1, 0:1], 1.0, None, ALU.min))
                ch.link(nc.vector.tensor_copy(g.unsorted[0:1, 0:1], fall_all[:, :]))
                for k, to in enumerate((g.src, g.dst, g.w)):
                    dve.wait_ge(columns, k + 1)
                    ch.link(nc.vector.tensor_copy(to[:, :], tr[:, k, 0:NT]))
                for k, key in enumerate((g.src, g.dst)):
                    ch.link(nc.vector.tensor_copy(digit_i[:, k], key[:, :]))
                    ch.link(nc.vector.tensor_scalar(digit_j[:, 2 * k], digit_i[:, k], LO - 1, None, ALU.bitwise_and))
                    ch.link(nc.vector.tensor_scalar(digit_j[:, 2 * k + 1], digit_i[:, k], 8, None,
                                                    ALU.logical_shift_right))
                    ch.link(nc.vector.tensor_copy(g.lo[k][:, :], digit_j[:, 2 * k]))
                    ch.link(nc.vector.tensor_copy(g.hi[k][:, :], digit_j[:, 2 * k + 1]))
                dve.wait_ge(small_done, 1)
                ch.link(nc.vector.tensor_tensor(g.hb[:, :], small[:, 0, 0:1], g.b1[:, :], ALU.add))
                nc.vector.tensor_scalar(hbase[:, :], g.hb[:, :], 0.0, None, ALU.max).then_inc(rows_ready, 1)
                dve.wait_ge(small_done, 2)
                ch.link(nc.vector.memset(g.fill_m[:, :, D:D + 1], 0.0))
                nc.vector.tensor_tensor(g.base[0:1, :], small[0:1, 1, 0:D], g.b2[0:1, :], ALU.add
                                        ).then_inc(rows_ready, 1)
                dve.wait_ge(small_done, 3)
                ch.link(nc.vector.tensor_copy(g.base_all[:, :], small[:, 2, 0:D]))
                ch.link(nc.vector.tensor_copy(g.fill_m[:, :, 0:D],
                                              g.base_all[:, :].unsqueeze(1).broadcast_to([P, ITEMS, D])))
                ch.link(nc.vector.memset(g.zero_row[:, :], 0.0))
                ch.link(nc.vector.memset(g.eps[:, :], EPS))
                ch.link(nc.vector.memset(g.fill_nd[:, :, 0:1], 0.0))
                ch.link(nc.vector.memset(g.fill_nd[:, :, 1:2], float(EP)))
                ch.link(nc.vector.tensor_copy(g.l2w[:, :], small[0:D, 3, 0:D]))
                for to, row in ((g.fill_1, g.root1_b), (g.fill_2, g.l2b), (g.fill_3, g.l3b)):
                    ch.link(nc.vector.tensor_copy(to[:, :, :], row[:, :].unsqueeze(1).broadcast_to(list(to.shape))))

            @block.tensor
            def _(pe):
                pe.wait_ge(made, 12)
                pe.wait_ge(loaded, 16 * 20)
                pe.wait_ge(cast, 2)
                pe.wait_ge(fall_ready, 1)
                nc.tensor.matmul(fall_ps[0:1, 0:1], fall[:, :], g.ones_f[0:QT, 0:1], start=True, stop=True
                                 ).then_inc(fall_ready, 1)
                for k in range(3):
                    for q in range(4):
                        last = nc.tensor.transpose(tr[:, k, q * QT:(q + 1) * QT], rows_f[:, k, q, :],
                                                   g.ident[0:QT, 0:QT])
                    last.then_inc(columns, 1)
                pe.wait_ge(wloaded, 16 * len(loads))
                nc.tensor.transpose(small[0:D, 3, 0:D], w2t[:, :], g.ident[0:D, 0:D])
                pe.wait_ge(padded, 6)
                nc.tensor.matmul(small[:, 0, 0:1], g.w1u[0:1, :], g.uval[0:1, :], start=True, stop=True
                                 ).then_inc(small_done, 1)
                pe.wait_ge(rows_ready, 1)
                nc.tensor.matmul(small[0:1, 1, 0:D], hbase[:, :], g.w2[:, :], start=True, stop=True
                                 ).then_inc(small_done, 1)
                pe.wait_ge(rows_ready, 2)
                nc.tensor.matmul(small[:, 2, 0:D], g.ones_f[0:1, 0:P], g.base[0:1, :], start=True, stop=True
                                 ).then_inc(small_done, 1)


def guarded(eng, body, flag, wanted):
    if flag is None:
        body()
    else:
        with eng.If(eng.value_load(flag) == wanted):
            body()


def hist_phase(b, g, name, digit, buckets, first_pos, flag=None):
    nc = b.nc
    with ExitStack() as c:
        hot = b.sb(name + "_hot", [P, 2, TB, buckets], BF16, c)
        counts = b.sb(name + "_counts", [P, buckets], F32, c)
        incl = b.sb(name + "_incl", [P, buckets], F32, c)
        acc = b.ps(name + "_acc", [P, 512], F32, c)
        hot_ready = b.sem(name + "_hot_ready", c)
        hot_used = b.sem(name + "_hot_used", c)
        chain = b.sem(name + "_chain", c)
        with nc.Block() as block:
            @block.vector
            def _(dve):
                def body(j, first, last):
                    for s in range(2):
                        if not first:
                            dve.wait_ge(hot_used, 2 * j + s - 1)
                        for i in range(TB):
                            ins = nc.vector.tensor_scalar(hot[:, s, i, :], g.iota16[:, 0:buckets],
                                                          digit[:, bass.ds((2 * j + s) * TB + i, 1)], None,
                                                          ALU.is_equal)
                        ins.then_inc(hot_ready, 1)

                def program():
                    turns(dve, body)
                    dve.wait_ge(hot_used, NB)
                    first_places(nc, dve, g, chain, acc, counts, incl, first_pos, buckets)
                guarded(dve, program, flag, 1)

            @block.tensor
            def _(pe):
                def body(j, first, last):
                    for s in range(2):
                        hold(pe, hot_ready, 2 * j + s + 1, g.pe_tick)
                        for i in range(TB):
                            ins = nc.tensor.matmul(acc[:, 0:buckets], g.ones_b[:, :], hot[:, s, i, :],
                                                   start=first and s == 0 and i == 0,
                                                   stop=last and s == 1 and i == TB - 1, skip_group_check=True)
                        ins.then_inc(hot_used, 1)
                guarded(pe, lambda: turns(pe, body), flag, 1)


def first_places(nc, dve, g, sem, acc, counts, incl, first_pos, buckets):
    ch = Chain(dve, sem, 0)
    ch.step(0)
    ch.link(nc.vector.tensor_copy(counts[:, 0:buckets], acc[:, 0:buckets]))
    ch.link(nc.vector.tensor_tensor_scan(incl[:, 0:buckets], g.ones_f[:, 0:buckets], counts[:, 0:buckets], 0.0,
                                         ALU.mult, ALU.add))
    ch.link(nc.vector.tensor_tensor(first_pos[:, 0:buckets], incl[:, 0:buckets], counts[:, 0:buckets],
                                    ALU.subtract))


def radix_phase(b, g, name, rows_in, loads_w, make, width, digit, buckets, first_pos, out, fill=None, then=None,
                flag=None):
    nc = b.nc
    with ExitStack() as c:
        whole = b.sb(name + "_whole", [P, NT, max(loads_w, 1)], F32, c)
        rows = b.sb(name + "_rows", [P, 2, TB, width], F32, c)
        hot = b.sb(name + "_hot", [P, 2, TB, buckets], BF16, c)
        junk = b.sb(name + "_junk", [P, 2, buckets], BF16, c)
        place_f = b.sb(name + "_place_f", [P, 2, TB], F32, c)
        place_i = b.sb(name + "_place_i", [P, 2, TB], I32, c)
        seen = b.ps(name + "_seen", [P, 2, 512], F32, c)
        if then:
            hot2 = b.sb(name + "_hot2", [P, 2, TB, then[1]], BF16, c)
            counts = b.sb(name + "_counts", [P, then[1]], F32, c)
            incl = b.sb(name + "_incl", [P, then[1]], F32, c)
            acc = b.ps(name + "_acc", [P, 512], F32, c)
            hot2_ready = b.sem(name + "_hot2_ready", c)
            hot2_used = b.sem(name + "_hot2_used", c)
            chain = b.sem(name + "_chain", c)
        cleared = b.sem(name + "_cleared", c)
        loaded = [b.sem(f"{name}_loaded{s}", c) for s in range(2)]
        copied = b.sem(name + "_copied", c)
        hot_ready = b.sem(name + "_hot_ready", c)
        seen_ready = b.sem(name + "_seen_ready", c)
        summed = b.sem(name + "_summed", c)
        place_ready = b.sem(name + "_place_ready", c)
        sent = [b.sem(f"{name}_sent{s}", c) for s in range(2)]
        filled = b.sem(name + "_filled", c)
        partial = rows_in is not None and rows_in.shape[0] < EP

        def arrive(eng, j, s, last):
            eng.wait_ge(loaded[s], 16 * (j + 1 + (last and s == 1 and partial)))

        with nc.Block() as block:
            @block.sync
            def _(sp):
                def load_tiles(t, n, s):
                    sp.dma_start(whole[:, bass.ds(t, n), :], rows_in[bass.ds(t * P, n * P), 0:loads_w]
                                 .rearrange("(t p) c -> p t c", p=P)).then_inc(loaded[s], 16)

                def body(j, first, last):
                    for s in range(2):
                        if not first:
                            hold(sp, loaded[s], 16 * j, g.sp_tick)
                        if last and s == 1 and partial:
                            full, rest = divmod(rows_in.shape[0], P)
                            load_tiles((NB - 1) * TB, full - (NB - 1) * TB, s)
                            sp.wait_ge(cleared, 1)
                            sp.dma_start(whole[0:rest, full, :], rows_in[full * P:, 0:loads_w]
                                         ).then_inc(loaded[s], 16)
                        else:
                            load_tiles((2 * j + s) * TB, TB, s)
                if loads_w:
                    guarded(sp, lambda: turns(sp, body), flag, 1)
                if fill:
                    fill_table(sp, g.sp_tick, filled, place_ready, *fill, behind=NB - CHUNKS - 2)

            @block.scalar
            def _(act):
                def body(j, first, last):
                    for s in range(2):
                        if not first:
                            act.wait_ge(sent[s], 16 * TB * j)
                        arrive(act, j, s, last)
                        nc.scalar.activation(rows[:, s, :, 0:loads_w],
                                             whole[:, bass.ds((2 * j + s) * TB, TB), :], ACT.Copy
                                             ).then_inc(copied, 1)

                if loads_w:
                    guarded(act, lambda: turns(act, body), flag, 1)

            @block.gpsimd
            def _(pool):
                limit = pool.to_reg(EP - 1)

                def body(j, first, last):
                    for s in range(2):
                        hold(pool, place_ready, 2 * j + s + 1, g.pool_tick)
                        if loads_w:
                            hold(pool, copied, 2 * j + s + 1, g.pool_tick)
                        for i in range(TB):
                            nc.gpsimd.indirect_dma_start(
                                out[:, :], bass.IndirectOffsetOnAxis(ap=place_i[:, s, i:i + 1], axis=0),
                                rows[:, s, i, :], None, bounds_check=limit, oob_is_err=False
                            ).then_inc(sent[s], 16)

                def program():
                    turns(pool, body)
                    for s in range(2):
                        pool.wait_ge(sent[s], 16 * TB * TURNS)
                guarded(pool, program, flag, 1)

            @block.vector
            def _(dve):
                def one_hot(j, s, i):
                    t = (2 * j + s) * TB + i
                    col = digit[:, bass.ds(t, 1)] if digit is not None else whole[:, bass.ds(t, 1), width - 1]
                    nc.vector.tensor_scalar(hot[:, s, i, :], g.iota16[:, 0:buckets], col, None,
                                            ALU.is_equal).then_inc(hot_ready, 1)

                def body(j, first, last):
                    for s in range(2):
                        blk = 2 * j + s
                        if then and not first:
                            dve.wait_ge(hot2_used, blk - 1)
                        for i in range(TB):
                            dve.wait_ge(seen_ready, blk * TB + i + 1)
                            nc.vector.scalar_tensor_tensor(junk[:, i % 2, :], seen[:, i % 2, 0:buckets], 1.0,
                                                           hot[:, s, i, :], ALU.mult, ALU.mult,
                                                           accum_out=place_f[:, s, i:i + 1]).then_inc(summed, 1)
                            if not (last and s == 1):
                                jn, sn = (j, 1) if s == 0 else (j + 1, 0)
                                if digit is None and i == 0:
                                    arrive(dve, jn, sn, last)
                                one_hot(jn, sn, i)
                            if then:
                                ins = nc.vector.tensor_scalar(hot2[:, s, i, :], g.iota16[:, 0:then[1]],
                                                              then[0][:, bass.ds(blk * TB + i, 1)], None,
                                                              ALU.is_equal)
                        if then:
                            ins.then_inc(hot2_ready, 1)
                        if not first:
                            dve.wait_ge(sent[s], 16 * TB * j)
                        for at, table in make:
                            nc.vector.tensor_scalar(rows[:, s, :, at], table[:, bass.ds(blk * TB, TB)], 1.0,
                                                    None, ALU.mult)
                        dve.wait_ge(summed, (blk + 1) * TB)
                        nc.vector.tensor_scalar(place_i[:, s, :], place_f[:, s, :], 1.0, None, ALU.mult
                                                ).then_inc(place_ready, 1)

                def program():
                    if partial:
                        nc.vector.memset(whole[:, rows_in.shape[0] // P:NT, :], 0.0).then_inc(cleared, 1)
                    if digit is None:
                        arrive(dve, 0, 0, False)
                    for i in range(TB):
                        one_hot(0, 0, i)
                    turns(dve, body)
                    if then:
                        dve.wait_ge(hot2_used, NB)
                        first_places(nc, dve, g, chain, acc, counts, incl, then[2], then[1])
                guarded(dve, program, flag, 1)

            @block.tensor
            def _(pe):
                def count(blk, s, first, last):
                    hold(pe, hot2_ready, blk + 1, g.pe_tick)
                    for i in range(TB):
                        ins = nc.tensor.matmul(acc[:, 0:then[1]], g.ones_b[:, :], hot2[:, s, i, :],
                                               start=first and i == 0, stop=last and i == TB - 1,
                                               skip_group_check=True)
                    ins.then_inc(hot2_used, 1)

                def body(j, first, last):
                    for s in range(2):
                        for i in range(TB):
                            t = (2 * j + s) * TB + i
                            mine, other = seen[:, i % 2, 0:buckets], seen[:, 1 - i % 2, 0:buckets]
                            end = last and s == 1 and i == TB - 1
                            pe.wait_ge(hot_ready, t + 1)
                            nc.tensor.matmul(mine, g.before[:, :], hot[:, s, i, :], start=False,
                                             stop=last and s == 1 and i >= TB - 2, skip_group_check=True
                                             ).then_inc(seen_ready, 1)
                            if not (first and s == 0 and i == 0):
                                pe.wait_ge(summed, t)
                                if not end:
                                    s_before, i_before = (s, i - 1) if i else (1 - s, TB - 1)
                                    nc.tensor.matmul(other, g.since[:, :], hot[:, s_before, i_before, :], start=False,
                                                     stop=False, skip_group_check=True)
                            if not end:
                                nc.tensor.matmul(other, g.ones_b[:, :], hot[:, s, i, :], start=False,
                                                 stop=False, skip_group_check=True)
                            if then and i == 1 and not (first and s == 0):
                                count(2 * j + s - 1, 1 - s, first and s == 1, False)
                    if then and last:
                        count(NB - 1, 1, False, True)

                def program():
                    for k in range(2):
                        nc.tensor.matmul(seen[:, k, 0:buckets], g.ident[:, :], first_pos[:, 0:buckets], start=True,
                                         stop=False, skip_group_check=True)
                    turns(pe, body)
                guarded(pe, program, flag, 1)


def tables_phase(b, g, o, rows, cols, kept=None):
    nc = b.nc
    key_at = 0 if o.name == "S" else 1
    with ExitStack() as c:
        cur = b.sb(o.name + "_cur", [P, NT, 4], F32, c)
        key = b.sb(o.name + "_key", [P, NT], F32, c)
        same = b.sb(o.name + "_same", [P, NT], F32, c)
        flag_rows = b.sb(o.name + "_flag_rows", [QT, 4, P], F32, c)
        zero = b.sb(o.name + "_zero", [1, 1], F32, c)
        nxt = b.ps(o.name + "_nxt", [P, 512], F32, c)
        tr = b.ps(o.name + "_flag_tr", [QT, 4, P], F32, c)
        loaded = b.sem(o.name + "_loaded", c)
        ch_sem = b.sem(o.name + "_chain", c)
        key_ready = b.sem(o.name + "_key_ready", c)
        nxt_ready = b.sem(o.name + "_nxt_ready", c)
        same_ready = b.sem(o.name + "_same_ready", c)
        turned = b.sem(o.name + "_turned", c)
        rows_ready = b.sem(o.name + "_rows_ready", c)
        stored = b.sem(o.name + "_stored", c)
        flag = None if kept is None else g.unsorted[0:1, 0:1]
        with nc.Block() as block:
            @block.sync
            def _(sp):
                def load():
                    for q in range(4):
                        a = q * QT
                        sp.dma_start(cur[:, a:a + QT, :], rows[a * P:(a + QT) * P, cols:cols + 4]
                                     .rearrange("(t p) c -> p t c", p=P)).then_inc(loaded, 16)
                guarded(sp, load, flag, 1)
                hold(sp, rows_ready, 1, g.sp_tick)
                for q in range(4):
                    k = QT if q < 3 else QT - 1
                    sp.dma_start(o.flags[q * QT * P + 1:(q * QT + k) * P + 1].rearrange("(t p) -> t p", p=P),
                                 flag_rows[0:k, q, :]).then_inc(stored, 16)
                sp.dma_start(o.flags[EP - P + 1:EP].rearrange("(t p) -> t p", t=1),
                             flag_rows[QT - 1:QT, 3, 0:P - 1]).then_inc(stored, 16)
                sp.dma_start(o.flags[0:1].rearrange("(t p) -> t p", t=1), zero[:, :]).then_inc(stored, 16)
                hold(sp, stored, 16 * 6, g.sp_tick)

            @block.vector
            def _(dve):
                ch = Chain(dve, ch_sem, 0)
                ch.step(0)
                ch.link(nc.vector.memset(zero[:, :], 0.0))
                if kept is not None:
                    def take():
                        for k, table in enumerate(kept):
                            nc.vector.tensor_copy(cur[:, :, k], table[:, :]).then_inc(loaded, 16)
                        dve.sem_inc(loaded, 16)
                    guarded(dve, take, flag, 0)
                dve.wait_ge(loaded, 16 * 4)
                nc.vector.tensor_copy(key[:, :], cur[:, :, key_at]).then_inc(key_ready, 1)
                dve.wait_ge(nxt_ready, 1)
                nc.vector.tensor_tensor(same[:, :], cur[:, :, key_at], nxt[:, 0:NT], ALU.is_equal
                                        ).then_inc(same_ready, 1)
                dve.wait_ge(same_ready, 1)
                ch.link(nc.vector.scalar_tensor_tensor(o.put[:, :], same[:, :], float(BIG), cur[:, :, key_at],
                                                       ALU.mult, ALU.add))
                ch.link(nc.vector.tensor_scalar(o.get[:, :], cur[:, :, 1 - key_at], float(N - 1), None, ALU.min))
                ch.link(nc.vector.tensor_copy(o.w[:, :], cur[:, :, 2]))
                dve.wait_ge(turned, 1)
                nc.vector.tensor_copy(flag_rows[:, :, :], tr[:, :, :]).then_inc(rows_ready, 1)

            @block.tensor
            def _(pe):
                pe.wait_ge(key_ready, 1)
                nc.tensor.matmul(nxt[:, 0:NT], g.down[:, :], key[:, :], start=True, stop=False, skip_group_check=True)
                nc.tensor.matmul(nxt[:, 0:NT - 1], g.around[:, :], key[:, 1:NT], start=False, stop=True,
                                 skip_group_check=True).then_inc(nxt_ready, 1)
                pe.wait_ge(same_ready, 1)
                for q in range(4):
                    last = nc.tensor.transpose(tr[:, q, :], same[:, q * QT:(q + 1) * QT], g.ident[:, :])
                last.then_inc(turned, 1)


def load_row(sp, row, ring, done, blk, s):
    sp.dma_start(ring[:, s, :], row[bass.ds(blk * (TB * P), TB * P)].rearrange("(a n) -> a n", a=1)
                 .broadcast_to([ring.shape[0], TB * P])).then_inc(done[s], 16)


def totals_phase(b, g, o, count, fills=()):
    nc = b.nc
    n = o.name + "_tot_"
    with ExitStack() as c:
        flags = b.sb(n + "flags", [NB, TB * P], F32, c)
        run = b.sb(n + "run", [NB, TB * P], F32, c)
        kept = b.sb(n + "kept", [NB, 2], F32, c)
        ends = b.sb(n + "ends", [1, 2, NB], F32, c)
        carry = b.sb(n + "carry", [1, NB + 1], F32, c)
        carry_col = b.sb(n + "carry_col", [NB, 1], F32, c)
        total = b.sb(n + "total", [NB, TB * P], F32, c)
        inverse = b.sb(n + "inverse", [NB, TB * P], F32, c)
        col = b.sb(n + "col", [P, NT], F32, c)
        low = b.sb(n + "low", [P, NT], F32, c)
        some = b.sb(n + "some", [P, NT], F32, c)
        root = b.sb(n + "root", [P, NT], F32, c)
        inv = b.sb(n + "inv", [P, NT], F32, c)
        w_ps = b.ps(n + "w_ps", [NB, TB, P], F32, c)
        ends_ps = b.ps(n + "ends_ps", [1, 2, 256], F32, c)
        carry_ps = b.ps(n + "carry_ps", [NB, 512], F32, c)
        col_ps = b.ps(n + "col_ps", [P, 512], F32, c)
        flags_in = b.sem(n + "flags_in", c)
        values_ready = b.sem(n + "values_ready", c)
        ends_ready = b.sem(n + "ends_ready", c)
        ends_turned = b.sem(n + "ends_turned", c)
        carry_ready = b.sem(n + "carry_ready", c)
        carry_turned = b.sem(n + "carry_turned", c)
        total_ready = b.sem(n + "total_ready", c)
        inverse_ready = b.sem(n + "inverse_ready", c)
        col_ready = b.sem(n + "col_ready", c)
        low_ready = b.sem(n + "low_ready", c)
        root_ready = b.sem(n + "root_ready", c)
        chain = b.sem(n + "chain", c)
        stored = b.sem(n + "stored", c)
        filled = b.sem(n + "filled", c)
        with nc.Block() as block:
            @block.sync
            def _(sp):
                sp.dma_start(flags[:, :], o.flags.rearrange("(r n) -> r n", r=NB)).then_inc(flags_in, 16)
                for rows, tile in fills:
                    sp.dma_start(rows, tile).then_inc(filled, 16)
                if fills:
                    sp.wait_ge(filled, 16 * len(fills))
                if count:
                    sp.wait_ge(inverse_ready, 1)
                    sp.dma_start(o.inverse.rearrange("(r n) -> r n", r=NB), inverse[:, :]).then_inc(stored, 16)
                    sp.wait_ge(stored, 16)

            @block.tensor
            def _(pe):
                if not count:
                    for i in range(TB):
                        ins = nc.tensor.transpose(w_ps[:, i, :], o.w[:, :].rearrange("p (r i) -> p i r", i=TB)[:, i],
                                                  g.ident[:, :])
                    ins.then_inc(values_ready, 1)
                pe.wait_ge(ends_ready, 1)
                for k, t in ((0, kept[:, 1:2]), (1, run[:, TB * P - 1:TB * P])):
                    ins = nc.tensor.matmul(ends_ps[:, k, 0:NB], t, g.ident[0:NB, 0:NB], start=True, stop=True)
                ins.then_inc(ends_turned, 1)
                pe.wait_ge(carry_ready, 1)
                nc.tensor.matmul(carry_ps[:, 0:1], carry[:, 0:NB], g.ones_f[0:1, 0:1], start=True, stop=True
                                 ).then_inc(carry_turned, 1)
                pe.wait_ge(total_ready, 1)
                for i in range(TB):
                    ins = nc.tensor.transpose(col_ps[:, i * NB:(i + 1) * NB], total[:, i * P:(i + 1) * P],
                                              g.ident[0:NB, 0:NB])
                ins.then_inc(col_ready, 1)

            @block.scalar
            def _(act):
                act.wait_ge(low_ready, 1)
                nc.scalar.activation(root[:, :], low[:, :], ACT.Sqrt).then_inc(root_ready, 1)

            @block.vector
            def _(dve):
                ch = Chain(dve, chain, 0)
                ch.step(0)
                ch.link(nc.vector.memset(carry[:, :], 0.0))
                dve.wait_ge(flags_in, 16)
                if count:
                    values = g.ones_f[0:NB, :]
                else:
                    dve.wait_ge(values_ready, 1)
                    values = w_ps[:, :, :].rearrange("r i p -> r (i p)")
                nc.vector.reduce_sum(kept[:, 0:1], flags[:, :], axis=AX)
                ch.link(nc.vector.tensor_tensor_scan(run[:, :], flags[:, :], values, 0.0, ALU.mult, ALU.add))
                nc.vector.tensor_scalar(kept[:, 1:2], kept[:, 0:1], float(TB * P), None, ALU.is_ge
                                        ).then_inc(ends_ready, 1)
                dve.wait_ge(ends_turned, 1)
                ch.link(nc.vector.tensor_copy(ends[:, :, :], ends_ps[:, :, 0:NB]))
                nc.vector.tensor_tensor_scan(carry[:, 1:NB + 1], ends[:, 0, :], ends[:, 1, :], 0.0, ALU.mult, ALU.add
                                             ).then_inc(carry_ready, 1)
                dve.wait_ge(carry_turned, 1)
                ch.link(nc.vector.tensor_copy(carry_col[:, :], carry_ps[:, 0:1]))
                nc.vector.tensor_tensor_scan(total[:, :], flags[:, :], values, carry_col[:, 0:1], ALU.mult, ALU.add
                                             ).then_inc(total_ready, 1)
                if count:
                    dve.wait_ge(total_ready, 1)
                    nc.vector.reciprocal(inverse[:, :], total[:, :]).then_inc(inverse_ready, 1)
                dve.wait_ge(col_ready, 1)
                ch.link(nc.vector.tensor_copy(col[:, :].rearrange("p (r i) -> p i r", i=TB),
                                              col_ps[:, 0:NT].rearrange("p (i r) -> p i r", i=TB)))
                nc.vector.tensor_scalar(low[:, :], col[:, :], 1.0 if count else 1e-12, None, ALU.max
                                        ).then_inc(low_ready, 1)
                nc.vector.tensor_scalar(some[:, :], col[:, :], 0.0, None, ALU.is_gt)
                dve.wait_ge(root_ready, 1)
                ch.link(nc.vector.reciprocal(inv[:, :], root[:, :]))
                ch.link(nc.vector.tensor_tensor(o.root[:, :], inv[:, :], some[:, :], ALU.mult))


def degree_phase(b, g, o, table, digit, buckets, first_pos, fills):
    nc = b.nc
    with ExitStack() as c:
        put = b.sb("deg_put", [P, 2, TB], I32, c)
        stage = b.sb("deg_stage", [P, 2, TB, 2], F32, c)
        hot = b.sb("deg_hot", [P, 2, TB, buckets], BF16, c)
        counts = b.sb("deg_counts", [P, buckets], F32, c)
        incl = b.sb("deg_incl", [P, buckets], F32, c)
        acc = b.ps("deg_acc", [P, 512], F32, c)
        stage_ready = b.sem("deg_stage_ready", c)
        hot_ready = b.sem("deg_hot_ready", c)
        hot_used = b.sem("deg_hot_used", c)
        chain = b.sem("deg_chain", c)
        filled = [b.sem(f"deg_filled{k}", c) for k in range(2)]
        sent = [b.sem(f"deg_sent{s}", c) for s in range(2)]
        with nc.Block() as block:
            @block.vector
            def _(dve):
                def body(j, first, last):
                    for s in range(2):
                        blk = 2 * j + s
                        at = bass.ds(blk * TB, TB)
                        if not first:
                            dve.wait_ge(sent[s], 16 * TB * j)
                            dve.wait_ge(hot_used, blk - 1)
                        nc.vector.tensor_scalar(put[:, s, :], o.put[:, at], 1.0, None, ALU.mult)
                        nc.vector.tensor_scalar(stage[:, s, :, 0], o.root[:, at], 1.0, None, ALU.mult)
                        nc.vector.tensor_scalar(stage[:, s, :, 1], g.pos[:, at], 1.0, None, ALU.mult
                                                ).then_inc(stage_ready, 1)
                        for i in range(TB):
                            ins = nc.vector.tensor_scalar(hot[:, s, i, :], g.iota16[:, 0:buckets],
                                                          digit[:, bass.ds(blk * TB + i, 1)], None, ALU.is_equal)
                        ins.then_inc(hot_ready, 1)
                turns(dve, body)
                dve.wait_ge(hot_used, NB)
                first_places(nc, dve, g, chain, acc, counts, incl, first_pos, buckets)

            @block.sync
            def _(sp):
                fill_table(sp, g.sp_tick, filled[0], stage_ready, *fills[0])

            @block.scalar
            def _(act):
                fill_table(act, g.act_tick, filled[1], stage_ready, *fills[1])

            @block.tensor
            def _(pe):
                def body(j, first, last):
                    for s in range(2):
                        hold(pe, hot_ready, 2 * j + s + 1, g.pe_tick)
                        for i in range(TB):
                            ins = nc.tensor.matmul(acc[:, 0:buckets], g.ones_b[:, :], hot[:, s, i, :],
                                                   start=first and s == 0 and i == 0,
                                                   stop=last and s == 1 and i == TB - 1, skip_group_check=True)
                        ins.then_inc(hot_used, 1)
                turns(pe, body)

            @block.gpsimd
            def _(pool):
                limit = pool.to_reg(N - 1)

                def body(j, first, last):
                    for s in range(2):
                        hold(pool, stage_ready, 2 * j + s + 1, g.pool_tick)
                        for i in range(TB):
                            nc.gpsimd.indirect_dma_start(
                                table[:, :], bass.IndirectOffsetOnAxis(ap=put[:, s, i:i + 1], axis=0),
                                stage[:, s, i, :], None, bounds_check=limit, oob_is_err=False
                            ).then_inc(sent[s], 16)
                turns(pool, body)
                for s in range(2):
                    pool.wait_ge(sent[s], 16 * TB * TURNS)


def edge_mlp_phase(b, g, o, rows, table):
    nc = b.nc
    with ExitStack() as c:
        attr = b.sb("mlp_attr", [P, 2, TB, A], F32, c)
        flags = b.sb("mlp_flags", [A, 2, TB * P], F32, c)
        inverse = b.sb("mlp_inverse", [A, 2, TB * P], F32, c)
        cut = b.sb("mlp_cut", [A, TB * P], F32, c)
        cat = b.sb("mlp_cat", [3 * A, 2, TB * P], F32, c)
        most = b.sb("mlp_most", [A, 2, TB * P], F32, c)
        hid = b.sb("mlp_hid", [P, 2, TB * P], F32, c)
        stage = b.sb("mlp_stage", [P, 2, TB, D + 1], F32, c)
        put = b.sb("mlp_put", [P, 2, TB], I32, c)
        turned = b.ps("mlp_turned", [A, 2, TB * P], F32, c)
        hidden = b.ps("mlp_hidden", [P, 2, 512], F32, c)
        res = b.ps("mlp_res", [P, 2, 512], F32, c)
        rows_in = [b.sem(f"mlp_rows_in{s}", c) for s in range(2)]
        attr_in = [b.sem(f"mlp_attr_in{s}", c) for s in range(2)]
        turned_ready = b.sem("mlp_turned_ready", c)
        chain = b.sem("mlp_chain", c)
        cat_ready = b.sem("mlp_cat_ready", c)
        hidden_ready = b.sem("mlp_hidden_ready", c)
        hid_ready = b.sem("mlp_hid_ready", c)
        res_ready = b.sem("mlp_res_ready", c)
        stage_ready = b.sem("mlp_stage_ready", c)
        zeroed = b.sem("mlp_zeroed", c)
        sent = [b.sem(f"mlp_sent{s}", c) for s in range(2)]
        with nc.Block() as block:
            @block.sync
            def _(sp):
                def load(blk, s, turn):
                    if had(blk):
                        hold(sp, turned_ready, blk - 1, g.sp_tick)
                    sp.dma_start(attr[:, s, :, :], rows[bass.ds(blk * (TB * P), TB * P), 0:A]
                                 .rearrange("(i p) c -> p i c", p=P)).then_inc(attr_in[s], 16)
                    if had(blk):
                        hold(sp, cat_ready, blk - 1, g.sp_tick)
                    load_row(sp, o.flags, flags, rows_in, blk, s)
                    load_row(sp, o.inverse, inverse, rows_in, blk, s)
                lagged(sp, (0, load))

            @block.tensor
            def _(pe):
                def turn_attr(blk, s, turn):
                    hold(pe, attr_in[s], 16 * (turn + 1), g.pe_tick)
                    if had(blk):
                        hold(pe, cat_ready, blk - 1, g.pe_tick)
                    for i in range(TB):
                        ins = nc.tensor.transpose(turned[:, s, i * P:(i + 1) * P], attr[:, s, i, :], g.ident[:, :])
                    ins.then_inc(turned_ready, 1)

                def first_product(blk, s, turn):
                    hold(pe, cat_ready, blk + 1, g.pe_tick)
                    if had(blk):
                        hold(pe, hid_ready, blk - 1, g.pe_tick)
                    nc.tensor.matmul(hidden[:, s, :], g.w1[:, :], cat[:, s, :], start=True, stop=True
                                     ).then_inc(hidden_ready, 1)

                def second_product(blk, s, turn):
                    hold(pe, hid_ready, blk + 1, g.pe_tick)
                    if had(blk):
                        hold(pe, stage_ready, blk - 1, g.pe_tick)
                    for i in range(TB):
                        ins = nc.tensor.matmul(res[:, s, i * D:(i + 1) * D], hid[:, s, i * P:(i + 1) * P], g.w2[:, :],
                                               start=True, stop=True)
                    ins.then_inc(res_ready, 1)
                lagged(pe, (0, turn_attr), (1, first_product), (2, second_product))

            @block.scalar
            def _(act):
                def relu(blk, s, turn):
                    act.wait_ge(hidden_ready, blk + 1)
                    if had(blk):
                        act.wait_ge(res_ready, blk - 1)
                    nc.scalar.activation(hid[:, s, :], hidden[:, s, :], ACT.Relu, bias=g.hb[:, 0:1]
                                         ).then_inc(hid_ready, 1)
                lagged(act, (0, relu))

            @block.vector
            def _(dve):
                ch = Chain(dve, chain, 2)
                end = slice(TB * P - 1, TB * P)
                for t in (cat, most):
                    nc.vector.memset(t[:, 1, :], 0.0).then_inc(zeroed, 1)
                dve.wait_ge(zeroed, 2)

                def scans(blk, s, turn):
                    ch.step(blk)
                    dve.wait_ge(rows_in[s], 32 * (turn + 1))
                    dve.wait_ge(turned_ready, blk + 1)
                    if had(blk):
                        dve.wait_ge(hidden_ready, blk - 1)
                    if had(blk, 1):
                        dve.wait_ge(cat_ready, blk)
                    ch.link(nc.vector.tensor_scalar(cut[:, :], flags[:, s, :], 1.0, HUGE, ALU.subtract, ALU.mult))
                    nc.vector.tensor_tensor_scan(cat[0:A, s, :], flags[:, s, :], turned[:, s, :],
                                                 cat[0:A, 1 - s, end], ALU.mult, ALU.add)
                    ch.link(nc.vector.tensor_tensor_scan(most[:, s, :], cut[:, :], turned[:, s, :],
                                                         most[:, 1 - s, end], ALU.add, ALU.max))
                    nc.vector.tensor_copy(cat[A:2 * A, s, :], most[:, s, :])
                    nc.vector.tensor_tensor(cat[2 * A:3 * A, s, :], cat[0:A, s, :], inverse[:, s, :], ALU.mult
                                            ).then_inc(cat_ready, 1)

                def finish(blk, s, turn):
                    at = bass.ds(blk * TB, TB)
                    dve.wait_ge(res_ready, blk + 1)
                    if had(blk):
                        dve.wait_ge(sent[s], 16 * TB * turn)
                    nc.vector.tensor_scalar(put[:, s, :], o.put[:, at], 1.0, None, ALU.mult)
                    nc.vector.tensor_scalar(stage[:, s, :, D], o.root[:, at], 1.0, None, ALU.mult)
                    nc.vector.tensor_tensor(stage[:, s, :, 0:D],
                                            res[:, s, 0:TB * D].rearrange("p (i f) -> p i f", f=D),
                                            g.b2[:, :].unsqueeze(1).broadcast_to([P, TB, D]), ALU.add
                                            ).then_inc(stage_ready, 1)
                lagged(dve, (0, scans), (2, finish))

            @block.gpsimd
            def _(pool):
                limit = pool.to_reg(N - 1)

                def scatter(blk, s, turn):
                    hold(pool, stage_ready, blk + 1, g.pool_tick)
                    for i in range(TB):
                        nc.gpsimd.indirect_dma_start(
                            table[:, :], bass.IndirectOffsetOnAxis(ap=put[:, s, i:i + 1], axis=0),
                            stage[:, s, i, :], None, bounds_check=limit, oob_is_err=False
                        ).then_inc(sent[s], 16)
                lagged(pool, (0, scatter))
                for s in range(2):
                    pool.wait_ge(sent[s], 16 * TB * TURNS)


def message_phase(b, g, o, name, table, width, factor_at, weight, out, bias=None, scale_out=False, saved=None):
    nc = b.nc
    with ExitStack() as c:
        got = b.sb(name + "_got", [P, 2, TB, width], F32, c)
        msg = b.sb(name + "_msg", [P, 2, TB, D], F32, c)
        get = b.sb(name + "_get", [P, 2, TB], I32, c)
        put = b.sb(name + "_put", [P, 2, TB], I32, c)
        flags = b.sb(name + "_flags", [D, 2, TB * P], F32, c)
        tot = b.sb(name + "_tot", [D, 2, TB * P], F32, c)
        stage = b.sb(name + "_stage", [P, 2, TB, D], F32, c)
        scaled = b.sb(name + "_scaled", [P, TB, D], F32, c)
        feats = b.sb(name + "_feats", [P, 2, TB, D], F32, c)
        turned = b.ps(name + "_turned", [D, 2, TB * P], F32, c)
        res = b.ps(name + "_res", [P, 2, 512], F32, c)
        flags_in = [b.sem(f"{name}_flags_in{s}", c) for s in range(2)]
        got_in = [b.sem(f"{name}_got_in{s}", c) for s in range(2)]
        sent = [b.sem(f"{name}_sent{s}", c) for s in range(2)]
        kept = [b.sem(f"{name}_kept{s}", c) for s in range(2)]
        get_ready = b.sem(name + "_get_ready", c)
        fac_ready = b.sem(name + "_fac_ready", c)
        feats_ready = b.sem(name + "_feats_ready", c)
        msg_ready = b.sem(name + "_msg_ready", c)
        turned_ready = b.sem(name + "_turned_ready", c)
        scanned = b.sem(name + "_scanned", c)
        res_ready = b.sem(name + "_res_ready", c)
        scaled_ready = b.sem(name + "_scaled_ready", c)
        stage_ready = b.sem(name + "_stage_ready", c)
        zeroed = b.sem(name + "_zeroed", c)
        store = saved is not None
        slot_sent = 16 if store else 16 * TB
        with nc.Block() as block:
            @block.gpsimd
            def _(pool):
                limit = pool.to_reg(N - 1)

                def gather(blk, s, turn):
                    hold(pool, get_ready, blk + 1, g.pool_tick)
                    if had(blk):
                        hold(pool, msg_ready, blk - 1, g.pool_tick)
                        if store:
                            hold(pool, feats_ready, blk - 1, g.pool_tick)
                    for i in range(TB):
                        nc.gpsimd.indirect_dma_start(
                            got[:, s, i, :], None, table[:, :],
                            bass.IndirectOffsetOnAxis(ap=get[:, s, i:i + 1], axis=0),
                            bounds_check=limit, oob_is_err=False).then_inc(got_in[s], 16)

                def scatter(blk, s, turn):
                    hold(pool, stage_ready, blk + 1, g.pool_tick)
                    for i in range(TB):
                        nc.gpsimd.indirect_dma_start(
                            out[:, :], bass.IndirectOffsetOnAxis(ap=put[:, s, i:i + 1], axis=0),
                            stage[:, s, i, :], None, bounds_check=limit, oob_is_err=False
                        ).then_inc(sent[s], 16)
                if store:
                    lagged(pool, (0, gather))
                else:
                    lagged(pool, (0, gather), (4, scatter))
                for s in range(2):
                    pool.wait_ge(got_in[s], 16 * TB * TURNS)
                    if not store:
                        pool.wait_ge(sent[s], slot_sent * TURNS)

            @block.sync
            def _(sp):
                def load(blk, s, turn):
                    if had(blk):
                        hold(sp, scanned, blk - 1, g.sp_tick)
                    load_row(sp, o.flags, flags, flags_in, blk, s)
                lagged(sp, (0, load))

            @block.scalar
            def _(act):
                if not store:
                    return

                def rows_of(dram, blk):
                    return dram[bass.ds(blk * (TB * P), TB * P), :].rearrange("(i p) c -> p i c", p=P)

                def keep(blk, s, turn):
                    act.wait_ge(got_in[s], 16 * TB * (turn + 1))
                    if had(blk):
                        act.wait_ge(kept[s], 16 * turn)
                    nc.scalar.activation(feats[:, s], got[:, s, :, 0:D], ACT.Copy).then_inc(feats_ready, 1)
                    act.wait_ge(feats_ready, blk + 1)
                    act.dma_start(rows_of(saved, blk), feats[:, s]).then_inc(kept[s], 16)

                def keep_sums(blk, s, turn):
                    act.wait_ge(stage_ready, blk + 1)
                    act.dma_start(rows_of(out, blk), stage[:, s]).then_inc(sent[s], 16)
                lagged(act, (0, keep), (2, keep_sums))
                for s in range(2):
                    act.wait_ge(kept[s], 16 * TURNS)
                    act.wait_ge(sent[s], 16 * TURNS)

            @block.tensor
            def _(pe):
                def turn_messages(blk, s, turn):
                    hold(pe, msg_ready, blk + 1, g.pe_tick)
                    if had(blk):
                        hold(pe, scanned, blk - 1, g.pe_tick)
                    for i in range(TB):
                        ins = nc.tensor.transpose(turned[:, s, i * P:(i + 1) * P], msg[:, s, i, :], g.ident[:, :])
                    ins.then_inc(turned_ready, 1)

                def product(blk, s, turn):
                    hold(pe, scanned, blk + 1, g.pe_tick)
                    if had(blk):
                        hold(pe, stage_ready, blk - 1, g.pe_tick)
                    for i in range(TB):
                        to, sums = res[:, s, i * D:(i + 1) * D], tot[:, s, i * P:(i + 1) * P]
                        if weight is None:
                            ins = nc.tensor.transpose(to, sums, g.ident[0:D, 0:D])
                        else:
                            ins = nc.tensor.matmul(to, sums, weight[:, :], start=True, stop=True)
                    ins.then_inc(res_ready, 1)
                lagged(pe, (0, turn_messages), (1, product))

            @block.vector
            def _(dve):
                nc.vector.memset(tot[:, 1, :], 0.0).then_inc(zeroed, 1)
                dve.wait_ge(zeroed, 1)

                def places(blk, s, turn):
                    if had(blk):
                        dve.wait_ge(got_in[s], 16 * TB * turn)
                    nc.vector.tensor_scalar(get[:, s, :], o.get[:, bass.ds(blk * TB, TB)], 1.0, None, ALU.mult
                                            ).then_inc(get_ready, 1)

                def messages(blk, s, turn):
                    at = bass.ds(blk * TB, TB)
                    dve.wait_ge(got_in[s], 16 * TB * (turn + 1))
                    if had(blk):
                        dve.wait_ge(turned_ready, blk - 1)
                    if store:
                        nc.vector.tensor_scalar(o.end_root[:, at], got[:, s, :, D], 1.0, None, ALU.mult)
                        nc.vector.tensor_scalar(o.end_last[:, at], got[:, s, :, D + 1], 1.0, None, ALU.mult)
                    if factor_at is None:
                        factor = o.w[:, at]
                    else:
                        nc.vector.tensor_tensor(o.factor[:, at], got[:, s, :, factor_at], o.w[:, at], ALU.mult
                                                ).then_inc(fac_ready, 1)
                        dve.wait_ge(fac_ready, blk + 1)
                        factor = o.factor[:, at]
                    nc.vector.tensor_tensor(msg[:, s], got[:, s, :, 0:D], factor.unsqueeze(2).broadcast_to([P, TB, D]),
                                            ALU.mult).then_inc(msg_ready, 1)

                def scan(blk, s, turn):
                    dve.wait_ge(flags_in[s], 16 * (turn + 1))
                    dve.wait_ge(turned_ready, blk + 1)
                    if had(blk):
                        dve.wait_ge(res_ready, blk - 1)
                    if had(blk, 1):
                        dve.wait_ge(scanned, blk)
                    nc.vector.tensor_tensor_scan(tot[:, s, :], flags[:, s, :], turned[:, s, :],
                                                 tot[:, 1 - s, TB * P - 1:TB * P], ALU.mult, ALU.add
                                                 ).then_inc(scanned, 1)

                def finish(blk, s, turn):
                    at = bass.ds(blk * TB, TB)
                    dve.wait_ge(res_ready, blk + 1)
                    if had(blk):
                        dve.wait_ge(sent[s], slot_sent * turn)
                    if not store:
                        nc.vector.tensor_scalar(put[:, s, :], o.put[:, at], 1.0, None, ALU.mult)
                    r = res[:, s, 0:TB * D].rearrange("p (i f) -> p i f", f=D)
                    if scale_out:
                        if had(blk, 1):
                            dve.wait_ge(stage_ready, blk)
                        nc.vector.tensor_tensor(scaled[:, :, :], r, o.root[:, at].unsqueeze(2)
                                                .broadcast_to([P, TB, D]), ALU.mult).then_inc(scaled_ready, 1)
                        dve.wait_ge(scaled_ready, blk + 1)
                        r = scaled[:, :, :]
                    if bias is None:
                        nc.vector.tensor_copy(stage[:, s], r).then_inc(stage_ready, 1)
                    else:
                        nc.vector.tensor_tensor(stage[:, s], r, bias[:, :].unsqueeze(1).broadcast_to([P, TB, D]),
                                                ALU.add).then_inc(stage_ready, 1)
                lagged(dve, (0, places), (2, messages), (3, scan), (4, finish))


def conv_phase(b, g, o, rows, table, out):
    nc = b.nc
    W2 = 2 * D
    with ExitStack() as c:
        pair = b.sb("conv_pair", [P, 2, TB, W2], F32, c)
        get = b.sb("conv_get", [P, 2, TB], I32, c)
        put = b.sb("conv_put", [P, 2, TB], I32, c)
        lhs = b.sb("conv_lhs", [P, 2, TB * P], F32, c)
        hid = b.sb("conv_hid", [P, TB, W2], F32, c)
        msg = b.sb("conv_msg", [P, 2, TB, W2], F32, c)
        flags = b.sb("conv_flags", [P, 2, TB * P], F32, c)
        tot = b.sb("conv_tot", [P, 2, TB * P], F32, c)
        stage = b.sb("conv_stage", [P, 2, TB, W2], F32, c)
        scaled = b.sb("conv_scaled", [P, TB, W2], F32, c)
        pt = b.ps("conv_pt", [P, 2, 512], F32, c)
        pre = b.ps("conv_pre", [P, 2, 512], F32, c)
        turned = b.ps("conv_turned", [P, 2, 512], F32, c)
        res = b.ps("conv_res", [P, 2, 512], F32, c)
        flags_in = [b.sem(f"conv_flags_in{s}", c) for s in range(2)]
        x_in = [b.sem(f"conv_x_in{s}", c) for s in range(2)]
        got_in = [b.sem(f"conv_got_in{s}", c) for s in range(2)]
        sent = [b.sem(f"conv_sent{s}", c) for s in range(2)]
        get_ready = b.sem("conv_get_ready", c)
        pair_ready = b.sem("conv_pair_ready", c)
        pt_ready = b.sem("conv_pt_ready", c)
        lhs_ready = b.sem("conv_lhs_ready", c)
        pre_ready = b.sem("conv_pre_ready", c)
        hid_ready = b.sem("conv_hid_ready", c)
        msg_ready = b.sem("conv_msg_ready", c)
        turned_ready = b.sem("conv_turned_ready", c)
        scanned = b.sem("conv_scanned", c)
        res_ready = b.sem("conv_res_ready", c)
        scaled_ready = b.sem("conv_scaled_ready", c)
        stage_ready = b.sem("conv_stage_ready", c)
        zeroed = b.sem("conv_zeroed", c)
        with nc.Block() as block:
            @block.gpsimd
            def _(pool):
                limit_edges = pool.to_reg(EP)
                limit_nodes = pool.to_reg(N - 1)

                def gather(blk, s, turn):
                    hold(pool, get_ready, blk + 1, g.pool_tick)
                    if had(blk):
                        hold(pool, pt_ready, blk - 1, g.pool_tick)
                    for i in range(TB):
                        nc.gpsimd.indirect_dma_start(
                            pair[:, s, i, 0:D], None, table[:, :],
                            bass.IndirectOffsetOnAxis(ap=get[:, s, i:i + 1], axis=0),
                            bounds_check=limit_edges, oob_is_err=False).then_inc(got_in[s], 16)

                def scatter(blk, s, turn):
                    hold(pool, stage_ready, blk + 1, g.pool_tick)
                    for i in range(TB):
                        nc.gpsimd.indirect_dma_start(
                            out[:, :], bass.IndirectOffsetOnAxis(ap=put[:, s, i:i + 1], axis=0),
                            stage[:, s, i, :], None, bounds_check=limit_nodes, oob_is_err=False
                        ).then_inc(sent[s], 16)
                lagged(pool, (0, gather), (4, scatter))
                for s in range(2):
                    pool.wait_ge(got_in[s], 16 * TB * TURNS)
                    pool.wait_ge(sent[s], 16 * TB * TURNS)

            @block.sync
            def _(sp):
                def load(blk, s, turn):
                    if had(blk):
                        hold(sp, pt_ready, blk - 1, g.sp_tick)
                    sp.dma_start(pair[:, s, :, D:W2], rows[bass.ds(blk * (TB * P), TB * P), :]
                                 .rearrange("(i p) c -> p i c", p=P)).then_inc(x_in[s], 16)

                def load_flags(blk, s, turn):
                    if had(blk):
                        hold(sp, scanned, blk - 1, g.sp_tick)
                    load_row(sp, o.flags, flags, flags_in, blk, s)
                lagged(sp, (0, load), (1, load_flags))

            @block.scalar
            def _(act):
                def copy(blk, s, turn):
                    act.wait_ge(pt_ready, blk + 1)
                    if had(blk):
                        act.wait_ge(pre_ready, blk - 1)
                    nc.scalar.activation(lhs[:, s, :], pt[:, s, :], ACT.Copy).then_inc(lhs_ready, 1)
                lagged(act, (0, copy))

            @block.tensor
            def _(pe):
                def turn_pair(blk, s, turn):
                    hold(pe, pair_ready, blk + 1, g.pe_tick)
                    hold(pe, x_in[s], 16 * (turn + 1), g.pe_tick)
                    if had(blk):
                        hold(pe, lhs_ready, blk - 1, g.pe_tick)
                    for i in range(TB):
                        ins = nc.tensor.transpose(pt[:, s, i * P:(i + 1) * P], pair[:, s, i, :], g.ident[:, :])
                    ins.then_inc(pt_ready, 1)

                def first_product(blk, s, turn):
                    hold(pe, lhs_ready, blk + 1, g.pe_tick)
                    if had(blk):
                        hold(pe, hid_ready, blk - 1, g.pe_tick)
                    for i in range(TB):
                        ins = nc.tensor.matmul(pre[:, s, i * P:(i + 1) * P], lhs[:, s, i * P:(i + 1) * P],
                                               g.conv0[:, :], start=True, stop=True)
                    ins.then_inc(pre_ready, 1)

                def turn_messages(blk, s, turn):
                    hold(pe, msg_ready, blk + 1, g.pe_tick)
                    if had(blk):
                        hold(pe, scanned, blk - 1, g.pe_tick)
                    for i in range(TB):
                        ins = nc.tensor.transpose(turned[:, s, i * P:(i + 1) * P], msg[:, s, i, :], g.ident[:, :])
                    ins.then_inc(turned_ready, 1)

                def second_product(blk, s, turn):
                    hold(pe, scanned, blk + 1, g.pe_tick)
                    if had(blk):
                        hold(pe, stage_ready, blk - 1, g.pe_tick)
                    for i in range(TB):
                        ins = nc.tensor.matmul(res[:, s, i * P:(i + 1) * P], tot[:, s, i * P:(i + 1) * P],
                                               g.conv1[:, :], start=True, stop=True)
                    ins.then_inc(res_ready, 1)
                lagged(pe, (1, first_product), (3, second_product), (2, turn_messages), (0, turn_pair))

            @block.vector
            def _(dve):
                nc.vector.memset(tot[:, 1, :], 0.0).then_inc(zeroed, 1)
                dve.wait_ge(zeroed, 1)

                def places(blk, s, turn):
                    if had(blk):
                        dve.wait_ge(got_in[s], 16 * TB * turn)
                    nc.vector.tensor_scalar(get[:, s, :], o.end_last[:, bass.ds(blk * TB, TB)], 1.0, None, ALU.mult
                                            ).then_inc(get_ready, 1)

                def scale(blk, s, turn):
                    dve.wait_ge(got_in[s], 16 * TB * (turn + 1))
                    nc.vector.tensor_tensor(pair[:, s, :, 0:D], pair[:, s, :, 0:D],
                                            o.end_root[:, bass.ds(blk * TB, TB)].unsqueeze(2)
                                            .broadcast_to([P, TB, D]), ALU.mult).then_inc(pair_ready, 1)

                def messages(blk, s, turn):
                    dve.wait_ge(pre_ready, blk + 1)
                    if had(blk, 1):
                        dve.wait_ge(msg_ready, blk)
                    nc.vector.tensor_tensor(hid[:, :, :], pre[:, s, :].rearrange("p (i f) -> p i f", f=W2),
                                            g.conv_b[:, :].unsqueeze(1).broadcast_to([P, TB, W2]), ALU.add
                                            ).then_inc(hid_ready, 1)
                    dve.wait_ge(hid_ready, blk + 1)
                    if had(blk):
                        dve.wait_ge(turned_ready, blk - 1)
                    nc.vector.scalar_tensor_tensor(msg[:, s], hid[:, :, :], 0.0,
                                                   o.factor[:, bass.ds(blk * TB, TB)].unsqueeze(2)
                                                   .broadcast_to([P, TB, W2]), ALU.max, ALU.mult
                                                   ).then_inc(msg_ready, 1)

                def scan(blk, s, turn):
                    dve.wait_ge(flags_in[s], 16 * (turn + 1))
                    dve.wait_ge(turned_ready, blk + 1)
                    if had(blk):
                        dve.wait_ge(res_ready, blk - 1)
                    if had(blk, 1):
                        dve.wait_ge(scanned, blk)
                    nc.vector.tensor_tensor_scan(tot[:, s, :], flags[:, s, :], turned[:, s, :],
                                                 tot[:, 1 - s, TB * P - 1:TB * P], ALU.mult, ALU.add
                                                 ).then_inc(scanned, 1)

                def finish(blk, s, turn):
                    at = bass.ds(blk * TB, TB)
                    dve.wait_ge(res_ready, blk + 1)
                    if had(blk):
                        dve.wait_ge(sent[s], 16 * TB * turn)
                    nc.vector.tensor_scalar(put[:, s, :], o.put[:, at], 1.0, None, ALU.mult)
                    if had(blk, 1):
                        dve.wait_ge(stage_ready, blk)
                    nc.vector.tensor_tensor(scaled[:, :, :], res[:, s, :].rearrange("p (i f) -> p i f", f=W2),
                                            o.root[:, at].unsqueeze(2).broadcast_to([P, TB, W2]), ALU.mult
                                            ).then_inc(scaled_ready, 1)
                    dve.wait_ge(scaled_ready, blk + 1)
                    nc.vector.tensor_tensor(stage[:, s], scaled[:, :, :], g.root1_b[:, :].unsqueeze(1)
                                            .broadcast_to([P, TB, W2]), ALU.add).then_inc(stage_ready, 1)
                lagged(dve, (0, places), (1, scale), (2, messages), (3, scan), (4, finish))


def node_rows(table, k, tail):
    if tail:
        return table[P * PER:N, :].rearrange("(p n) f -> p n f", n=TAIL_ITEMS)
    return table[0:P * PER, :].rearrange("(p n) f -> p n f", p=P)[:, bass.ds(k * ITEMS, ITEMS), :]


def arrived(k, s):
    return (k - s) * (16 // RING) + 16


def chunks(eng, *stages):
    def step(at, slot_of, lowest, highest):
        for n, stage in enumerate(stages):
            if stage is not None and lowest <= n <= highest:
                stage(at(n), slot_of(n), False)
    for k in range(2 * RING):
        step(lambda n: k - n, lambda n: (k - n) % RING, 0, k)
    with eng.Fori(2, CHUNKS // RING) as h:
        for k in range(RING):
            step(lambda n: h * RING + (k - n), lambda n: (k - n) % RING, 0, len(stages))
    for k in range(CHUNKS, CHUNKS + len(stages)):
        for n, stage in enumerate(stages):
            if stage is not None and k - n <= CHUNKS:
                stage(k - n, (k - n) % RING, k - n == CHUNKS)


def old(k, lag=None):
    return not isinstance(k, int) or k >= (RING if lag is None else lag)


def dense_phase(b, g, name, x, msgs, out, extra=None, aux=(), root=False):
    nc = b.nc
    wx, wm, wo = x.shape[1], msgs.shape[1], out.shape[1]
    we = extra.shape[1] if extra is not None else 1
    pairs = (ITEMS + 1) // 2
    keep = ()
    if root:
        keep = [(0, which, place, w) for _, which, place, w in aux]
        aux = [(at, "e", 0, w) for at, _, _, w in aux]
        assert len(aux) == 1
    with ExitStack() as c:
        xs = b.sb(name + "_x", [P, RING, ITEMS, wx], F32, c)
        ms = b.sb(name + "_m", [P, RING, ITEMS, wm], F32, c)
        es = b.sb(name + "_e", [P, RING, ITEMS, we], F32, c)
        pre = b.sb(name + "_pre", [P, RING, ITEMS, D], F32, c)
        cen = b.sb(name + "_cen", [P, RING, ITEMS, D], F32, c)
        sq = b.sb(name + "_sq", [P, RING, ITEMS, D], F32, c)
        row = b.sb(name + "_row", [P, RING, ITEMS, wo], F32, c)
        stat = b.sb(name + "_stat", [P, 4, RING, ITEMS], F32, c)
        total, total2, dev, inv = (stat[:, k] for k in range(4))
        x_in = [b.sem(f"{name}_x_in{s}", c) for s in range(RING)]
        m_in = [b.sem(f"{name}_m_in{s}", c) for s in range(RING)]
        e_in = [b.sem(f"{name}_e_in{s}", c) for s in range(RING)]
        pre_ready = b.sem(name + "_pre_ready", c)
        total_ready = b.sem(name + "_total_ready", c)
        cen_ready = b.sem(name + "_cen_ready", c)
        sq_ready = b.sem(name + "_sq_ready", c)
        total2_ready = b.sem(name + "_total2_ready", c)
        dev_ready = b.sem(name + "_dev_ready", c)
        inv_ready = b.sem(name + "_inv_ready", c)
        aux_ready = b.sem(name + "_aux_ready", c)
        row_ready = b.sem(name + "_row_ready", c)
        stored = [b.sem(f"{name}_stored{s}", c) for s in range(RING)]
        if root:
            packed = b.sb(name + "_packed", [P, RING, ITEMS * D], F32, c)
            packed_ready = b.sem(name + "_packed_ready", c)
            xt = b.sb(name + "_xt", [P, 2, pairs * P], F32, c)
            z = b.sb(name + "_z", [P, 2, ITEMS, 2 * D], F32, c)
            xt_ps = b.ps(name + "_xt_ps", [P, 2, 1024], F32, c)
            root_ps = b.ps(name + "_root_ps", [P, 4 * 512], F32, c)
            xt_ps_ready = b.sem(name + "_xt_ps_ready", c)
            xt_ready = b.sem(name + "_xt_ready", c)
            root_ready = b.sem(name + "_root_ready", c)
            z_ready = b.sem(name + "_z_ready", c)
            act_ready = b.sem(name + "_act_ready", c)
            both_ready = b.sem(name + "_both_ready", c)

        def sizes(tail):
            return (TAIL_P, TAIL_ITEMS) if tail else (P, ITEMS)

        def halves(n):
            return [(0, 8), (8, n)] if n > 8 else [(0, n)]

        def spans(p, n):
            whole = n // 2
            yield 0, whole * p, P
            if n % 2:
                yield whole * p, (whole + 1) * p, D

        with nc.Block() as block:
            @block.sync
            def _(sp):
                def load(k, s, tail):
                    p, n = sizes(tail)
                    if old(k):
                        if root:
                            hold(sp, packed_ready, k - RING + 1, g.sp_tick)
                            hold(sp, z_ready, 2 * (k - RING + 1), g.sp_tick)
                        else:
                            hold(sp, pre_ready, k - RING + 1, g.sp_tick)
                            if aux:
                                hold(sp, aux_ready, k - RING + 1, g.sp_tick)
                    sp.dma_start(xs[0:p, s, 0:n, :], node_rows(x, k, tail)).then_inc(x_in[s], 16)
                    sp.dma_start(ms[0:p, s, 0:n, :], node_rows(msgs, k, tail)).then_inc(m_in[s], 16)
                    if extra is not None:
                        sp.dma_start(es[0:p, s, 0:n, :], node_rows(extra, k, tail)).then_inc(e_in[s], 16)

                chunks(sp, load)

            @block.gpsimd
            def _(pool):
                def sums(k, s, tail):
                    p, n = sizes(tail)
                    if root:
                        hold(pool, act_ready, k + 1, g.pool_tick)
                        hold(pool, packed_ready, k + 1, g.pool_tick)
                        a, m = z[0:p, s % 2, 0:n, 0:D], z[0:p, s % 2, 0:n, D:2 * D]
                    else:
                        hold(pool, x_in[s], arrived(k, s), g.pool_tick)
                        hold(pool, m_in[s], arrived(k, s), g.pool_tick)
                        a, m = xs[0:p, s, 0:n, 0:D], ms[0:p, s, 0:n, 0:D]
                    if old(k):
                        hold(pool, cen_ready, k - RING + 1, g.pool_tick)
                    made = pre[0:p, s, 0:n]
                    ins = nc.gpsimd.tensor_tensor(made, a, m, ALU.add)
                    if root:
                        ins.then_inc(both_ready, 1)
                        hold(pool, both_ready, k + 1, g.pool_tick)
                        ins = nc.gpsimd.tensor_tensor(made, made, packed[0:p, s, 0:n * D]
                                                      .rearrange("p (n f) -> p n f", f=D), ALU.add)
                    ins.then_inc(pre_ready, 1)

                def rows(k, s, tail):
                    p, n = sizes(tail)
                    hold(pool, inv_ready, k + 1, g.pool_tick)
                    if old(k):
                        hold(pool, stored[s], arrived(k, s) - 16, g.pool_tick)
                    nc.gpsimd.tensor_tensor(row[0:p, s, 0:n, 0:D], cen[0:p, s, 0:n],
                                            inv[0:p, s, 0:n].unsqueeze(2).broadcast_to([p, n, D]), ALU.mult
                                            ).then_inc(row_ready, 1)
                chunks(pool, sums, None, None, rows)

            @block.vector
            def _(dve):
                def root_sum(k, s, tail):
                    p, n = sizes(tail)
                    t = s % 2
                    dve.wait_ge(m_in[s], arrived(k, s))
                    if old(k, 2):
                        dve.wait_ge(pre_ready, k - 1)
                    for h, (a, e) in enumerate(halves(n)):
                        dve.wait_ge(root_ready, 2 * k + h + 1)
                        nc.vector.tensor_tensor(z[0:p, t, a:e], root_ps[0:p, a * 2 * D:e * 2 * D]
                                                .rearrange("p (n f) -> p n f", f=2 * D), ms[0:p, s, a:e], ALU.add
                                                ).then_inc(z_ready, 1)

                def center(k, s, tail):
                    p, n = sizes(tail)
                    dve.wait_ge(pre_ready, k + 1)
                    nc.vector.reduce_sum(total[0:p, s, 0:n], pre[0:p, s, 0:n], axis=AX).then_inc(total_ready, 1)
                    dve.wait_ge(total_ready, k + 1)
                    if old(k):
                        dve.wait_ge(row_ready, k - RING + 1)
                        dve.wait_ge(sq_ready, k - RING + 1)
                    nc.vector.scalar_tensor_tensor(cen[0:p, s, 0:n],
                                                   total[0:p, s, 0:n].unsqueeze(2).broadcast_to([p, n, D]),
                                                   -1.0 / D, pre[0:p, s, 0:n], ALU.mult, ALU.add
                                                   ).then_inc(cen_ready, 1)

                def variance(k, s, tail):
                    p, n = sizes(tail)
                    dve.wait_ge(sq_ready, k + 1)
                    if old(k):
                        dve.wait_ge(dev_ready, k - RING + 1)
                    nc.vector.reduce_sum(total2[0:p, s, 0:n], sq[0:p, s, 0:n], axis=AX).then_inc(total2_ready, 1)

                def inverse(k, s, tail):
                    p, n = sizes(tail)
                    dve.wait_ge(dev_ready, k + 1)
                    if old(k):
                        dve.wait_ge(row_ready, k - RING + 1)
                    nc.vector.reciprocal(inv[0:p, s, 0:n], dev[0:p, s, 0:n]).then_inc(inv_ready, 1)
                if root:
                    chunks(dve, root_sum, center, variance, inverse)
                else:
                    chunks(dve, center, variance, inverse)

            @block.scalar
            def _(act):
                def store(k, s, tail):
                    p, n = sizes(tail)
                    act.wait_ge(row_ready, k + 1)
                    if aux:
                        act.wait_ge(aux_ready, k + 1)
                    act.dma_start(node_rows(out, k, tail), row[0:p, s, 0:n, :]).then_inc(stored[s], 16)

                def turned_rows(k, s, tail):
                    p, n = sizes(tail)
                    t = s % 2
                    act.wait_ge(xt_ps_ready, k + 1)
                    if old(k, 2):
                        act.wait_ge(root_ready, 2 * (k - 1))
                    for lo, hi, rows in spans(p, n):
                        ins = nc.scalar.activation(xt[0:rows, t, lo:hi], xt_ps[0:rows, t, lo:hi], ACT.Copy)
                    ins.then_inc(xt_ready, 1)

                def pack(k, s, tail):
                    p, n = sizes(tail)
                    act.wait_ge(x_in[s], arrived(k, s))
                    if old(k):
                        act.wait_ge(xt_ps_ready, k - RING + 1)
                        act.wait_ge(pre_ready, k - RING + 1)
                        act.wait_ge(aux_ready, k - RING + 1)
                    for at, which, place, w in keep:
                        nc.scalar.activation(es[0:p, s, 0:n, at:at + w], xs[0:p, s, 0:n, place:place + w], ACT.Copy)
                    nc.scalar.activation(packed[0:p, s, 0:n * D].rearrange("p (n f) -> p n f", f=D),
                                         xs[0:p, s, 0:n, 0:D], ACT.Copy).then_inc(packed_ready, 1)

                def relu(k, s, tail):
                    p, n = sizes(tail)
                    act.wait_ge(z_ready, 2 * k + len(halves(n)))
                    nc.scalar.activation(z[0:p, s % 2, 0:n], z[0:p, s % 2, 0:n], ACT.Relu, scale=0.5
                                         ).then_inc(act_ready, 1)

                def square(k, s, tail):
                    p, n = sizes(tail)
                    act.wait_ge(cen_ready, k + 1)
                    if old(k):
                        act.wait_ge(total2_ready, k - RING + 1)
                    nc.scalar.activation(sq[0:p, s, 0:n], cen[0:p, s, 0:n], ACT.Square).then_inc(sq_ready, 1)
                    if aux:
                        if old(k):
                            act.wait_ge(stored[s], arrived(k, s) - 16)
                        if root:
                            act.wait_ge(packed_ready, k + 1)
                        else:
                            act.wait_ge(x_in[s], arrived(k, s))
                            act.wait_ge(m_in[s], arrived(k, s))
                        if extra is not None:
                            act.wait_ge(e_in[s], arrived(k, s))
                        for at, which, place, w in aux:
                            ins = nc.scalar.activation(row[0:p, s, 0:n, at:at + w],
                                                       {"x": xs, "m": ms, "e": es}[which][0:p, s, 0:n, place:place + w],
                                                       ACT.Copy)
                        ins.then_inc(aux_ready, 1)

                def deviation(k, s, tail):
                    p, n = sizes(tail)
                    act.wait_ge(total2_ready, k + 1)
                    if old(k):
                        act.wait_ge(inv_ready, k - RING + 1)
                    nc.scalar.activation(dev[0:p, s, 0:n], total2[0:p, s, 0:n], ACT.Sqrt, bias=g.eps[0:p, 0:1],
                                         scale=1.0 / D).then_inc(dev_ready, 1)
                if root:
                    chunks(act, pack, turned_rows, relu, square, deviation, None, store)
                else:
                    chunks(act, square, deviation, None, store)
                for s in range(RING):
                    act.wait_ge(stored[s], 16 * (CHUNKS // RING + (s == CHUNKS % RING)))

            if root:
                @block.tensor
                def _(pe):
                    def turn(k, s, tail):
                        p, n = sizes(tail)
                        hold(pe, packed_ready, k + 1, g.pe_tick)
                        if old(k, 2):
                            hold(pe, xt_ready, k - 1, g.pe_tick)
                        for i in range(0, n, 2):
                            m = min(2, n - i)
                            ins = nc.tensor.transpose(xt_ps[0:m * D, s % 2, i // 2 * p:(i // 2 + 1) * p],
                                                      packed[0:p, s, i * D:(i + m) * D], g.ident[0:p, 0:p])
                        ins.then_inc(xt_ps_ready, 1)

                    def product(k, s, tail):
                        p, n = sizes(tail)
                        hold(pe, xt_ready, k + 1, g.pe_tick)
                        for h, (a, e) in enumerate(halves(n)):
                            if old(k, 1):
                                hold(pe, z_ready, 2 * k - 1 + h, g.pe_tick)
                            for i in range(a, e, 2):
                                m = min(2, e - i)
                                ins = nc.tensor.matmul(root_ps[0:p, i * 2 * D:(i + m) * 2 * D],
                                                       xt[0:m * D, s % 2, i // 2 * p:(i // 2 + 1) * p],
                                                       g.root1[0:m * D, 0:m * 2 * D], start=True, stop=True)
                            ins.then_inc(root_ready, 1)

                    chunks(pe, turn, product)


class Globals:
    pass


class Order:

    def __init__(self, b, name):
        self.name = name
        self.put = b.sb(name + "_put_table", [P, NT], F32)
        self.get = b.sb(name + "_get_table", [P, NT], F32)
        self.w = b.sb(name + "_w_table", [P, NT], F32)
        self.root = b.sb(name + "_root_table", [P, NT], F32)
        self.factor = b.sb(name + "_factor_table", [P, NT], F32)
        self.flags = b.dram(name + "_flags_dram", [EP])
        self.inverse = b.dram(name + "_inverse_dram", [EP])


def fill_table(eng, tick, done, pace, table, tile, behind=0):
    with eng.Fori(0, CHUNKS) as k:
        hold(eng, pace, k + (behind + 1), tick)
        eng.dma_start(node_rows(table, k, False), tile).then_inc(done, 16)
    eng.dma_start(node_rows(table, CHUNKS, True), tile[0:TAIL_P, 0:TAIL_ITEMS, :]).then_inc(done, 16)
    eng.wait_ge(done, 16 * (CHUNKS + 1))


def build(nc, x, src, dst, attr, w, u, W1, b1, W2, b2, init, weight, root, bias, l2W, l2b, l3W, l3b, out):
    with ExitStack() as ctx:
        b = Build(nc, ctx)
        g = Globals()
        g.pool_tick = b.sem("pool_tick")
        g.pe_tick = b.sem("pe_tick")
        g.sp_tick = b.sem("sp_tick")
        g.act_tick = b.sem("act_tick")
        g.unsorted = b.sb("unsorted", [1, 2], I32)
        g.ident = b.sb("ident", [P, P], F32)
        g.down = b.sb("down", [P, P], F32)
        g.around = b.sb("around", [P, P], F32)
        g.before = b.sb("before", [P, P], BF16)
        g.since = b.sb("since", [P, P], BF16)
        g.ones_b = b.sb("ones_b", [P, P], BF16)
        g.ones_f = b.sb("ones_f", [P, TB * P], F32)
        g.iota16 = b.sb("iota16", [P, NT], F16)
        g.pos = b.sb("pos", [P, NT], F32)
        g.src = b.sb("src_table", [P, NT], F32)
        g.dst = b.sb("dst_table", [P, NT], F32)
        g.w = b.sb("w_table", [P, NT], F32)
        g.lo = [b.sb(f"lo{k}", [P, NT], F32) for k in range(2)]
        g.hi = [b.sb(f"hi{k}", [P, NT], F32) for k in range(2)]
        g.first = [b.sb(f"first{k}", [P, HI], F32) for k in range(4)]
        g.w1 = b.sb("w1", [3 * A, HID], F32)
        g.w1u = b.sb("w1u", [1, HID], F32)
        g.uval = b.sb("uval", [1, 1], F32)
        g.w2 = b.sb("w2", [HID, D], F32)
        g.b1 = b.sb("b1", [HID, 1], F32)
        g.hb = b.sb("hb", [HID, 1], F32)
        g.b2 = b.sb("b2", [P, D], F32)
        g.conv0 = b.sb("conv0", [2 * D, 2 * D], F32)
        g.conv1 = b.sb("conv1", [2 * D, 2 * D], F32)
        g.conv_b = b.sb("conv_b", [P, 2 * D], F32)
        g.root1 = b.sb("root1", [2 * D, 4 * D], F32)
        g.root1_b = b.sb("root1_b", [P, 2 * D], F32)
        g.l2w = b.sb("l2w", [D, D], F32)
        g.l2b = b.sb("l2b", [P, D], F32)
        g.l3w = b.sb("l3w", [D, D], F32)
        g.l3b = b.sb("l3b", [P, D], F32)
        g.base = b.sb("base", [1, D], F32)
        g.base_all = b.sb("base_all", [P, D], F32)
        g.fill_m = b.sb("fill_m", [P, ITEMS, D + 1], F32)
        g.fill_nd = b.sb("fill_nd", [ND_P, N // ND_P, 2], F32)
        g.fill_1 = b.sb("fill_1", [P, ITEMS, 2 * D], F32)
        g.eps = b.sb("eps", [P, 1], F32)
        g.zero_row = b.sb("zero_row", [1, D], F32)
        g.fill_2 = b.sb("fill_2", [P, ITEMS, D], F32)
        g.fill_3 = b.sb("fill_3", [P, ITEMS, D], F32)
        order_d, order_s = Order(b, "D"), Order(b, "S")
        order_d.end_root = b.sb("end_root_table", [P, NT], F32)
        order_d.end_last = b.sb("end_last_table", [P, NT], F32)

        s_half = b.dram("s_half", [EP, SROW])
        s_rows = b.dram("s_rows", [EP, SROW])
        d_half = b.dram("d_half", [EP, DROW])
        d_rows = b.dram("d_rows", [EP, DROW])
        m0 = b.dram("m0", [N, D + 1])
        nd = b.dram("nd", [N, 2])
        x1 = b.dram("x1", [N, R1])
        x1_edges = b.dram("x1_edges", [EP, D])
        sums1 = b.dram("sums1", [EP + 1, D])
        m1 = b.dram("m1", [N, 2 * D])
        x2 = b.dram("x2", [N, R2])
        m2 = b.dram("m2", [N, D])
        x3 = b.dram("x3", [N, R2])
        m3 = b.dram("m3", [N, D])

        setup_phase(b, g, src, dst, w, {
            "W1": W1, "u0": u[0:1, :], "W2": W2, "b1": b1, "b2": b2, "init": init, "weight": weight, "root": root,
            "bias0": bias[0:1], "bias1": bias[1:2], "l2W": l2W, "l2b": l2b, "l3W": l3W, "l3b": l3b})
        b.clear()
        unsorted = g.unsorted[0:1, 0:1]
        hist_phase(b, g, "d0", g.lo[1], LO, g.first[2], flag=unsorted)
        b.clear()
        radix_phase(b, g, "d1", None, 0, [(0, g.src), (1, g.dst), (2, g.w), (3, g.hi[1])], DROW,
                    g.lo[1], LO, g.first[2], d_half, then=(g.hi[1], HI, g.first[3]), flag=unsorted)
        b.clear()
        radix_phase(b, g, "d2", d_half, DROW, [], DROW, None, HI, g.first[3], d_rows, flag=unsorted)
        b.clear()
        tables_phase(b, g, order_d, d_rows, 0, kept=(g.src, g.dst, g.w))
        b.clear()
        totals_phase(b, g, order_d, False, fills=(
            (nd.rearrange("(p n) c -> p n c", p=ND_P), g.fill_nd[:, :, :]), (sums1[EP:EP + 1, :], g.zero_row[:, :])))
        b.clear()
        degree_phase(b, g, order_d, nd, g.lo[0], LO, g.first[0],
                     fills=((m0, g.fill_m[:, :, :]), (m3, g.fill_3[:, :, :])))
        b.clear()

        radix_phase(b, g, "s1", attr, A, [(A, g.src), (A + 1, g.dst), (A + 2, g.w), (A + 3, g.hi[0])], SROW,
                    g.lo[0], LO, g.first[0], s_half, fill=(m1, g.fill_1[:, :, :]), then=(g.hi[0], HI, g.first[1]))
        b.clear()
        radix_phase(b, g, "s2", s_half, SROW, [], SROW, None, HI, g.first[1], s_rows, fill=(m2, g.fill_2[:, :, :]))
        b.clear()
        tables_phase(b, g, order_s, s_rows, A)
        b.clear()
        totals_phase(b, g, order_s, True)
        b.clear()
        edge_mlp_phase(b, g, order_s, s_rows, m0)
        b.clear()
        dense_phase(b, g, "l0", x, m0, x1, extra=nd, aux=((D, "e", 0, 2), (D + 2, "m", D, 1)))
        b.clear()
        message_phase(b, g, order_d, "p1", x1, R1, D, None, sums1, saved=x1_edges)
        b.clear()
        conv_phase(b, g, order_d, x1_edges, sums1, m1)
        b.clear()
        dense_phase(b, g, "l1", x1, m1, x2, aux=((D, "x", D + 2, 1),), root=True)
        b.clear()
        message_phase(b, g, order_s, "p3", x2, R2, None, g.l2w, m2, bias=g.l2b)
        b.clear()
        dense_phase(b, g, "l2", x2, m2, x3, aux=((D, "x", D, 1),))
        b.clear()
        message_phase(b, g, order_s, "p4", x3, R2, D, g.l3w, m3, bias=g.l3b, scale_out=True)
        b.clear()
        dense_phase(b, g, "l3", x3, m3, out)
        b.clear()


_INS = ["x", "src", "dst", "edge_attr_32", "edge_weight", "L0_gnn_u", "L0_gnn_W1", "L0_gnn_b1", "L0_gnn_W2",
        "L0_gnn_b2", "L1_gnn_init_weight", "L1_gnn_weight", "L1_gnn_root_weight", "L1_gnn_bias", "L2_gnn_W",
        "L2_gnn_b", "L3_gnn_weight", "L3_gnn_bias"]


def kernel(**inputs):
    import numpy as _np
    import concourse.bacc as _bacc
    from concourse import mybir as _mybir
    from concourse.bass_utils import run_bass_kernel_spmd as _run

    nc = _bacc.Bacc("TRN2", target_bir_lowering=False, num_devices=1)
    arrays, args = {}, []
    for name in _INS:
        a = _np.ascontiguousarray(inputs[name])
        arrays[f"in_{name}_dram"] = a
        args.append(nc.dram_tensor(f"in_{name}_dram", a.shape, _mybir.dt.from_np(a.dtype), kind="ExternalInput").ap())
    out = nc.dram_tensor("out_0_dram", (N, D), _mybir.dt.float32, kind="ExternalOutput").ap()
    build(nc, *args, out)
    r = _run(nc, [arrays], core_ids=[0])
    return r.results[0]["out_0_dram"]
```
